# Optimizing a Trainium2 kernel written in Bass

```python
import numpy as np
import jax
import jax.numpy as jnp

def _softmax(x, axis=-1):
    return jax.nn.softmax(x, axis=axis)

def _gelu(x):
    return jax.nn.gelu(x, approximate=True)

def _silu(x):
    return jax.nn.silu(x)

def _sigmoid(x):
    return jax.nn.sigmoid(x)

def _layernorm(x, axis=-1, eps=1e-05):
    m = jnp.mean(x, axis=axis, keepdims=True)
    v = jnp.var(x, axis=axis, keepdims=True)
    return (x - m) / jnp.sqrt(v + eps)

def _scatter_add(tgt, idx, src, axis=0):
    return tgt.at[idx].add(src)

def _segment_sum(src, seg, n):
    return jax.ops.segment_sum(src, seg, n)
kernel_name = 'mk_gnn_resnorm_d2_gnn_r32_43eabe'

def setup_inputs(seed: int=0):
    np.random.seed(seed)
    _w = jnp.asarray

    def _rec_inputs():
        import jax
        import jax.numpy as jnp
        _gk = jax.random.key(seed)
        x = -0.000202 + 1 * jax.random.normal(jax.random.fold_in(_gk, 1), (50000, 128), jnp.float32)
        src = jax.random.randint(jax.random.fold_in(_gk, 2), (50000,), 0, 50000, jnp.int32)
        dst = jax.random.randint(jax.random.fold_in(_gk, 3), (50000,), 0, 50000, jnp.int32)
        _o = jnp.argsort(dst, stable=True)
        src = src[_o]
        dst = dst[_o]
        edge_attr_128 = -4.21973e-05 + 0.999841 * jax.random.normal(jax.random.fold_in(_gk, 12), (50000, 128), jnp.float32)
        edge_weight = jax.random.uniform(jax.random.fold_in(_gk, 13), (50000,), jnp.float32, 0.0, 0.0624999)
        return (x, src, dst, edge_attr_128, edge_weight)
    x, src, dst, edge_attr_128, edge_weight = _rec_inputs()

    def _L0_gnn_setup():
        import jax, jax.numpy as jnp
        import numpy as np
        N_NODES = 50000
        N_EDGES = 18750
        D = 128
        NEG_SLOPE = (1.0 / 8.0 + 1.0 / 3.0) / 2.0

        def _layer(h, efeat, src, dst, W1, b1, W2, b2, W3, b3):
            m = (h[src] + efeat) @ W1 + b1
            score = jnp.sum(h[dst] * m, axis=-1)
            smax = jax.ops.segment_max(score, dst, num_segments=N_NODES)
            smax = jnp.where(jnp.isfinite(smax), smax, 0.0)
            w = jnp.exp(score - smax[dst])
            denom = jax.ops.segment_sum(w, dst, num_segments=N_NODES)
            wsum = jax.ops.segment_sum(w[:, None] * m, dst, num_segments=N_NODES)
            neigh = wsum / jnp.maximum(denom, 1e-30)[:, None]
            deg = jax.ops.segment_sum(jnp.ones_like(score), dst, num_segments=N_NODES)
            self_msg = h @ W2 + b2
            iso_msg = h @ W3 + b3
            self_msg = jnp.where((deg == 0)[:, None], iso_msg, self_msg)
            x = self_msg + neigh
            return jnp.where(x >= 0, x, x * NEG_SLOPE)
        key = jax.random.key(seed)
        ks = jax.random.split(key, 16)
        inp = {'node_feats': jax.random.normal(ks[0], (N_NODES, D), dtype=jnp.float32), 'edge_feats': jax.random.normal(ks[1], (N_EDGES, D), dtype=jnp.float32), 'src': jax.random.randint(ks[2], (N_EDGES,), 0, N_NODES, dtype=jnp.int32), 'dst': jax.random.randint(ks[3], (N_EDGES,), 0, N_NODES, dtype=jnp.int32)}
        scale = 1.0 / np.sqrt(D)
        i = 4
        for l in range(2):
            for w in (1, 2, 3):
                inp[f'W{w}_l{l}'] = jax.random.uniform(ks[i], (D, D), jnp.float32, -scale, scale)
                i += 1
                inp[f'b{w}_l{l}'] = jnp.zeros((D,), jnp.float32)
        return inp
    _L0_gnn_all = _L0_gnn_setup()
    _L0_gnn_in = {k: v for k, v in _L0_gnn_all.items() if k in ('W1_l0', 'b1_l0', 'W2_l0', 'b2_l0', 'W3_l0', 'b3_l0', 'W1_l1', 'b1_l1', 'W2_l1', 'b2_l1', 'W3_l1', 'b3_l1')}
    del _L0_gnn_all

    def _L1_gnn_setup():
        import jax, jax.numpy as jnp
        import numpy as np
        N = 50000
        D = 128
        E = 25000
        C = 1.0
        MIN_NORM = 1e-15
        PROJ_EPS = 0.004

        def _artanh(y):
            return jnp.arctanh(jnp.clip(y, -1.0 + 1e-07, 1.0 - 1e-07))
        key = jax.random.key(seed)
        k1, k2, k3, k4 = jax.random.split(key, 4)
        x = 0.05 * jax.random.normal(k1, (N, D), dtype=jnp.float32)
        edge_row = jax.random.randint(k2, (E,), 0, N, dtype=jnp.int32)
        edge_col = jax.random.randint(k3, (E,), 0, N, dtype=jnp.int32)
        edge_w = jax.random.uniform(k4, (E,), dtype=jnp.float32) / 16.0
        return {'x': x, 'edge_w': edge_w, 'edge_row': edge_row, 'edge_col': edge_col}
    _L1_gnn_all = _L1_gnn_setup()
    _L1_gnn_in = {k: v for k, v in _L1_gnn_all.items() if k in ()}
    del _L1_gnn_all
    return {'x': x, 'src': src, 'dst': dst, 'edge_attr_128': edge_attr_128, 'edge_weight': edge_weight, 'L0_gnn_W1_l0': _L0_gnn_in['W1_l0'], 'L0_gnn_b1_l0': _L0_gnn_in['b1_l0'], 'L0_gnn_W2_l0': _L0_gnn_in['W2_l0'], 'L0_gnn_b2_l0': _L0_gnn_in['b2_l0'], 'L0_gnn_W3_l0': _L0_gnn_in['W3_l0'], 'L0_gnn_b3_l0': _L0_gnn_in['b3_l0'], 'L0_gnn_W1_l1': _L0_gnn_in['W1_l1'], 'L0_gnn_b1_l1': _L0_gnn_in['b1_l1'], 'L0_gnn_W2_l1': _L0_gnn_in['W2_l1'], 'L0_gnn_b2_l1': _L0_gnn_in['b2_l1'], 'L0_gnn_W3_l1': _L0_gnn_in['W3_l1'], 'L0_gnn_b3_l1': _L0_gnn_in['b3_l1']}

def reference(x, src, dst, edge_attr_128, edge_weight, L0_gnn_W1_l0, L0_gnn_b1_l0, L0_gnn_W2_l0, L0_gnn_b2_l0, L0_gnn_W3_l0, L0_gnn_b3_l0, L0_gnn_W1_l1, L0_gnn_b1_l1, L0_gnn_W2_l1, L0_gnn_b2_l1, L0_gnn_W3_l1, L0_gnn_b3_l1):
    import jax
    import jax.numpy as jnp

    def _L0_gnn_ref(node_feats, edge_feats, src, dst, W1_l0, b1_l0, W2_l0, b2_l0, W3_l0, b3_l0, W1_l1, b1_l1, W2_l1, b2_l1, W3_l1, b3_l1):
        import jax, jax.numpy as jnp
        import numpy as np
        N_NODES = 50000
        N_EDGES = 18750
        D = 128
        NEG_SLOPE = (1.0 / 8.0 + 1.0 / 3.0) / 2.0

        def _layer(h, efeat, src, dst, W1, b1, W2, b2, W3, b3):
            m = (h[src] + efeat) @ W1 + b1
            score = jnp.sum(h[dst] * m, axis=-1)
            smax = jax.ops.segment_max(score, dst, num_segments=N_NODES)
            smax = jnp.where(jnp.isfinite(smax), smax, 0.0)
            w = jnp.exp(score - smax[dst])
            denom = jax.ops.segment_sum(w, dst, num_segments=N_NODES)
            wsum = jax.ops.segment_sum(w[:, None] * m, dst, num_segments=N_NODES)
            neigh = wsum / jnp.maximum(denom, 1e-30)[:, None]
            deg = jax.ops.segment_sum(jnp.ones_like(score), dst, num_segments=N_NODES)
            self_msg = h @ W2 + b2
            iso_msg = h @ W3 + b3
            self_msg = jnp.where((deg == 0)[:, None], iso_msg, self_msg)
            x = self_msg + neigh
            return jnp.where(x >= 0, x, x * NEG_SLOPE)
        h = _layer(node_feats, edge_feats, src, dst, W1_l0, b1_l0, W2_l0, b2_l0, W3_l0, b3_l0)
        h = _layer(h, edge_feats, src, dst, W1_l1, b1_l1, W2_l1, b2_l1, W3_l1, b3_l1)
        return h

    def _L1_gnn_ref(x, edge_w, edge_row, edge_col):
        import jax, jax.numpy as jnp
        import numpy as np
        N = 50000
        D = 128
        E = 25000
        C = 1.0
        MIN_NORM = 1e-15
        PROJ_EPS = 0.004

        def _artanh(y):
            return jnp.arctanh(jnp.clip(y, -1.0 + 1e-07, 1.0 - 1e-07))
        sqrt_c = jnp.float32(np.sqrt(C))
        pn = jnp.maximum(jnp.linalg.norm(x, axis=-1, keepdims=True), MIN_NORM)
        x_tangent = _artanh(sqrt_c * pn) / (sqrt_c * pn) * x
        msgs = edge_w[:, None] * x_tangent[edge_col]
        support_t = jax.ops.segment_sum(msgs, edge_row, num_segments=N)
        un = jnp.maximum(jnp.linalg.norm(support_t, axis=-1, keepdims=True), MIN_NORM)
        y = jnp.tanh(sqrt_c * un) / (sqrt_c * un) * support_t
        yn = jnp.maximum(jnp.linalg.norm(y, axis=-1, keepdims=True), MIN_NORM)
        maxnorm = (1.0 - PROJ_EPS) / sqrt_c
        return jnp.where(yn > maxnorm, y / yn * maxnorm, y)
    x = _layernorm(x + _L0_gnn_ref(x, edge_attr_128, src, dst, L0_gnn_W1_l0, L0_gnn_b1_l0, L0_gnn_W2_l0, L0_gnn_b2_l0, L0_gnn_W3_l0, L0_gnn_b3_l0, L0_gnn_W1_l1, L0_gnn_b1_l1, L0_gnn_W2_l1, L0_gnn_b2_l1, L0_gnn_W3_l1, L0_gnn_b3_l1), axis=-1)
    x = _layernorm(x + _L1_gnn_ref(x, edge_weight, src, dst), axis=-1)
    return x

_drawn_inputs = setup_inputs


def setup_inputs(seed=0):
    import zlib

    import numpy as np

    out = dict(_drawn_inputs(seed))
    spreads = {'L0_gnn_b1_l0': (0.0, 0.1),
     'L0_gnn_b2_l0': (0.0, 0.1),
     'L0_gnn_b3_l0': (0.0, 0.322),
     'L0_gnn_b1_l1': (0.0, 0.1),
     'L0_gnn_b2_l1': (0.0, 0.1),
     'L0_gnn_b3_l1': (0.0, 0.1)}
    factors = {'edge_weight': 4.764}
    for name, (base, spread) in spreads.items():
        noise = np.random.default_rng([zlib.crc32(name.encode()), seed]).standard_normal(out[name].shape)
        drawn = base * np.exp(spread * noise) if base else spread * noise
        out[name] = jnp.asarray(drawn.astype(out[name].dtype))
    for name, factor in factors.items():
        out[name] = (out[name] * factor).astype(out[name].dtype)
    return out
```

```python
import numpy as np
from contextlib import ExitStack
import concourse.bass as bass
from concourse import mybir

F32, BF16, I32 = mybir.dt.float32, mybir.dt.bfloat16, mybir.dt.int32
ALU = mybir.AluOpType
ACT = mybir.ActivationFunctionType
AX = mybir.AxisListType

P = 128
N = 50000
E = 50000
NB = -(-N // P)
NPAD = NB * P
KC = 392
EPAD = P * KC
TAIL = E - (P - 1) * KC
ITEMS = NB + NB - 1
IC = -(-ITEMS // P)
FILL_KEY = float(NPAD)
SLOPE = (1.0 / 8.0 + 1.0 / 3.0) / 2.0
EPS = 1e-5
MASKED = -1.0e30
M_NONE = -1.0e29
XW = 132


def wait(eng, sem, value):
    eng.wait_ge(sem, value)


def wait_apart(eng, sem, value):
    eng.wait_ge(sem, value)
    eng.nop(nofuse=True)


class Chain:

    def __init__(self, eng, sem, per_turn=0, turn=None):
        self.eng, self.sem, self.per_turn, self.turn, self.n = eng, sem, per_turn, turn, 0

    def __call__(self, ins, alone=False):
        self.n += 1
        ins.then_inc(self.sem, 1)
        (wait_apart if alone else wait)(self.eng, self.sem, self.n if self.turn is None else self.turn * self.per_turn + self.n)

    def end(self):
        assert self.turn is None or self.n == self.per_turn, (self.n, self.per_turn)


def rsqrt_steps(nc, link, out, v, t1, t2):
    vi, oi = v.bitcast(I32), out.bitcast(I32)
    link(nc.vector.tensor_scalar(oi, vi, 1, None, ALU.arith_shift_right))
    link(nc.vector.tensor_scalar(oi, oi, -1, 0x5F3759DF, ALU.mult, ALU.add))
    for _ in range(4):
        link(nc.vector.tensor_tensor(t1, out, v, ALU.mult))
        link(nc.vector.tensor_tensor(t2, t1, out, ALU.mult))
        link(nc.vector.tensor_scalar(t1, t2, -0.5, 1.5, ALU.mult, ALU.add))
        link(nc.vector.tensor_tensor(out, out, t1, ALU.mult))


def even_poly_steps(nc, link, out, x2, coefficients, t1):
    link(nc.vector.tensor_scalar(out, x2, coefficients[-1], coefficients[-2], ALU.mult, ALU.add))
    for c in coefficients[-3::-1]:
        link(nc.vector.tensor_tensor(t1, out, x2, ALU.mult))
        link(nc.vector.tensor_scalar(out, t1, c, None, ALU.add))


ARTANH_C = [1.0 / (2 * k + 1) for k in range(6)]
TANH_C = [1.0, -1 / 3, 2 / 15, -17 / 315, 62 / 2835, -1382 / 155925]


def build(nc, x, src, dst, ea, ew, W1a, b1a, W2a, b2a, W3a, b3a, W1b, b1b, W2b, b2b, W3b, b3b, out):
    dram = lambda name, shape, dt: nc.dram_tensor(name, shape, dt, kind="Internal").ap()
    xpad = dram("xpad", [NPAD, P], F32)
    h1 = dram("h1", [NPAD, P], F32)
    h2 = dram("h2", [NPAD, P], F32)
    xtab = dram("xtab", [NPAD, XW], F32)
    outpad = dram("outpad", [NPAD, P], F32)
    sorted_recs = {"dst": dram("dst_sorted", [EPAD, 4], F32), "src": dram("src_sorted", [EPAD, 4], F32)}
    item_tab = {"dst": dram("dst_items", [P * IC, 2], I32), "src": dram("src_items", [P * IC, 2], I32)}
    lay = [(W1a, b1a, W2a, b2a, W3a, b3a), (W1b, b1b, W2b, b2b, W3b, b3b)]

    ctx = ExitStack()
    with ctx:
        sb = lambda name, shape, dt: ctx.enter_context(nc.sbuf_tensor(name, shape, dt))
        pb = lambda name, shape, dt: ctx.enter_context(nc.psum_tensor(name, shape, dt))
        sem = lambda name: ctx.enter_context(nc.semaphore(name))

        ident = sb("ident", [P, P], F32)
        identb = sb("identb", [P, P], BF16)
        iota_n = sb("iota_n", [P, P], F32)
        iota_b = sb("iota_b", [P, KC], F32)
        below = sb("below", [P, P], BF16)
        notbelow = sb("notbelow", [P, P], BF16)
        onesb = sb("onesb", [P, P], BF16)
        zrow = sb("zrow", [NPAD - N, P], F32)
        s_const = sem("s_const")
        s_const0 = sem("s_const0")
        s_cp = sem("s_cp")
        with nc.Block() as block:
            @block.gpsimd
            def _(pool):
                pool.memset(ident[:, :], 0.0).then_inc(s_const0, 1)
                pool.memset(identb[:, :], 0.0).then_inc(s_const0, 1)
                pool.memset(onesb[:, :], 1.0).then_inc(s_const0, 1)
                pool.memset(zrow[:, :], 0.0).then_inc(s_const0, 1)
                pool.iota(iota_n[:, :], pattern=[[1, P]], base=0, channel_multiplier=0,
                          allow_small_or_imprecise_dtypes=True).then_inc(s_const, 1)
                pool.iota(iota_b[:, :], pattern=[[1, KC]], base=0, channel_multiplier=0,
                          allow_small_or_imprecise_dtypes=True).then_inc(s_const, 1)
                pool.wait_ge(s_const0, 4)
                for m in (ident, identb):
                    pool.affine_select(out=m[:, :], in_=m[:, :], compare_op=ALU.not_equal, fill=1.0,
                                       base=0, pattern=[[-1, P]], channel_multiplier=1).then_inc(s_const, 1)
                pool.affine_select(out=below[:, :], in_=onesb[:, :], compare_op=ALU.is_gt, fill=0.0,
                                   base=0, pattern=[[1, P]], channel_multiplier=-1).then_inc(s_const, 1)
                pool.affine_select(out=notbelow[:, :], in_=onesb[:, :], compare_op=ALU.is_ge, fill=0.0,
                                   base=0, pattern=[[-1, P]], channel_multiplier=1).then_inc(s_const, 1)
                pool.wait_ge(s_const, 6)

            @block.sync
            def _(sp):
                sp.dma_start(xpad[0:N, :], x).then_inc(s_cp, 16)
                sp.wait_ge(s_const0, 4)
                sp.dma_start(xpad[N:NPAD, :], zrow[:, :]).then_inc(s_cp, 16)
                sp.wait_ge(s_cp, 32)

        tables = {}
        for kind, key_in, oth_in in (("dst", dst, src), ("src", src, dst)):
            tables[kind] = counting_sort(nc, ctx, kind, key_in, oth_in, ew, sorted_recs[kind], item_tab[kind],
                                         iota_b, below, notbelow, onesb)

        for l, (hin, hout) in enumerate(((xpad, h1), (h1, h2))):
            layer(nc, l, hin, hout, ea, sorted_recs["dst"], item_tab["dst"], tables["dst"], lay[l],
                  ident, identb, iota_n)
        norm_pass(nc, xpad, h2, xtab)
        last_stage(nc, xtab, outpad, sorted_recs["src"], item_tab["src"], tables["src"], iota_n)

        s_final = sem("s_final")
        with nc.Block() as block:
            @block.sync
            def _(sp):
                sp.dma_start(out, outpad[0:N, :]).then_inc(s_final, 16)
                sp.wait_ge(s_final, 16)


def counting_sort(nc, outer, kind, key_in, oth_in, ew, recs_out, items_out, iota_b, below, notbelow, onesb):
    keep = outer.enter_context(nc.sbuf_tensor(f"{kind}_keep", [P, P * IC], F32))
    base = outer.enter_context(nc.sbuf_tensor(f"{kind}_base", [P, P * IC], F32))
    ctx = ExitStack()
    with ctx:
        sb = lambda name, shape, dt: ctx.enter_context(nc.sbuf_tensor(f"{kind}_{name}", shape, dt))
        pb = lambda name, shape, dt: ctx.enter_context(nc.psum_tensor(f"{kind}_{name}", shape, dt))
        sem = lambda name: ctx.enter_context(nc.semaphore(f"{kind}_{name}"))
        ints = sb("ints", [P, 2, KC], I32)
        blk_i = sb("blk_i", [P, KC], I32)
        blk = sb("blk", [P, KC], F32)
        rank = sb("rank", [P, KC], F32)
        third = sb("third", [P, KC], F32)
        recs = sb("recs", [P, KC, 4], F32)
        oh = sb("oh", [P, 4, KC], BF16)
        scr = sb("scr", [P, KC], F32)
        counts = sb("counts", [P, KC], F32)
        off = sb("off", [P, KC], F32)
        ones = sb("ones", [P, KC], F32)
        offsel = sb("offsel", [P, 4], F32)
        pos = sb("pos", [P, 4], I32)
        rec4 = sb("rec4", [P, 4, 4], F32)
        tile_i = sb("tile_i", [P, KC], I32)
        last_item = sb("last_item", [P, KC], F32)
        item_id = sb("item_id", [P, IC], F32)
        item_blk = sb("item_blk", [P, IC], F32)
        item_rows = sb("item_rows", [P, IC, 2], I32)
        item_f = sb("item_f", [P, IC, 2], F32)
        rows_bc = sb("rows_bc", [P, P * IC, 2], I32)
        bank = [pb(f"bank{i}", [P, 512], F32) for i in range(2)]
        s_load, s_fill, s_iota, s_dve = sem("load"), sem("fill"), sem("iota"), sem("dve")
        s_keys, s_oh, s_cnt, s_rank, s_total = sem("keys"), sem("oh"), sem("cnt"), sem("rank"), sem("total")
        s_pos, s_rec, s_off = sem("pos"), sem("rec"), sem("off")
        s_sc = [sem(f"sc{i}") for i in range(4)]
        s_items, s_itab, s_bc = sem("items"), sem("itab"), sem("bc")

        with nc.Block() as block:
            @block.gpsimd
            def _(pool):
                pool.memset(ints[:, 0, :], NPAD).then_inc(s_fill, 1)
                pool.memset(ints[:, 1, :], 0).then_inc(s_fill, 1)
                if kind == "src":
                    pool.memset(third[:, :], 0.0).then_inc(s_fill, 1)
                else:
                    pool.iota(third[:, :], pattern=[[1, KC]], base=0, channel_multiplier=KC,
                              allow_small_or_imprecise_dtypes=True).then_inc(s_fill, 1)
                pool.iota(item_id[:, :], pattern=[[1, IC]], base=0, channel_multiplier=IC,
                          allow_small_or_imprecise_dtypes=True).then_inc(s_iota, 1)

                def turn(c):
                    for j in range(4):
                        pool.wait_ge(s_pos, c + j + 1)
                        wait_apart(pool, s_rec, c + j + 1)
                        pool.indirect_dma_start(
                            out=recs_out, out_offset=bass.IndirectOffsetOnAxis(ap=pos[:, j:j + 1], axis=0),
                            in_=rec4[:, j, :], in_offset=None, bounds_check=last_row, oob_is_err=False,
                        ).then_inc(s_sc[j], 16)
                last_row = pool.to_reg(EPAD - 1)
                with pool.Fori(0, KC // 4) as q:
                    turn(q * 4)
                for j in range(4):
                    pool.wait_ge(s_sc[j], 16 * KC // 4)

            @block.sync
            def _(sp):
                sp.wait_ge(s_fill, 3)
                for n, a in enumerate((key_in, oth_in)):
                    sp.dma_start(ints[0:P - 1, n, :], a[0:(P - 1) * KC].rearrange("(p c) -> p c", c=KC)).then_inc(s_load, 16)
                    sp.dma_start(ints[P - 1:P, n, 0:TAIL], a[(P - 1) * KC:E].rearrange("(p c) -> p c", c=TAIL)).then_inc(s_load, 16)
                if kind == "src":
                    sp.dma_start(third[0:P - 1, :], ew[0:(P - 1) * KC].rearrange("(p c) -> p c", c=KC)).then_inc(s_load, 16)
                    sp.dma_start(third[P - 1:P, 0:TAIL], ew[(P - 1) * KC:E].rearrange("(p c) -> p c", c=TAIL)).then_inc(s_load, 16)
                sp.wait_ge(s_items, 1)
                sp.dma_start(items_out.rearrange("(p c) t -> p c t", c=IC), item_rows[:, :, :]).then_inc(s_itab, 16)
                sp.wait_ge(s_itab, 16)
                sp.dma_start(rows_bc[:, :, :],
                             items_out.rearrange("(o c) t -> o c t", o=1).to_broadcast([P, P * IC, 2])).then_inc(s_bc, 16)

            @block.vector
            def _(dve):
                link = Chain(dve, s_dve)
                dve.wait_ge(s_load, 96 if kind == "src" else 64)
                link(nc.vector.tensor_scalar(blk_i[:, :], ints[:, 0, :], 7, None, ALU.arith_shift_right))
                link(nc.vector.tensor_copy(blk[:, :], blk_i[:, :]))
                link(nc.vector.memset(recs[:, :, :], 0.0))
                link(nc.vector.tensor_copy(recs[:, :, 0], ints[:, 0, :]))
                link(nc.vector.tensor_copy(recs[:, :, 1], ints[:, 1, :]))
                link(nc.vector.tensor_copy(recs[:, :, 2], third[:, :]))
                if kind == "dst":
                    link(nc.vector.tensor_scalar(rank[:, :], third[:, :], float(E), None, ALU.is_lt))
                    link(nc.vector.tensor_tensor(recs[:, :, 2], third[:, :], rank[:, :], ALU.mult))
                nc.vector.memset(ones[:, :], 1.0).then_inc(s_keys, 1)

                def onehot(c, j):
                    nc.vector.tensor_scalar(oh[:, j, :], iota_b[:, :], blk[:, bass.ds(c, 1)], None,
                                            ALU.is_equal).then_inc(s_oh, 1)

                def take_rank(c, j):
                    dve.wait_ge(s_cnt, c + 1)
                    nc.vector.scalar_tensor_tensor(scr[:, :], iota_b[:, :], blk[:, bass.ds(c, 1)],
                                                   bank[j % 2][:, 0:KC], ALU.is_equal, ALU.mult,
                                                   accum_out=rank[:, bass.ds(c, 1)]).then_inc(s_rank, 1)

                nc.vector.memset(oh[:, :, :], 0.0).then_inc(s_rank, 2)
                dve.wait_ge(s_keys, 1)
                dve.wait_ge(s_rank, 2)
                with dve.Fori(0, KC // 4) as q:
                    c = q * 4
                    for j in range(4):
                        onehot(c + j, j)
                        take_rank(c + j, j)
                dve.wait_ge(s_total, 1)
                link(nc.vector.tensor_copy(counts[:, :], bank[1][:, 0:KC]))
                link(nc.vector.tensor_tensor_scan(off[:, :], ones[:, :], counts[:, :], 0.0, ALU.mult, ALU.add))
                link(nc.vector.tensor_copy(tile_i[:, :], off[:, :]))
                link(nc.vector.tensor_scalar(tile_i[:, :], tile_i[:, :], 7, None, ALU.arith_shift_right))
                link(nc.vector.tensor_tensor(last_item[:, :], tile_i[:, :], iota_b[:, :], ALU.add))
                link(nc.vector.tensor_tensor(off[:, :], off[:, :], counts[:, :], ALU.subtract))
                dve.wait_ge(s_iota, 1)
                for j in range(IC):
                    link(nc.vector.tensor_scalar(scr[:, 0:NB], last_item[:, 0:NB], item_id[:, j:j + 1], None,
                                                 ALU.is_lt, ALU.add, accum_out=item_blk[:, j:j + 1]))
                link(nc.vector.tensor_scalar(item_f[:, :, 0], item_blk[:, :], float(P), None, ALU.mult))
                link(nc.vector.tensor_tensor(item_f[:, :, 1], item_id[:, :], item_blk[:, :], ALU.subtract))
                link(nc.vector.tensor_scalar(item_f[:, :, 1], item_f[:, :, 1], float(P), None, ALU.mult))
                nc.vector.tensor_copy(item_rows[:, :, :], item_f[:, :, :]).then_inc(s_items, 1)

                with dve.Fori(0, KC // 4) as q:
                    c = q * 4
                    for j in range(4):
                        nc.vector.scalar_tensor_tensor(scr[:, :], iota_b[:, :], blk[:, bass.ds(c + j, 1)],
                                                       off[:, :], ALU.is_equal, ALU.mult,
                                                       accum_out=offsel[:, j:j + 1]).then_inc(s_off, 1)
                        dve.wait_ge(s_off, c + j + 1)
                        nc.vector.tensor_tensor(pos[:, j:j + 1], offsel[:, j:j + 1], rank[:, bass.ds(c + j, 1)],
                                                ALU.add).then_inc(s_pos, 1)
                        nc.vector.tensor_copy(rec4[:, j, :], recs[:, bass.ds(c + j, 1), :].rearrange("p a b -> p (a b)")).then_inc(s_rec, 1)
                    for j in range(4):
                        dve.wait_ge(s_sc[j], q * 16 + 16)

                dve.wait_ge(s_bc, 16)
                link(nc.vector.tensor_copy(base[:, :], rows_bc[:, :, 0]))
                link(nc.vector.memset(keep[:, 0:1], 0.0))
                link(nc.vector.tensor_tensor(keep[:, 1:], base[:, 1:], base[:, :P * IC - 1], ALU.is_equal))

            @block.tensor
            def _(pe):
                mm = lambda c, w, j, **k: nc.tensor.matmul(bank[c][:, 0:KC], w[:, :], oh[:, j, :], skip_group_check=True, **k)
                pe.wait_ge(s_rank, 2)
                mm(0, onesb, 2, start=True, stop=True)
                mm(1, onesb, 3, start=True, stop=True)
                with pe.Fori(0, KC // 4) as q:
                    c = q * 4
                    for j in range(4):
                        pe.wait_ge(s_oh, c + j + 1)
                        pe.wait_ge(s_rank, c + j + 1)
                        mm(j % 2, notbelow, (j - 2) % 4, start=False, stop=True)
                        mm(j % 2, onesb, (j - 1) % 4, start=False, stop=True)
                        mm(j % 2, below, j, start=False, stop=True).then_inc(s_cnt, 1)
                pe.wait_ge(s_rank, KC + 2)
                mm(1, notbelow, 3, start=False, stop=True).then_inc(s_total, 1)
    return keep, base


def layer(nc, l, hin, hout, ea, recs, items, tables, weights, ident, identb, iota_n):
    keep, base = tables
    W1, b1, W2, b2, W3, b3 = weights
    ctx = ExitStack()
    with ctx:
        sb = lambda name, shape, dt: ctx.enter_context(nc.sbuf_tensor(f"l{l}_{name}", shape, dt))
        pb = lambda name, shape, dt: ctx.enter_context(nc.psum_tensor(f"l{l}_{name}", shape, dt))
        sem = lambda name: ctx.enter_context(nc.semaphore(f"l{l}_{name}"))
        w1 = sb("w1", [P, P], F32)
        w1t = sb("w1t", [P, P], F32)
        w23 = sb("w23", [P, 2, P], F32)
        w2 = sb("w2", [P, P], F32)
        b1col = sb("b1col", [P, 1], F32)
        b1bc = sb("b1bc", [P, P], F32)
        brow = sb("brow", [P, 3, P], F32)
        b23 = sb("b23", [P, 2, P], F32)
        rec = sb("rec", [P, 4], F32)
        idx = sb("idx", [P, 2], I32)
        hb = sb("hb", [P, P], F32)
        hs = sb("hs", [P, P], F32)
        ev = sb("ev", [P, P], F32)
        g = sb("g", [P, P], F32)
        loc = sb("loc", [P, 1], F32)
        pen = sb("pen", [P, P], BF16)
        hT = sb("hT", [P, P], F32)
        qT = sb("qT", [P, P], F32)
        gT = sb("gT", [P, P], F32)
        w = sb("w", [P, P], F32)
        wT = sb("wT", [P, P], F32)
        acc = sb("acc", [P, P], F32)
        accn = sb("accn", [P, P], F32)
        accT = sb("accT", [P, P], F32)
        A = sb("A", [P, 2, P], F32)
        pre = sb("pre", [P, P], F32)
        o = sb("o", [P, P], F32)
        st = sb("st", [P, 16], F32)
        col = {n: st[:, k:k + 1] for k, n in enumerate(
            ("M", "L", "Mold", "mx", "Mn", "nMn", "alpha", "Lnew", "ka", "inv", "has", "t"))}
        pT, pQ, pA, pS, pW, pG, pN = [pb(f"p{k}", [P, 512], F32) for k in range(7)]
        names = ("wload", "wdve", "wT", "prep", "rec", "h", "idx", "hs", "ev", "g", "pen", "hT", "hTs", "q", "qs",
                 "a", "gT", "gTs", "s", "m", "al", "w", "wTp", "wTs", "G", "accn", "aT", "aTs", "N", "out", "st", "dve")
        s = {n: sem(n) for n in names}
        K = 14

        with nc.Block() as block:
            @block.sync
            def _(sp):
                sp.dma_start(w1[:, :], W1).then_inc(s["wload"], 16)
                sp.dma_start(w2[:, :], W2).then_inc(s["wload"], 16)
                sp.dma_start(w23[:, 0, :], W3).then_inc(s["wload"], 16)
                for n, b in enumerate((b1, b2, b3)):
                    sp.dma_start(brow[:, n, :], b.rearrange("(o n) -> o n", o=1).to_broadcast([P, P])).then_inc(s["wload"], 16)
                sp.dma_start(b1col[:, :], b1.rearrange("(n o) -> n o", o=1)).then_inc(s["wload"], 16)
                with sp.Fori(0, ITEMS) as i:
                    row = sp.value_load(items[bass.ds(i, 1), 0:1], min_val=0, max_val=NPAD - P)
                    erow = sp.value_load(items[bass.ds(i, 1), 1:2], min_val=0, max_val=EPAD - P)
                    sp.dma_start(rec[:, :], recs[bass.ds(erow, P), :]).then_inc(s["rec"], 16)
                    sp.dma_start(hb[:, :], hin[bass.ds(row, P), :]).then_inc(s["h"], 16)
                    sp.wait_ge(s["out"], i + 1)
                    sp.dma_start(hout[bass.ds(row, P), :], o[:, :]).then_inc(s["st"], 16)
                    wait_apart(sp, s["st"], i * 16 + 16)

            @block.gpsimd
            def _(pool):
                last_row = pool.to_reg(N - 1)
                with pool.Fori(0, ITEMS) as i:
                    wait_apart(pool, s["idx"], i + 1)
                    pool.indirect_dma_start(out=hs[:, :], out_offset=None, in_=hin,
                                            in_offset=bass.IndirectOffsetOnAxis(ap=idx[:, 0:1], axis=0),
                                            bounds_check=last_row, oob_is_err=False).then_inc(s["hs"], 16)
                    pool.indirect_dma_start(out=ev[:, :], out_offset=None, in_=ea,
                                            in_offset=bass.IndirectOffsetOnAxis(ap=idx[:, 1:2], axis=0),
                                            bounds_check=last_row, oob_is_err=False).then_inc(s["ev"], 16)

            @block.vector
            def _(dve):
                dve.wait_ge(s["wload"], 7 * 16)
                link = Chain(dve, s["wdve"])
                link(nc.vector.tensor_tensor(w23[:, 1, :], w2[:, :], w23[:, 0, :], ALU.subtract))
                link(nc.vector.tensor_copy(b23[:, 0, :], brow[:, 2, :]))
                link(nc.vector.tensor_tensor(b23[:, 1, :], brow[:, 0, :], brow[:, 1, :], ALU.add))
                link(nc.vector.tensor_tensor(b23[:, 1, :], b23[:, 1, :], brow[:, 2, :], ALU.subtract))
                link(nc.vector.memset(b1bc[:, :], 0.0))
                link(nc.vector.tensor_scalar(b1bc[:, :], b1bc[:, :], b1col[:, 0:1], None, ALU.add))
                link(nc.vector.memset(st[:, :], 0.0))
                link(nc.vector.memset(acc[:, :], 0.0))
                dve.wait_ge(s["wT"], 1)
                nc.vector.tensor_copy(w1t[:, :], pT[:, 0:P]).then_inc(s["prep"], 1)
                dve.wait_ge(s["prep"], 1)
                with dve.Fori(0, ITEMS) as i:
                    link = Chain(dve, s["dve"], K, i)
                    here = lambda t: t[:, bass.ds(i, 1)]
                    dve.wait_ge(s["rec"], i * 16 + 16)
                    nc.vector.tensor_copy(idx[:, :], rec[:, 1:3]).then_inc(s["idx"], 1)
                    link(nc.vector.tensor_tensor(loc[:, :], rec[:, 0:1], here(base), ALU.subtract))
                    nc.vector.tensor_scalar(pen[:, :], iota_n[:, :], loc[:, 0:1], MASKED, ALU.not_equal, ALU.mult).then_inc(s["pen"], 1)
                    dve.wait_ge(s["hs"], i * 16 + 16)
                    dve.wait_ge(s["ev"], i * 16 + 16)
                    nc.vector.tensor_tensor(g[:, :], hs[:, :], ev[:, :], ALU.add).then_inc(s["g"], 1)
                    link(nc.vector.tensor_tensor(col["Mold"], col["M"], here(keep), ALU.mult))
                    link(nc.vector.tensor_scalar(col["t"], here(keep), -1.0, -M_NONE, ALU.add, ALU.mult))
                    link(nc.vector.tensor_tensor(col["Mold"], col["Mold"], col["t"], ALU.add))
                    dve.wait_ge(s["s"], i + 1)
                    link(nc.vector.reduce_max(col["mx"], pS[:, 0:P], AX.X))
                    link(nc.vector.tensor_tensor(col["Mn"], col["mx"], col["Mold"], ALU.max))
                    nc.vector.tensor_scalar(col["nMn"], col["Mn"], -1.0, None, ALU.mult).then_inc(s["m"], 1)
                    dve.wait_ge(s["al"], i + 1)
                    link(nc.vector.tensor_tensor(col["ka"], col["alpha"], here(keep), ALU.mult))
                    dve.wait_ge(s["w"], i + 1)
                    link(nc.vector.scalar_tensor_tensor(col["L"], col["L"], col["ka"], col["Lnew"], ALU.mult, ALU.add))
                    link(nc.vector.tensor_copy(col["M"], col["Mn"]))
                    dve.wait_ge(s["G"], i + 1)
                    link(nc.vector.scalar_tensor_tensor(acc[:, :], acc[:, :], col["ka"], pG[:, 0:P], ALU.mult, ALU.add))
                    link(nc.vector.tensor_scalar(col["t"], col["L"], 1e-30, None, ALU.max))
                    link(nc.vector.reciprocal(col["inv"], col["t"]))
                    link(nc.vector.tensor_scalar(col["has"], col["L"], 0.0, None, ALU.is_gt))
                    nc.vector.tensor_scalar(accn[:, :], acc[:, :], col["inv"], None, ALU.mult).then_inc(s["accn"], 1)
                    dve.wait_ge(s["a"], i + 1)
                    link(nc.vector.tensor_tensor(A[:, :, :], pA[:, 0:2 * P].rearrange("p (a b) -> p a b", a=2), b23[:, :, :], ALU.add))
                    dve.wait_ge(s["accn"], i + 1)
                    nc.vector.scalar_tensor_tensor(pre[:, :], A[:, 1, :], col["has"], A[:, 0, :], ALU.mult, ALU.add).then_inc(s["wdve"], 1)
                    dve.wait_ge(s["wdve"], i * 2 + 8 + 1)
                    dve.wait_ge(s["N"], i + 1)
                    nc.vector.tensor_tensor(accn[:, :], pre[:, :], pN[:, 0:P], ALU.add).then_inc(s["wdve"], 1)
                    dve.wait_ge(s["wdve"], i * 2 + 8 + 2)
                    nc.vector.scalar_tensor_tensor(o[:, :], accn[:, :], SLOPE, accn[:, :], ALU.mult, ALU.max).then_inc(s["out"], 1)
                    link.end()

            @block.scalar
            def _(act):
                with act.Fori(0, ITEMS) as i:
                    act.wait_ge(s["hT"], i + 1)
                    nc.scalar.copy(hT[:, :], pT[:, 0:P]).then_inc(s["hTs"], 1)
                    act.wait_ge(s["q"], i + 1)
                    nc.scalar.copy(qT[:, :], pQ[:, 0:P]).then_inc(s["qs"], 1)
                    act.wait_ge(s["gT"], i + 1)
                    nc.scalar.copy(gT[:, :], pT[:, P:2 * P]).then_inc(s["gTs"], 1)
                    act.wait_ge(s["m"], i + 1)
                    nc.scalar.activation(col["alpha"], col["Mold"], ACT.Exp, bias=col["nMn"]).then_inc(s["al"], 1)
                    nc.scalar.activation(w[:, :], pS[:, 0:P], ACT.Exp, bias=col["nMn"], accum_out=col["Lnew"]).then_inc(s["w"], 1)
                    act.wait_ge(s["wTp"], i + 1)
                    nc.scalar.copy(wT[:, :], pW[:, 0:P]).then_inc(s["wTs"], 1)
                    act.wait_ge(s["aT"], i + 1)
                    nc.scalar.copy(accT[:, :], pW[:, P:2 * P]).then_inc(s["aTs"], 1)

            @block.tensor
            def _(pe):
                pe.wait_ge(s["wload"], 7 * 16)
                nc.tensor.transpose(pT[:, 0:P], w1[:, :], ident[:, :]).then_inc(s["wT"], 1)
                pe.wait_ge(s["prep"], 1)
                with pe.Fori(0, ITEMS) as i:
                    pe.wait_ge(s["h"], i * 16 + 16)
                    nc.tensor.transpose(pT[:, 0:P], hb[:, :], ident[:, :]).then_inc(s["hT"], 1)
                    pe.wait_ge(s["hTs"], i + 1)
                    nc.tensor.matmul(pQ[:, 0:P], w1t[:, :], hT[:, :], start=True, stop=True).then_inc(s["q"], 1)
                    nc.tensor.matmul(pA[:, 0:2 * P], hT[:, :], w23[:, :, :].rearrange("p a b -> p (a b)"), start=True, stop=True).then_inc(s["a"], 1)
                    pe.wait_ge(s["g"], i + 1)
                    nc.tensor.transpose(pT[:, P:2 * P], g[:, :], ident[:, :]).then_inc(s["gT"], 1)
                    pe.wait_ge(s["qs"], i + 1)
                    pe.wait_ge(s["gTs"], i + 1)
                    pe.wait_ge(s["pen"], i + 1)
                    nc.tensor.matmul(pS[:, 0:P], qT[:, :], gT[:, :], start=True, stop=False)
                    nc.tensor.matmul(pS[:, 0:P], hT[:, :], b1bc[:, :], start=False, stop=False)
                    nc.tensor.matmul(pS[:, 0:P], pen[:, :], identb[:, :], start=False, stop=True).then_inc(s["s"], 1)
                    pe.wait_ge(s["w"], i + 1)
                    nc.tensor.transpose(pW[:, 0:P], w[:, :], ident[:, :]).then_inc(s["wTp"], 1)
                    pe.wait_ge(s["wTs"], i + 1)
                    nc.tensor.matmul(pG[:, 0:P], wT[:, :], g[:, :], start=True, stop=True).then_inc(s["G"], 1)
                    pe.wait_ge(s["accn"], i + 1)
                    nc.tensor.transpose(pW[:, P:2 * P], accn[:, :], ident[:, :]).then_inc(s["aT"], 1)
                    pe.wait_ge(s["aTs"], i + 1)
                    nc.tensor.matmul(pN[:, 0:P], accT[:, :], w1[:, :], start=True, stop=True).then_inc(s["N"], 1)


def normalise_steps(nc, link, out, z, st6, mv, v, r, t1, t2):
    link(nc.vector.bn_stats(st6, z), alone=True)
    link(nc.vector.bn_aggr(mv, st6))
    link(nc.vector.tensor_scalar(v, mv[:, 1:2], EPS, None, ALU.add))
    rsqrt_steps(nc, link, r, v, t1, t2)
    link(nc.vector.tensor_scalar(out, z, mv[:, 0:1], r, ALU.subtract, ALU.mult))


def norm_steps(nc, link, z, scratch, ss, n, r, t1, t2):
    link(nc.vector.tensor_tensor_reduce(out=scratch, in0=z, in1=z, scale=1.0, scalar=0.0,
                                        op0=ALU.mult, op1=ALU.add, accum_out=ss))
    rsqrt_steps(nc, link, r, ss, t1, t2)
    link(nc.vector.tensor_tensor(n, ss, r, ALU.mult))
    link(nc.vector.tensor_scalar(n, n, 1e-15, None, ALU.max))
    link(nc.vector.reciprocal(r, n))


def norm_pass(nc, xpad, h2, xtab):
    ctx = ExitStack()
    with ctx:
        sb = lambda name, shape, dt: ctx.enter_context(nc.sbuf_tensor(f"n_{name}", shape, dt))
        sem = lambda name: ctx.enter_context(nc.semaphore(f"n_{name}"))
        xb, hb, scr = sb("xb", [P, P], F32), sb("hb", [P, P], F32), sb("scr", [P, P], F32)
        row = sb("row", [P, XW], F32)
        st6 = sb("st6", [P, 6], F32)
        c = sb("c", [P, 16], F32)
        at = lambda k: c[:, k:k + 1]
        s_in, s_dve, s_cl, s_ln, s_out, s_st = sem("in"), sem("dve"), sem("cl"), sem("ln"), sem("out"), sem("st")
        s_in2 = sem("in2")
        K = 1 + 3 + 18 + 1 + 22 + 1 + 1 + 4
        with nc.Block() as block:
            @block.sync
            def _(sp):
                with sp.Fori(0, NB) as b:
                    sp.dma_start(xb[:, :], xpad[bass.ds(b * P, P), :]).then_inc(s_in, 16)
                    sp.dma_start(hb[:, :], h2[bass.ds(b * P, P), :]).then_inc(s_in2, 16)
                    sp.wait_ge(s_out, b + 1)
                    sp.dma_start(xtab[bass.ds(b * P, P), :], row[:, :]).then_inc(s_st, 16)
                    wait_apart(sp, s_st, b * 16 + 16)

            @block.vector
            def _(dve):
                nc.vector.memset(row[:, :], 0.0).then_inc(s_dve, 1)
                dve.wait_ge(s_dve, 1)
                with dve.Fori(0, NB) as b:
                    link = OffsetChain(dve, s_dve, NORM_K, b, 1)
                    dve.wait_ge(s_in, b * 16 + 16)
                    dve.wait_ge(s_in2, b * 16 + 16)
                    link(nc.vector.tensor_tensor(xb[:, :], xb[:, :], hb[:, :], ALU.add))
                    normalise_steps(nc, link, row[:, 0:P], xb[:, :], st6[:, :], c[:, 0:2], at(2), at(3), at(4), at(5))
                    norm_steps(nc, link, row[:, 0:P], scr[:, :], at(6), at(7), at(3), at(4), at(5))
                    nc.vector.tensor_scalar(at(8), at(7), 1.0 - 1e-7, None, ALU.min).then_inc(s_cl, 1)
                    dve.wait_ge(s_cl, b + 1)
                    link(nc.vector.tensor_scalar(at(9), at(8), 0.25, None, ALU.min))
                    link(nc.vector.tensor_tensor(at(9), at(9), at(9), ALU.mult))
                    even_poly_steps(nc, link, at(10), at(9), ARTANH_C, at(4))
                    dve.wait_ge(s_ln, 2 * b + 2)
                    link(nc.vector.tensor_tensor(at(11), at(12), at(13), ALU.subtract))
                    link(nc.vector.tensor_scalar(at(11), at(11), at(3), 0.5, ALU.mult, ALU.mult))
                    link(nc.vector.tensor_tensor(at(10), at(10), at(11), ALU.subtract))
                    link(nc.vector.tensor_scalar(at(4), at(8), 0.25, None, ALU.is_lt))
                    nc.vector.scalar_tensor_tensor(row[:, P:P + 1], at(10), at(4), at(11), ALU.mult, ALU.add).then_inc(s_out, 1)
                    link.end()

            @block.scalar
            def _(act):
                with act.Fori(0, NB) as b:
                    act.wait_ge(s_cl, b + 1)
                    nc.scalar.activation(at(12), at(8), ACT.Ln, bias=1.0, scale=1.0).then_inc(s_ln, 1)
                    nc.scalar.activation(at(13), at(8), ACT.Ln, bias=1.0, scale=-1.0).then_inc(s_ln, 1)


RS_K = 2 + 4 * 4
NORMALISE_K = 3 + RS_K + 1
NORMLEN_K = 1 + RS_K + 3
POLY_K = 1 + 2 * 4
NORM_K = 1 + NORMALISE_K + NORMLEN_K + 2 + POLY_K + 4


class OffsetChain(Chain):

    def __init__(self, eng, sem, per_turn, turn, ahead):
        super().__init__(eng, sem, per_turn, turn)
        self.ahead = ahead

    def __call__(self, ins, alone=False):
        self.n += 1
        ins.then_inc(self.sem, 1)
        (wait_apart if alone else wait)(self.eng, self.sem, self.turn * self.per_turn + (self.n + self.ahead))


def last_stage(nc, xtab, outpad, recs, items, tables, iota_n):
    keep, base = tables
    ctx = ExitStack()
    with ctx:
        sb = lambda name, shape, dt: ctx.enter_context(nc.sbuf_tensor(f"f_{name}", shape, dt))
        pb = lambda name, shape, dt: ctx.enter_context(nc.psum_tensor(f"f_{name}", shape, dt))
        sem = lambda name: ctx.enter_context(nc.semaphore(f"f_{name}"))
        rec, idx = sb("rec", [P, 4], F32), sb("idx", [P, 1], I32)
        xb, xg = sb("xb", [P, XW], F32), sb("xg", [P, XW], F32)
        wf, loc, A = sb("wf", [P, 1], F32), sb("loc", [P, 1], F32), sb("A", [P, P], F32)
        acc, scr, z, o = (sb(n, [P, P], F32) for n in ("acc", "scr", "z", "o"))
        st6 = sb("st6", [P, 6], F32)
        c = sb("c", [P, 20], F32)
        at = lambda k: c[:, k:k + 1]
        pG = pb("pG", [P, 512], F32)
        s = {n: sem(n) for n in ("rec", "x", "idx", "xg", "A", "G", "dve", "u", "e", "out", "st")}
        K = 2 + 1 + NORMLEN_K + 2 + POLY_K + 5 + 8 + 1 + NORMALISE_K
        with nc.Block() as block:
            @block.sync
            def _(sp):
                with sp.Fori(0, ITEMS) as i:
                    row = sp.value_load(items[bass.ds(i, 1), 0:1], min_val=0, max_val=NPAD - P)
                    erow = sp.value_load(items[bass.ds(i, 1), 1:2], min_val=0, max_val=EPAD - P)
                    sp.dma_start(rec[:, :], recs[bass.ds(erow, P), :]).then_inc(s["rec"], 16)
                    sp.dma_start(xb[:, :], xtab[bass.ds(row, P), :]).then_inc(s["x"], 16)
                    sp.wait_ge(s["out"], i + 1)
                    sp.dma_start(outpad[bass.ds(row, P), :], o[:, :]).then_inc(s["st"], 16)
                    wait_apart(sp, s["st"], i * 16 + 16)

            @block.gpsimd
            def _(pool):
                last_row = pool.to_reg(N - 1)
                with pool.Fori(0, ITEMS) as i:
                    wait_apart(pool, s["idx"], i + 1)
                    pool.indirect_dma_start(out=xg[:, :], out_offset=None, in_=xtab,
                                            in_offset=bass.IndirectOffsetOnAxis(ap=idx[:, 0:1], axis=0),
                                            bounds_check=last_row, oob_is_err=False).then_inc(s["xg"], 16)

            @block.scalar
            def _(act):
                with act.Fori(0, ITEMS) as i:
                    act.wait_ge(s["u"], i + 1)
                    nc.scalar.activation(at(8), at(7), ACT.Exp, scale=-2.0).then_inc(s["e"], 1)

            @block.tensor
            def _(pe):
                with pe.Fori(0, ITEMS) as i:
                    pe.wait_ge(s["A"], i + 1)
                    nc.tensor.matmul(pG[:, 0:P], A[:, :], xg[:, 0:P], start=True, stop=True).then_inc(s["G"], 1)

            @block.vector
            def _(dve):
                nc.vector.memset(acc[:, :], 0.0).then_inc(s["dve"], 1)
                dve.wait_ge(s["dve"], 1)
                with dve.Fori(0, ITEMS) as i:
                    link = OffsetChain(dve, s["dve"], K, i, 1)
                    here = lambda t: t[:, bass.ds(i, 1)]
                    dve.wait_ge(s["rec"], i * 16 + 16)
                    nc.vector.tensor_copy(idx[:, :], rec[:, 1:2]).then_inc(s["idx"], 1)
                    link(nc.vector.tensor_tensor(loc[:, :], rec[:, 0:1], here(base), ALU.subtract))
                    dve.wait_ge(s["xg"], i * 16 + 16)
                    link(nc.vector.tensor_tensor(wf[:, :], rec[:, 2:3], xg[:, P:P + 1], ALU.mult))
                    nc.vector.tensor_scalar(A[:, :], iota_n[:, :], loc[:, 0:1], wf[:, 0:1], ALU.is_equal, ALU.mult).then_inc(s["A"], 1)
                    dve.wait_ge(s["G"], i + 1)
                    link(nc.vector.scalar_tensor_tensor(acc[:, :], acc[:, :], here(keep), pG[:, 0:P], ALU.mult, ALU.add))
                    norm_steps(nc, link, acc[:, :], scr[:, :], at(6), at(16), at(3), at(4), at(5))
                    nc.vector.tensor_copy(at(7), at(16)).then_inc(s["u"], 1)
                    link(nc.vector.tensor_scalar(at(9), at(16), 0.3, None, ALU.min))
                    link(nc.vector.tensor_tensor(at(9), at(9), at(9), ALU.mult))
                    even_poly_steps(nc, link, at(10), at(9), TANH_C, at(4))
                    dve.wait_ge(s["e"], i + 1)
                    link(nc.vector.tensor_scalar(at(11), at(8), 1.0, None, ALU.add))
                    link(nc.vector.reciprocal(at(12), at(11)))
                    link(nc.vector.tensor_scalar(at(11), at(8), -1.0, 1.0, ALU.mult, ALU.add))
                    link(nc.vector.tensor_scalar(at(11), at(11), at(12), at(3), ALU.mult, ALU.mult))
                    link(nc.vector.tensor_tensor(at(10), at(10), at(11), ALU.subtract))
                    link(nc.vector.tensor_scalar(at(4), at(16), 0.3, None, ALU.is_lt))
                    link(nc.vector.scalar_tensor_tensor(at(13), at(10), at(4), at(11), ALU.mult, ALU.add))
                    link(nc.vector.tensor_tensor(at(14), at(13), at(16), ALU.mult))
                    link(nc.vector.tensor_scalar(at(14), at(14), 1e-15, None, ALU.max))
                    link(nc.vector.tensor_scalar(at(4), at(14), 0.996, None, ALU.is_gt))
                    link(nc.vector.reciprocal(at(15), at(14)))
                    link(nc.vector.tensor_scalar(at(15), at(15), 0.996, -1.0, ALU.mult, ALU.add))
                    link(nc.vector.tensor_scalar(at(15), at(15), at(4), None, ALU.mult))
                    link(nc.vector.tensor_scalar(at(15), at(15), 1.0, at(13), ALU.add, ALU.mult))
                    dve.wait_ge(s["x"], i * 16 + 16)
                    link(nc.vector.scalar_tensor_tensor(z[:, :], acc[:, :], at(15), xb[:, 0:P], ALU.mult, ALU.add))
                    link(nc.vector.bn_stats(st6[:, :], z[:, :]), alone=True)
                    link(nc.vector.bn_aggr(c[:, 0:2], st6[:, :]))
                    link(nc.vector.tensor_scalar(at(2), at(1), EPS, None, ALU.add))
                    rsqrt_steps(nc, link, at(3), at(2), at(4), at(5))
                    nc.vector.tensor_scalar(o[:, :], z[:, :], at(0), at(3), ALU.subtract, ALU.mult).then_inc(s["out"], 1)

                    link.end()


_INS = ['x', 'src', 'dst', 'edge_attr_128', 'edge_weight'] + [f'L0_gnn_{p}{k}_l{l}' for l in (0, 1) for k in (1, 2, 3) for p in ('W', 'b')]


def kernel(**inputs):
    import numpy as _np
    import concourse.bacc as _bacc
    from concourse import mybir as _mybir
    from concourse.bass_utils import run_bass_kernel_spmd as _run

    nc = _bacc.Bacc("TRN2", target_bir_lowering=False, num_devices=1)
    arrays, args = {}, []
    for name in _INS:
        a = _np.ascontiguousarray(inputs[name])
        arrays[f"in_{name}_dram"] = a
        args.append(nc.dram_tensor(f"in_{name}_dram", a.shape, _mybir.dt.from_np(a.dtype), kind="ExternalInput").ap())
    args.append(nc.dram_tensor("out_0_dram", (N, P), F32, kind="ExternalOutput").ap())
    build(nc, *args)
    r = _run(nc, [arrays], core_ids=[0])
    return r.results[0]["out_0_dram"]
```

```python
import numpy as np
from contextlib import ExitStack, contextmanager
import concourse.bass as bass
from concourse import mybir

F32, F16, BF16, I32 = mybir.dt.float32, mybir.dt.float16, mybir.dt.bfloat16, mybir.dt.int32
ALU = mybir.AluOpType
ACT = mybir.ActivationFunctionType
AX = mybir.AxisListType

P = 128
N = 50000
E = 50000
NB = -(-N // P)
NPAD = NB * P
KC = 392
EPAD = P * KC
TAIL = E - (P - 1) * KC
ITEMS = NB + NB - 1
IC = -(-ITEMS // P)
FILL_KEY = float(NPAD)
SLOPE = (1.0 / 8.0 + 1.0 / 3.0) / 2.0
EPS = 1e-5
MASKED = -1.0e30
M_NONE = -1.0e29
LANES = 96
W = 2 * LANES
HG = 4
UN = 8
NORM_G = 8
HI, LO = 13, 32
HC = 28
XW = 132


def wait(eng, sem, value):
    eng.wait_ge(sem, value)


def wait_apart(eng, sem, value):
    eng.wait_ge(sem, value)
    eng.nop(nofuse=True)


@contextmanager
def phase_semaphores(nc):
    held = []

    def sem(name):
        held.append(nc.alloc_semaphore(name))
        return held[-1]
    yield sem
    nc.clear_and_free_semaphores(held)
    nc.all_engine_barrier()


@contextmanager
def only_if(eng, flag, wanted):
    value = eng.value_load(flag[0:1, 0:1], min_val=0, max_val=1)
    with eng.If(value == wanted):
        yield


class Chain:

    def __init__(self, eng, sem, per_turn=0, turn=None):
        self.eng, self.sem, self.per_turn, self.turn, self.n = eng, sem, per_turn, turn, 0

    def __call__(self, ins, alone=False):
        self.n += 1
        ins.then_inc(self.sem, 1)
        (wait_apart if alone else wait)(self.eng, self.sem, self.n if self.turn is None else self.turn * self.per_turn + self.n)

    def end(self):
        assert self.turn is None or self.n == self.per_turn, (self.n, self.per_turn)


def rsqrt_steps(nc, link, out, v, t1, t2):
    vi, oi = v.bitcast(I32), out.bitcast(I32)
    link(nc.vector.tensor_scalar(oi, vi, 1, None, ALU.arith_shift_right))
    link(nc.vector.tensor_scalar(oi, oi, -1, 0x5F3759DF, ALU.mult, ALU.add))
    for _ in range(3):
        link(nc.vector.tensor_tensor(t1, out, v, ALU.mult))
        link(nc.vector.tensor_tensor(t2, t1, out, ALU.mult))
        link(nc.vector.tensor_scalar(t1, t2, -0.5, 1.5, ALU.mult, ALU.add))
        link(nc.vector.tensor_tensor(out, out, t1, ALU.mult))


def even_poly_steps(nc, link, out, x2, coefficients, t1):
    link(nc.vector.tensor_scalar(out, x2, coefficients[-1], coefficients[-2], ALU.mult, ALU.add))
    for c in coefficients[-3::-1]:
        link(nc.vector.tensor_tensor(t1, out, x2, ALU.mult))
        link(nc.vector.tensor_scalar(out, t1, c, None, ALU.add))


ARTANH_C = [1.0 / (2 * k + 1) for k in range(6)]
TANH_C = [1.0, -1 / 3, 2 / 15, -17 / 315, 62 / 2835, -1382 / 155925]


def build(nc, x, src, dst, ea, ew, W1a, b1a, W2a, b2a, W3a, b3a, W1b, b1b, W2b, b2b, W3b, b3b, out):
    dram = lambda name, shape, dt: nc.dram_tensor(name, shape, dt, kind="Internal").ap()
    d = {
        "xpad": dram("xpad", [NPAD, P], F32), "h1": dram("h1", [NPAD, P], F32), "h2": dram("h2", [NPAD, P], F32),
        "xtab": dram("xtab", [N, XW], F32), "sup": dram("sup", [NPAD, P], F32),
        "pairs": dram("pairs", [EPAD, 2], I32),
    }
    for kind in ("dst", "src"):
        d[kind, "recs"] = dram(f"{kind}_sorted", [EPAD, 4], F32)
        d[kind, "items"] = dram(f"{kind}_items", [P * IC, 2], I32)
    lay = [(W1a, b1a, W2a, b2a, W3a, b3a), (W1b, b1b, W2b, b2b, W3b, b3b)]

    ctx = ExitStack()
    with ctx:
        sb = lambda name, shape, dt: ctx.enter_context(nc.sbuf_tensor(name, shape, dt))
        sem = lambda name: ctx.enter_context(nc.semaphore(name))

        ident = sb("ident", [P, P], F32)
        identb = sb("identb", [P, P], BF16)
        iota_n = sb("iota_n", [P, P], F32)
        iota_b = sb("iota_b", [P, KC], F32)
        iota_16 = sb("iota_16", [P, KC], F16)
        block_row = sb("block_row", [P, KC], F32)
        below = sb("below", [P, P], BF16)
        notbelow = sb("notbelow", [P, P], BF16)
        onesb = sb("onesb", [P, P], BF16)
        onesf = sb("onesf", [P, P], F32)
        s_const = sem("s_const")
        s_const0 = sem("s_const0")
        with nc.Block() as block:
            @block.gpsimd
            def _(pool):
                pool.memset(ident[:, :], 0.0).then_inc(s_const0, 1)
                pool.memset(identb[:, :], 0.0).then_inc(s_const0, 1)
                pool.memset(onesb[:, :], 1.0).then_inc(s_const0, 1)
                pool.memset(onesf[:, :], 1.0).then_inc(s_const0, 1)
                pool.iota(iota_n[:, :], pattern=[[1, P]], base=0, channel_multiplier=0,
                          allow_small_or_imprecise_dtypes=True).then_inc(s_const, 1)
                pool.iota(iota_b[:, :], pattern=[[1, KC]], base=0, channel_multiplier=0,
                          allow_small_or_imprecise_dtypes=True).then_inc(s_const, 1)
                pool.iota(iota_16[:, :], pattern=[[1, KC]], base=0, channel_multiplier=0,
                          allow_small_or_imprecise_dtypes=True).then_inc(s_const, 1)
                pool.iota(block_row[:, :], pattern=[[P, KC]], base=0, channel_multiplier=0,
                          allow_small_or_imprecise_dtypes=True).then_inc(s_const, 1)
                pool.wait_ge(s_const0, 4)
                for m in (ident, identb):
                    pool.affine_select(out=m[:, :], in_=m[:, :], compare_op=ALU.not_equal, fill=1.0,
                                       base=0, pattern=[[-1, P]], channel_multiplier=1).then_inc(s_const, 1)
                pool.affine_select(out=below[:, :], in_=onesb[:, :], compare_op=ALU.is_gt, fill=0.0,
                                   base=0, pattern=[[1, P]], channel_multiplier=-1).then_inc(s_const, 1)
                pool.affine_select(out=notbelow[:, :], in_=onesb[:, :], compare_op=ALU.is_ge, fill=0.0,
                                   base=0, pattern=[[-1, P]], channel_multiplier=1).then_inc(s_const, 1)
                pool.wait_ge(s_const, 8)

        consts = dict(iota_16=iota_16, ident=ident, identb=identb, iota_n=iota_n, iota_b=iota_b, block_row=block_row,
                      below=below, notbelow=notbelow, onesb=onesb, onesf=onesf)
        tables = {}
        for kind, key_in, oth_in in (("dst", dst, src), ("src", src, dst)):
            tables[kind] = counting_sort(nc, ctx, kind, key_in, oth_in, ew, x, d, consts)
        for l, (hin, hwide, hout) in enumerate(((x, d["xpad"], d["h1"]), (d["h1"], d["h1"], d["h2"]))):
            layer(nc, l, hin, hwide, hout, ea, d, tables["dst"], lay[l], consts)
        row_pass(nc, "first", x, d["h2"], d["xtab"], final=False)
        general_support(nc, d, tables["src"], consts)
        fast_support(nc, d, tables["src"], consts)
        row_pass(nc, "second", d["xtab"], d["sup"], out, final=True)


def counting_sort(nc, outer, kind, key_in, oth_in, ew, x, d, consts):
    is_dst = kind == "dst"
    ob = lambda name, shape, dt: outer.enter_context(nc.sbuf_tensor(f"{kind}_{name}", shape, dt))
    keep, base = ob("keep", [P, P * IC], F32), ob("base", [P, P * IC], F32)
    starts, flag = ob("starts", [P, KC], I32), ob("flag", [P, 1], I32)
    iota_b, below, notbelow, onesb, onesf, ident = (consts[n] for n in ("iota_b", "below", "notbelow", "onesb", "onesf", "ident"))
    ctx = ExitStack()
    with ctx:
        sb = lambda name, shape, dt: ctx.enter_context(nc.sbuf_tensor(f"{kind}_{name}", shape, dt))
        pb = lambda name, shape, dt: ctx.enter_context(nc.psum_tensor(f"{kind}_{name}", shape, dt))
        phase_sem = ctx.enter_context(phase_semaphores(nc))
        sem = lambda name: phase_sem(f"{kind}_{name}")
        ints = sb("ints", [P, 2, KC], I32)
        nxt = sb("nxt", [P, KC], I32)
        pairs = sb("pairs", [P, KC, 2], I32)
        dig_i = sb("dig_i", [P, KC], I32)
        hi = sb("hi", [P, KC], F32)
        lo = sb("lo", [P, KC], F32)
        blk = sb("blk", [P, KC + 4], F32)
        tmp = sb("tmp", [P, KC], F32)
        third = sb("third", [P, KC], F32)
        recs = sb("recs", [P, KC, 4], F32)
        ohi = sb("ohi", [P, 2, HC, HI], BF16)
        olo = sb("olo", [P, 2, HC, LO], BF16)
        hist = sb("hist", [HI, LO], F32)
        diag = sb("diag", [HI, HI, LO], F32)
        oh = sb("oh", [P, 4, KC], BF16)
        scr = sb("scr", [P, KC], F32)
        counts = sb("counts", [P, KC], F32)
        off = sb("off", [P, KC], F32)
        ones = sb("ones", [P, KC], F32)
        few = sb("few", [P, 4], F32)
        posf = sb("posf", [P, 4], F32)
        pos = sb("pos", [P, 4], I32)
        rec4 = sb("rec4", [P, 4, 4], F32)
        tile_i = sb("tile_i", [P, KC], I32)
        last_item = sb("last_item", [P, KC], F32)
        item_id = sb("item_id", [P, IC], F32)
        item_blk = sb("item_blk", [P, IC], F32)
        item_rows = sb("item_rows", [P, IC, 2], I32)
        item_f = sb("item_f", [P, IC, 2], F32)
        rows_bc = sb("rows_bc", [P, P * IC, 2], I32)
        zrow = sb("zrow", [NPAD - N, P], F32)
        bank = [pb(f"bank{i}", [P, 512], F32) for i in range(2)]
        hbank = pb("hbank", [P, 512], F32)
        s_load, s_fill, s_iota, s_dve = sem("load"), sem("fill"), sem("iota"), sem("dve")
        s_digit, s_hmm, s_hist, s_diag, s_total = sem("digit"), sem("hmm"), sem("hist"), sem("diag"), sem("total")
        s_items, s_itab, s_bc, s_pairs, s_pst = sem("items"), sem("itab"), sem("bc"), sem("pairs"), sem("pst")

        with nc.Block() as block:
            @block.gpsimd
            def _(pool):
                pool.memset(ints[:, 0, :], NPAD).then_inc(s_fill, 1)
                pool.memset(ints[:, 1, :], 0).then_inc(s_fill, 1)
                pool.memset(nxt[:, :], NPAD).then_inc(s_fill, 1)
                if is_dst:
                    pool.iota(third[:, :], pattern=[[1, KC]], base=0, channel_multiplier=KC,
                              allow_small_or_imprecise_dtypes=True).then_inc(s_fill, 1)
                else:
                    pool.memset(third[:, :], 0.0).then_inc(s_fill, 1)
                pool.iota(item_id[:, :], pattern=[[1, IC]], base=0, channel_multiplier=IC,
                          allow_small_or_imprecise_dtypes=True).then_inc(s_iota, 1)

            @block.sync
            def _(sp):
                def load(tile, a, n):
                    left = n - (P - 1) * KC
                    sp.dma_start(tile[0:P // 2, :], a[0:P // 2 * KC].rearrange("(p c) -> p c", c=KC)).then_inc(s_load, 16)
                    sp.dma_start(tile[P // 2:P - 1, :], a[P // 2 * KC:(P - 1) * KC].rearrange("(p c) -> p c", c=KC)).then_inc(s_load, 16)
                    sp.dma_start(tile[P - 1:P, 0:left], a[(P - 1) * KC:n].rearrange("(p c) -> p c", c=left)).then_inc(s_load, 16)

                sp.wait_ge(s_fill, 4)
                load(ints[:, 0, :], key_in, E)
                load(ints[:, 1, :], oth_in, E)
                if is_dst:
                    load(nxt[:, :], key_in[1:E], E - 1)
                    sp.wait_ge(s_pairs, 1)
                    sp.dma_start(d["pairs"].rearrange("(p c) t -> p c t", c=KC), pairs[:, :, :]).then_inc(s_pst, 16)
                else:
                    load(third[:, :], ew, E)
                sp.wait_ge(s_items, 1)
                sp.dma_start(d[kind, "items"].rearrange("(p c) t -> p c t", c=IC), item_rows[:, :, :]).then_inc(s_itab, 16)
                sp.wait_ge(s_itab, 16)
                sp.dma_start(rows_bc[:, :, :],
                             d[kind, "items"].rearrange("(o c) t -> o c t", o=1).to_broadcast([P, P * IC, 2])).then_inc(s_bc, 16)
                sp.wait_ge(s_bc, 16)
                if is_dst:
                    sp.wait_ge(s_pst, 16)

            @block.tensor
            def _(pe):
                pe.wait_ge(s_digit, 1)
                nc.tensor.matmul(hbank[0:HI, 0:LO], ohi[:, 0, 0, :], olo[:, 0, 0, :], start=True, stop=True, skip_group_check=True).then_inc(s_hmm, 1)
                with pe.Fori(0, KC // HC // 2) as q:
                    for b in range(2):
                        pe.wait_ge(s_digit, q * 2 + (b + 2))
                        for c in range(HC):
                            last = nc.tensor.matmul(hbank[0:HI, 0:LO], ohi[:, b, c, :], olo[:, b, c, :], start=False, stop=True, skip_group_check=True)
                        last.then_inc(s_hmm, 1)
                pe.wait_ge(s_diag, 1)
                if is_dst:
                    nc.tensor.matmul(bank[1][:, 0:1], onesf[:, :], few[:, 0:1], start=True, stop=True)
                nc.tensor.matmul(bank[0][:, 0:HI * LO], onesf[0:HI, :], diag[:, :, :].rearrange("p a b -> p (a b)"), start=True, stop=True).then_inc(s_total, 1)

            @block.vector
            def _(dve):
                link = Chain(dve, s_dve)
                link(nc.vector.memset(ohi[:, :, :, :], 0.0))
                nc.vector.memset(olo[:, :, :, :], 0.0).then_inc(s_digit, 1)
                link(nc.vector.memset(blk[:, :], 0.0))
                link(nc.vector.memset(recs[:, :, :], 0.0))
                link(nc.vector.memset(ones[:, :], 1.0))
                dve.wait_ge(s_load, 9 * 16)
                link(nc.vector.tensor_scalar(dig_i[:, :], ints[:, 0, :], 7, None, ALU.arith_shift_right))
                link(nc.vector.tensor_copy(blk[:, 0:KC], dig_i[:, :]))
                link(nc.vector.tensor_scalar(dig_i[:, :], dig_i[:, :], 5, None, ALU.arith_shift_right))
                link(nc.vector.tensor_copy(hi[:, :], dig_i[:, :]))
                link(nc.vector.scalar_tensor_tensor(lo[:, :], hi[:, :], -float(LO), blk[:, 0:KC], ALU.mult, ALU.add))
                with dve.Fori(0, KC // HC // 2) as q:
                    for b in range(2):
                        dve.wait_ge(s_hmm, q * 2 + 1)
                        for oh_d, dig, n in ((ohi, hi, HI), (olo, lo, LO)):
                            last = nc.vector.tensor_tensor(
                                oh_d[:, b, :, :], dig[:, bass.ds((q * 2 + b) * HC, HC)].unsqueeze(2).to_broadcast([P, HC, n]),
                                iota_b[:, 0:n].unsqueeze(1).to_broadcast([P, HC, n]), ALU.is_equal)
                        last.then_inc(s_digit, 1)
                link(nc.vector.tensor_copy(recs[:, :, 0], ints[:, 0, :]))
                link(nc.vector.tensor_copy(recs[:, :, 1], ints[:, 1, :]))
                if is_dst:
                    link(nc.vector.tensor_scalar(tmp[:, :], third[:, :], float(E), None, ALU.is_lt))
                    link(nc.vector.tensor_tensor(recs[:, :, 2], third[:, :], tmp[:, :], ALU.mult))
                    link(nc.vector.tensor_copy(pairs[:, :, 0], ints[:, 0, :]))
                    nc.vector.tensor_copy(pairs[:, :, 1], ints[:, 1, :]).then_inc(s_pairs, 1)
                    link(nc.vector.tensor_tensor(tmp[:, :], nxt[:, :], ints[:, 0, :], ALU.is_lt))
                    link(nc.vector.reduce_sum(few[:, 0:1], tmp[:, :], AX.X))
                else:
                    link(nc.vector.tensor_copy(recs[:, :, 2], third[:, :]))
                dve.wait_ge(s_hmm, KC // HC + 1)
                link(nc.vector.tensor_copy(hist[:, :], hbank[0:HI, 0:LO]))
                nc.vector.tensor_tensor(diag[:, :, :], hist[:, :].unsqueeze(1).to_broadcast([HI, HI, LO]),
                                        ident[0:HI, 0:HI].unsqueeze(2).to_broadcast([HI, HI, LO]), ALU.mult).then_inc(s_diag, 1)
                dve.wait_ge(s_total, 1)
                link(nc.vector.tensor_copy(counts[:, :], bank[0][:, 0:KC]))
                link(nc.vector.reduce_max(few[:, 1:2], counts[:, 0:NB], AX.X))
                link(nc.vector.tensor_scalar(few[:, 2:3], few[:, 1:2], float(W), None, ALU.is_le))
                if is_dst:
                    link(nc.vector.tensor_scalar(few[:, 3:4], bank[1][:, 0:1], 0.0, None, ALU.is_equal))
                    link(nc.vector.tensor_tensor(few[:, 2:3], few[:, 2:3], few[:, 3:4], ALU.mult))
                link(nc.vector.tensor_copy(flag[:, :], few[:, 2:3]))
                link(nc.vector.tensor_tensor_scan(off[:, :], ones[:, :], counts[:, :], 0.0, ALU.mult, ALU.add))
                link(nc.vector.tensor_copy(tile_i[:, :], off[:, :]))
                link(nc.vector.tensor_scalar(tile_i[:, :], tile_i[:, :], 7, None, ALU.arith_shift_right))
                link(nc.vector.tensor_tensor(last_item[:, :], tile_i[:, :], iota_b[:, :], ALU.add))
                link(nc.vector.tensor_tensor(off[:, :], off[:, :], counts[:, :], ALU.subtract))
                link(nc.vector.tensor_scalar(starts[:, :], off[:, :], float(E - W), None, ALU.min))
                dve.wait_ge(s_iota, 1)
                for j in range(IC):
                    link(nc.vector.tensor_scalar(scr[:, 0:NB], last_item[:, 0:NB], item_id[:, j:j + 1], None,
                                                 ALU.is_lt, ALU.add, accum_out=item_blk[:, j:j + 1]))
                link(nc.vector.tensor_scalar(item_f[:, :, 0], item_blk[:, :], float(P), None, ALU.mult))
                link(nc.vector.tensor_tensor(item_f[:, :, 1], item_id[:, :], item_blk[:, :], ALU.subtract))
                link(nc.vector.tensor_scalar(item_f[:, :, 1], item_f[:, :, 1], float(P), None, ALU.mult))
                nc.vector.tensor_copy(item_rows[:, :, :], item_f[:, :, :]).then_inc(s_items, 1)
                dve.wait_ge(s_bc, 16)
                link(nc.vector.tensor_copy(base[:, :], rows_bc[:, :, 0]))
                link(nc.vector.memset(keep[:, 0:1], 0.0))
                link(nc.vector.tensor_tensor(keep[:, 1:], base[:, 1:], base[:, :P * IC - 1], ALU.is_equal))

        s_oh, s_cnt, s_rank, s_posf, s_pos, s_rec = (sem(n) for n in ("oh", "cnt", "rank", "posf", "pos", "rec"))
        s_sc = [sem(f"sc{i}") for i in range(4)]
        s_cp, s_z = sem("cp"), sem("z")
        with nc.Block() as block:
            def guarded(eng, program):
                if not is_dst:
                    return program()
                with only_if(eng, flag, 0):
                    program()

            @block.gpsimd
            def _(pool):
                def program():
                    if is_dst:
                        pool.memset(zrow[:, :], 0.0).then_inc(s_z, 1)
                    last_row = pool.to_reg(EPAD - 1)
                    with pool.Fori(0, KC // 4) as q:
                        for j in range(4):
                            pool.wait_ge(s_pos, q * 4 + (j + 1))
                            wait_apart(pool, s_rec, q * 4 + (j + 1))
                            pool.indirect_dma_start(
                                out=d[kind, "recs"], out_offset=bass.IndirectOffsetOnAxis(ap=pos[:, j:j + 1], axis=0),
                                in_=rec4[:, j, :], in_offset=None, bounds_check=last_row, oob_is_err=False,
                            ).then_inc(s_sc[j], 16)
                    for j in range(4):
                        pool.wait_ge(s_sc[j], 16 * KC // 4)
                guarded(pool, program)

            @block.sync
            def _(sp):
                if is_dst:
                    def program():
                        sp.dma_start(d["xpad"][0:N, :], x).then_inc(s_cp, 16)
                        sp.wait_ge(s_z, 1)
                        sp.dma_start(d["xpad"][N:NPAD, :], zrow[:, :]).then_inc(s_cp, 16)
                        sp.wait_ge(s_cp, 32)
                    guarded(sp, program)

            @block.vector
            def _(dve):
                def onehot(q, j):
                    nc.vector.tensor_scalar(oh[:, j % 4, :], consts["iota_16"][:, :], blk[:, bass.ds(q * 4 + j, 1)], None,
                                            ALU.is_equal).then_inc(s_oh, 1)

                def turn(q):
                    for j in range(4):
                        dve.wait_ge(s_cnt, q * 4 + (j + 1))
                        nc.vector.scalar_tensor_tensor(scr[:, :], iota_b[:, :], blk[:, bass.ds(q * 4 + j, 1)],
                                                       bank[j % 2][:, 0:KC], ALU.is_equal, ALU.mult,
                                                       accum_out=posf[:, j:j + 1]).then_inc(s_rank, 1)
                        onehot(q, j + 2)
                        if not (isinstance(q, int) and q == 0):
                            dve.wait_ge(s_sc[j], q * 16)
                        dve.wait_ge(s_rank, q * 4 + (j + 3))
                        nc.vector.tensor_copy(pos[:, j:j + 1], posf[:, j:j + 1]).then_inc(s_pos, 1)
                        nc.vector.tensor_copy(rec4[:, j, :], recs[:, bass.ds(q * 4 + j, 1), :].rearrange("p a b -> p (a b)")).then_inc(s_rec, 1)

                def program():
                    nc.vector.memset(oh[:, :, :], 0.0).then_inc(s_rank, 2)
                    dve.wait_ge(s_rank, 2)
                    onehot(0, 0)
                    onehot(0, 1)
                    turn(0)
                    with dve.Fori(1, KC // 4) as q:
                        turn(q)
                guarded(dve, program)

            @block.tensor
            def _(pe):
                mm = lambda c, w, j, **k: nc.tensor.matmul(bank[c][:, 0:KC], w[:, :], oh[:, j, :], skip_group_check=True, **k)

                def program():
                    for c in range(2):
                        nc.tensor.matmul(bank[c][:, 0:KC], onesf[0:1, :], off[0:1, :], start=True, stop=True, skip_group_check=True)
                    with pe.Fori(0, KC // 4) as q:
                        for j in range(4):
                            pe.wait_ge(s_oh, q * 4 + (j + 1))
                            pe.wait_ge(s_rank, q * 4 + (j + 1))
                            mm(j % 2, notbelow, (j - 2) % 4, start=False, stop=True)
                            mm(j % 2, onesb, (j - 1) % 4, start=False, stop=True)
                            mm(j % 2, below, j, start=False, stop=True).then_inc(s_cnt, 1)
                guarded(pe, program)
    return dict(keep=keep, base=base, starts=starts, flag=flag)


def layer(nc, l, hin, hwide, hout, ea, d, tab, weights, consts):
    general_layer(nc, l, hwide, hout, ea, d, tab, weights, consts)
    fast_layer(nc, l, hin, hout, ea, d, tab, weights, consts)


def general_layer(nc, l, hin, hout, ea, d, tab, weights, consts):
    keep, base, flag = tab["keep"], tab["base"], tab["flag"]
    recs, items = d["dst", "recs"], d["dst", "items"]
    ident, identb, iota_n = consts["ident"], consts["identb"], consts["iota_n"]
    W1, b1, W2, b2, W3, b3 = weights
    ctx = ExitStack()
    with ctx:
        sb = lambda name, shape, dt: ctx.enter_context(nc.sbuf_tensor(f"l{l}_{name}", shape, dt))
        pb = lambda name, shape, dt: ctx.enter_context(nc.psum_tensor(f"l{l}_{name}", shape, dt))
        phase_sem = ctx.enter_context(phase_semaphores(nc))
        sem = lambda name: phase_sem(f"l{l}_{name}")
        w1 = sb("w1", [P, P], F32)
        w1t = sb("w1t", [P, P], F32)
        w23 = sb("w23", [P, 2, P], F32)
        w2 = sb("w2", [P, P], F32)
        b1col = sb("b1col", [P, 1], F32)
        b1bc = sb("b1bc", [P, P], F32)
        brow = sb("brow", [P, 3, P], F32)
        b23 = sb("b23", [P, 2, P], F32)
        rec = sb("rec", [P, 4], F32)
        idx = sb("idx", [P, 2], I32)
        hb = sb("hb", [P, P], F32)
        hs = sb("hs", [P, P], F32)
        ev = sb("ev", [P, P], F32)
        g = sb("g", [P, P], F32)
        loc = sb("loc", [P, 1], F32)
        pen = sb("pen", [P, P], BF16)
        hT = sb("hT", [P, P], F32)
        qT = sb("qT", [P, P], F32)
        gT = sb("gT", [P, P], F32)
        w = sb("w", [P, P], F32)
        wT = sb("wT", [P, P], F32)
        acc = sb("acc", [P, P], F32)
        accn = sb("accn", [P, P], F32)
        accT = sb("accT", [P, P], F32)
        A = sb("A", [P, 2, P], F32)
        pre = sb("pre", [P, P], F32)
        o = sb("o", [P, P], F32)
        st = sb("st", [P, 16], F32)
        col = {n: st[:, k:k + 1] for k, n in enumerate(
            ("M", "L", "Mold", "mx", "Mn", "nMn", "alpha", "Lnew", "ka", "inv", "has", "t"))}
        pT, pQ, pA, pS, pW, pG, pN, pT2 = [pb(f"p{k}", [P, 512], F32) for k in range(8)]
        names = ("wload", "wdve", "wT", "prep", "rec", "h", "idx", "hs", "ev", "g", "pen", "hT", "hTs", "q", "qs",
                 "a", "gT", "gTs", "s", "m", "al", "w", "wTp", "wTs", "G", "accn", "aT", "aTs", "N", "out", "st", "dve")
        s = {n: sem(n) for n in names}
        K = 14

        with nc.Block() as block:
            @block.sync
            def _(sp):
                with only_if(sp, flag, 0):
                    sp.dma_start(w1[:, :], W1).then_inc(s["wload"], 16)
                    sp.dma_start(w2[:, :], W2).then_inc(s["wload"], 16)
                    sp.dma_start(w23[:, 0, :], W3).then_inc(s["wload"], 16)
                    for n, b in enumerate((b1, b2, b3)):
                        sp.dma_start(brow[:, n, :], b.rearrange("(o n) -> o n", o=1).to_broadcast([P, P])).then_inc(s["wload"], 16)
                    sp.dma_start(b1col[:, :], b1.rearrange("(n o) -> n o", o=1)).then_inc(s["wload"], 16)
                    with sp.Fori(0, ITEMS) as i:
                        row = sp.value_load(items[bass.ds(i, 1), 0:1], min_val=0, max_val=NPAD - P)
                        erow = sp.value_load(items[bass.ds(i, 1), 1:2], min_val=0, max_val=EPAD - P)
                        sp.dma_start(rec[:, :], recs[bass.ds(erow, P), :]).then_inc(s["rec"], 16)
                        sp.dma_start(hb[:, :], hin[bass.ds(row, P), :]).then_inc(s["h"], 16)
                        sp.wait_ge(s["out"], i + 1)
                        sp.dma_start(hout[bass.ds(row, P), :], o[:, :]).then_inc(s["st"], 16)
                        wait_apart(sp, s["st"], i * 16 + 16)

            @block.gpsimd
            def _(pool):
                with only_if(pool, flag, 0):
                    last_row = pool.to_reg(N - 1)
                    with pool.Fori(0, ITEMS) as i:
                        wait_apart(pool, s["idx"], i + 1)
                        pool.indirect_dma_start(out=hs[:, :], out_offset=None, in_=hin,
                                                in_offset=bass.IndirectOffsetOnAxis(ap=idx[:, 0:1], axis=0),
                                                bounds_check=last_row, oob_is_err=False).then_inc(s["hs"], 16)
                        pool.indirect_dma_start(out=ev[:, :], out_offset=None, in_=ea,
                                                in_offset=bass.IndirectOffsetOnAxis(ap=idx[:, 1:2], axis=0),
                                                bounds_check=last_row, oob_is_err=False).then_inc(s["ev"], 16)

            @block.vector
            def _(dve):
                with only_if(dve, flag, 0):
                    dve.wait_ge(s["wload"], 7 * 16)
                    link = Chain(dve, s["wdve"])
                    link(nc.vector.tensor_tensor(w23[:, 1, :], w2[:, :], w23[:, 0, :], ALU.subtract))
                    link(nc.vector.tensor_copy(b23[:, 0, :], brow[:, 2, :]))
                    link(nc.vector.tensor_tensor(b23[:, 1, :], brow[:, 0, :], brow[:, 1, :], ALU.add))
                    link(nc.vector.tensor_tensor(b23[:, 1, :], b23[:, 1, :], brow[:, 2, :], ALU.subtract))
                    link(nc.vector.memset(b1bc[:, :], 0.0))
                    link(nc.vector.tensor_scalar(b1bc[:, :], b1bc[:, :], b1col[:, 0:1], None, ALU.add))
                    link(nc.vector.memset(st[:, :], 0.0))
                    link(nc.vector.memset(acc[:, :], 0.0))
                    dve.wait_ge(s["wT"], 1)
                    nc.vector.tensor_copy(w1t[:, :], pT[:, 0:P]).then_inc(s["prep"], 1)
                    dve.wait_ge(s["prep"], 1)
                    with dve.Fori(0, ITEMS) as i:
                        link = Chain(dve, s["dve"], K, i)
                        here = lambda t: t[:, bass.ds(i, 1)]
                        dve.wait_ge(s["rec"], i * 16 + 16)
                        nc.vector.tensor_copy(idx[:, :], rec[:, 1:3]).then_inc(s["idx"], 1)
                        link(nc.vector.tensor_tensor(loc[:, :], rec[:, 0:1], here(base), ALU.subtract))
                        nc.vector.tensor_scalar(pen[:, :], iota_n[:, :], loc[:, 0:1], MASKED, ALU.not_equal, ALU.mult).then_inc(s["pen"], 1)
                        dve.wait_ge(s["hs"], i * 16 + 16)
                        dve.wait_ge(s["ev"], i * 16 + 16)
                        nc.vector.tensor_tensor(g[:, :], hs[:, :], ev[:, :], ALU.add).then_inc(s["g"], 1)
                        link(nc.vector.tensor_tensor(col["Mold"], col["M"], here(keep), ALU.mult))
                        link(nc.vector.tensor_scalar(col["t"], here(keep), -1.0, -M_NONE, ALU.add, ALU.mult))
                        link(nc.vector.tensor_tensor(col["Mold"], col["Mold"], col["t"], ALU.add))
                        dve.wait_ge(s["s"], i + 1)
                        link(nc.vector.reduce_max(col["mx"], pS[:, 0:P], AX.X))
                        link(nc.vector.tensor_tensor(col["Mn"], col["mx"], col["Mold"], ALU.max))
                        nc.vector.tensor_scalar(col["nMn"], col["Mn"], -1.0, None, ALU.mult).then_inc(s["m"], 1)
                        dve.wait_ge(s["al"], i + 1)
                        link(nc.vector.tensor_tensor(col["ka"], col["alpha"], here(keep), ALU.mult))
                        dve.wait_ge(s["w"], i + 1)
                        link(nc.vector.scalar_tensor_tensor(col["L"], col["L"], col["ka"], col["Lnew"], ALU.mult, ALU.add))
                        link(nc.vector.tensor_copy(col["M"], col["Mn"]))
                        dve.wait_ge(s["G"], i + 1)
                        link(nc.vector.scalar_tensor_tensor(acc[:, :], acc[:, :], col["ka"], pG[:, 0:P], ALU.mult, ALU.add))
                        link(nc.vector.tensor_scalar(col["t"], col["L"], 1e-30, None, ALU.max))
                        link(nc.vector.reciprocal(col["inv"], col["t"]))
                        link(nc.vector.tensor_scalar(col["has"], col["L"], 0.0, None, ALU.is_gt))
                        nc.vector.tensor_scalar(accn[:, :], acc[:, :], col["inv"], None, ALU.mult).then_inc(s["accn"], 1)
                        dve.wait_ge(s["a"], i + 1)
                        link(nc.vector.tensor_tensor(A[:, :, :], pA[:, 0:2 * P].rearrange("p (a b) -> p a b", a=2), b23[:, :, :], ALU.add))
                        dve.wait_ge(s["accn"], i + 1)
                        nc.vector.scalar_tensor_tensor(pre[:, :], A[:, 1, :], col["has"], A[:, 0, :], ALU.mult, ALU.add).then_inc(s["wdve"], 1)
                        dve.wait_ge(s["wdve"], i * 2 + 8 + 1)
                        dve.wait_ge(s["N"], i + 1)
                        nc.vector.tensor_tensor(accn[:, :], pre[:, :], pN[:, 0:P], ALU.add).then_inc(s["wdve"], 1)
                        dve.wait_ge(s["wdve"], i * 2 + 8 + 2)
                        nc.vector.scalar_tensor_tensor(o[:, :], accn[:, :], SLOPE, accn[:, :], ALU.mult, ALU.max).then_inc(s["out"], 1)
                        link.end()

            @block.scalar
            def _(act):
                with only_if(act, flag, 0):
                    with act.Fori(0, ITEMS) as i:
                        act.wait_ge(s["hT"], i + 1)
                        nc.scalar.copy(hT[:, :], pT[:, 0:P]).then_inc(s["hTs"], 1)
                        act.wait_ge(s["q"], i + 1)
                        nc.scalar.copy(qT[:, :], pQ[:, 0:P]).then_inc(s["qs"], 1)
                        act.wait_ge(s["gT"], i + 1)
                        nc.scalar.copy(gT[:, :], pT2[:, 0:P]).then_inc(s["gTs"], 1)
                        act.wait_ge(s["m"], i + 1)
                        nc.scalar.activation(col["alpha"], col["Mold"], ACT.Exp, bias=col["nMn"]).then_inc(s["al"], 1)
                        nc.scalar.activation(w[:, :], pS[:, 0:P], ACT.Exp, bias=col["nMn"], accum_out=col["Lnew"]).then_inc(s["w"], 1)
                        act.wait_ge(s["wTp"], i + 1)
                        nc.scalar.copy(wT[:, :], pW[:, 0:P]).then_inc(s["wTs"], 1)
                        act.wait_ge(s["aT"], i + 1)
                        nc.scalar.copy(accT[:, :], pW[:, P:2 * P]).then_inc(s["aTs"], 1)

            @block.tensor
            def _(pe):
                with only_if(pe, flag, 0):
                    pe.wait_ge(s["wload"], 7 * 16)
                    nc.tensor.transpose(pT[:, 0:P], w1[:, :], ident[:, :]).then_inc(s["wT"], 1)
                    pe.wait_ge(s["prep"], 1)
                    with pe.Fori(0, ITEMS) as i:
                        pe.wait_ge(s["h"], i * 16 + 16)
                        nc.tensor.transpose(pT[:, 0:P], hb[:, :], ident[:, :]).then_inc(s["hT"], 1)
                        pe.wait_ge(s["hTs"], i + 1)
                        nc.tensor.matmul(pQ[:, 0:P], w1t[:, :], hT[:, :], start=True, stop=True).then_inc(s["q"], 1)
                        nc.tensor.matmul(pA[:, 0:2 * P], hT[:, :], w23[:, :, :].rearrange("p a b -> p (a b)"), start=True, stop=True).then_inc(s["a"], 1)
                        pe.wait_ge(s["g"], i + 1)
                        nc.tensor.transpose(pT2[:, 0:P], g[:, :], ident[:, :]).then_inc(s["gT"], 1)
                        pe.wait_ge(s["qs"], i + 1)
                        pe.wait_ge(s["gTs"], i + 1)
                        pe.wait_ge(s["pen"], i + 1)
                        nc.tensor.matmul(pS[:, 0:P], qT[:, :], gT[:, :], start=True, stop=False)
                        nc.tensor.matmul(pS[:, 0:P], hT[:, :], b1bc[:, :], start=False, stop=False)
                        nc.tensor.matmul(pS[:, 0:P], pen[:, :], identb[:, :], start=False, stop=True).then_inc(s["s"], 1)
                        pe.wait_ge(s["w"], i + 1)
                        nc.tensor.transpose(pW[:, 0:P], w[:, :], ident[:, :]).then_inc(s["wTp"], 1)
                        pe.wait_ge(s["wTs"], i + 1)
                        nc.tensor.matmul(pG[:, 0:P], wT[:, :], g[:, :], start=True, stop=True).then_inc(s["G"], 1)
                        pe.wait_ge(s["accn"], i + 1)
                        nc.tensor.transpose(pW[:, P:2 * P], accn[:, :], ident[:, :]).then_inc(s["aT"], 1)
                        pe.wait_ge(s["aTs"], i + 1)
                        nc.tensor.matmul(pN[:, 0:P], accT[:, :], w1[:, :], start=True, stop=True).then_inc(s["N"], 1)


RSQRT_K = 2 + 4 * 3
POLY_K = 1 + 2 * 4
NORMALISE_K = 3 + RSQRT_K
FIRST_K = 1 + NORMALISE_K + 2 + RSQRT_K + 3 + 2 + POLY_K + 5
SECOND_K = 2 + RSQRT_K + 3 + 2 + POLY_K + 9 + 8 + 1 + NORMALISE_K


class OffsetChain(Chain):

    def __init__(self, eng, sem, per_turn, turn, ahead):
        super().__init__(eng, sem, per_turn, turn)
        self.ahead = ahead

    def __call__(self, ins, alone=False):
        self.n += 1
        ins.then_inc(self.sem, 1)
        (wait_apart if alone else wait)(self.eng, self.sem, self.turn * self.per_turn + (self.n + self.ahead))


class Block_:

    def __init__(self, q, k):
        self.q, self.k = q, k

    def __sub__(self, back):
        return Block_(self.q, self.k - back)

    def __add__(self, ahead):
        return Block_(self.q, self.k + ahead)

    @property
    def number(self):
        return self.q * UN + self.k

    @property
    def slot(self):
        return self.k % UN

    def count(self, more=1):
        return self.q * UN + (self.k + more)

    def dma_count(self, turns_back=0):
        return (self.q + (self.k // UN + 1 - turns_back)) * 16

    def exists(self, back=0):
        if not isinstance(self.q, int):
            return True
        return 0 <= self.number - back < NB


def fast_turns(eng, body, ahead, behind):
    whole = NB // UN
    for k in range(-ahead, 2 * UN):
        body(Block_(0, k))
    with eng.Fori(2, whole - 1) as q:
        for k in range(UN):
            body(Block_(q, k))
    for k in range(UN + NB % UN + behind):
        body(Block_(whole - 1, k))


def fast_layer(nc, l, hin, hout, ea, d, tab, weights, consts):
    W1, b1, W2, b2, W3, b3 = weights
    ident, identb, iota_n, block_row = (consts[n] for n in ("ident", "identb", "iota_n", "block_row"))
    starts, flag = tab["starts"], tab["flag"]
    CB, CQ = 2 * P, 2 * P + 4
    AQ = CQ + P
    AHEAD = 6
    ctx = ExitStack()
    with ctx:
        sb = lambda name, shape, dt: ctx.enter_context(nc.sbuf_tensor(f"q{l}_{name}", shape, dt))
        pb = lambda name, shape, dt: ctx.enter_context(nc.psum_tensor(f"q{l}_{name}", shape, dt))
        phase_sem = ctx.enter_context(phase_semaphores(nc))
        sem = lambda name: phase_sem(f"q{l}_{name}")
        w1 = sb("w1", [P, P], F32)
        w1t = sb("w1t", [P, P], F32)
        w23 = sb("w23", [P, CQ], F32)
        w2 = sb("w2", [P, P], F32)
        brow = sb("brow", [3, 3, P], F32)
        bias = sb("bias", [3, CQ], F32)
        left = sb("left", [3, 2, CQ], F32)
        part = sb("part", [3, 3, CQ], BF16)
        own = sb("own", [3, 3, CQ], F32)
        parts = sb("parts", [3, CQ], BF16)
        rec = sb("rec", [LANES, UN, 2, 2], I32)
        hb = sb("hb", [P, UN, P], F32)
        hs = sb("hs", [LANES, UN, 2 * P], F32)
        ev = sb("ev", [LANES, UN, 2 * P], F32)
        g = sb("g", [LANES, UN, 2 * P], F32)
        loc = sb("loc", [LANES, UN, 2], F32)
        iota_h = sb("iota_h", [LANES, P], BF16)
        pen = sb("pen", [LANES, UN, 2, P], BF16)
        hgT = sb("hgT", [P, 4, P + W], F32)
        aq = sb("aq", [P, UN, AQ], F32)
        w = sb("w", [P, 2, W], F32)
        wT = sb("wT", [LANES, 2, 2, P], F32)
        sT = sb("sT", [P, 2, P], F32)
        pre = sb("pre", [P, 2, P], F32)
        o = sb("o", [P, UN, P], F32)
        col = {n: sb(n, [P, UN], F32) for n in ("mx", "M", "nM", "L", "Lg", "inv", "has")}
        pT = [pb(f"pT{k}", [P, 512], F32) for k in range(2)]
        pS = [pb(f"pS{k}", [P, 512], F32) for k in range(2)]
        pA, pW, pG, pN = (pb(n, [P, 512], F32) for n in ("pA", "pW", "pG", "pN"))
        s_wload, s_wT, s_prep, s_w = sem("wload"), sem("wT"), sem("prep"), sem("wdve")
        ring = lambda name: [sem(f"{name}{k}") for k in range(UN)]
        groups = lambda name: [sem(f"{name}{k}") for k in range(UN // HG)]
        s_h, s_st = groups("h"), groups("st")
        s_rec, s_ev, s_hsa, s_hsb = (ring(n) for n in ("rec", "ev", "hsa", "hsb"))
        (s_g, s_loc, s_pen, s_T, s_evT, s_A, s_evA, s_S, s_mx, s_M, s_nM, s_exp, s_Wt, s_evW, s_G, s_evG, s_N,
         s_L, s_inv, s_mix, s_pre, s_sum, s_out) = (
            sem(n) for n in ("g", "loc", "pen", "T", "evT", "A", "evA", "S", "mx", "M", "nM", "exp", "Wt", "evW", "G",
                             "evG", "N", "L", "inv", "mix", "pre", "sum", "out"))

        with nc.Block() as block:
            @block.sync
            def _(sp):
                begins = {}

                def begin(n):
                    if n.exists():
                        begins[n.slot] = sp.value_load(starts[0:1, bass.ds(n.number, 1)], min_val=0, max_val=E - W)

                def loads(n):
                    if not n.exists():
                        return
                    k = n.slot
                    start = begins[k]
                    if n.exists(UN):
                        sp.wait_ge(s_pen, n.count(1 - UN))
                        sp.wait_ge(s_g, n.count(1 - UN))
                    sp.dma_start(rec[:, k, :, :], d["pairs"][bass.ds(start, W), :].rearrange("(p j) t -> p j t", j=2)).then_inc(s_rec[k], 16)
                    sp.dma_start(ev[:, k, :], ea[bass.ds(start, W), :].rearrange("(p j) f -> p (j f)", j=2)).then_inc(s_ev[k], 16)

                def rows(n):
                    if not n.exists() or n.slot % HG:
                        return
                    k = n.slot
                    if n.exists(UN):
                        sp.wait_ge(s_T, n.count(HG - UN))
                    left = NB - n.number if isinstance(n.q, int) else HG
                    if left >= HG:
                        sp.dma_start(hb[:, k:k + HG, :], hin[bass.ds(n.number * P, HG * P), :].rearrange("(b p) f -> p b f", p=P)).then_inc(s_h[k // HG], 16)
                    else:
                        first = n.number * P
                        last = (NB - 1) * P
                        sp.dma_start(hb[:, k:k + left - 1, :], hin[first:last, :].rearrange("(b p) f -> p b f", p=P)).then_inc(s_h[k // HG], 16)
                        sp.dma_start(hb[0:hin.shape[0] - last, k + left - 1, :], hin[last:hin.shape[0], :]).then_inc(s_h[k // HG], 16)

                def store(n):
                    if not n.exists() or (n.slot % HG != HG - 1 and not (isinstance(n.q, int) and n.number == NB - 1)):
                        return
                    count = n.slot % HG + 1
                    first = n - (count - 1)
                    sp.wait_ge(s_out, n.count())
                    sp.dma_start(hout[bass.ds(first.number * P, count * P), :].rearrange("(b p) f -> p b f", p=P),
                                 o[:, first.slot:n.slot + 1, :]).then_inc(s_st[n.slot // HG], 16)

                def body(n):
                    if n.slot % HG == 0:
                        for k in range(HG):
                            begin(n + (AHEAD + k))
                    rows(n + 4)
                    loads(n + AHEAD)
                    store(n - 8)

                with only_if(sp, flag, 1):
                    sp.dma_start(w1[:, :], W1).then_inc(s_wload, 16)
                    sp.dma_start(w2[:, :], W2).then_inc(s_wload, 16)
                    sp.dma_start(w23[:, 0:P], W3).then_inc(s_wload, 16)
                    sp.dma_start(w23[:, 2 * P:2 * P + 1], b1.rearrange("(n o) -> n o", o=1)).then_inc(s_wload, 16)
                    for n, b in enumerate((b1, b2, b3)):
                        sp.dma_start(brow[:, n, :], b.rearrange("(o n) -> o n", o=1).to_broadcast([3, P])).then_inc(s_wload, 16)
                    fast_turns(sp, body, 8, 8)
                    for k in range(UN // HG):
                        sp.wait_ge(s_st[k], 16 * len(range(HG * k, NB, UN)))

            @block.gpsimd
            def _(pool):
                def body(last_row, n):
                    m = n + 2
                    if not m.exists():
                        return
                    k = m.slot
                    if m.exists(UN):
                        pool.wait_ge(s_g, m.count(1 - UN))
                    wait_apart(pool, s_rec[k], m.dma_count())
                    for j, s in enumerate((s_hsa, s_hsb)):
                        pool.indirect_dma_start(out=hs[:, k, j * P:(j + 1) * P], out_offset=None, in_=hin,
                                                in_offset=bass.IndirectOffsetOnAxis(ap=rec[:, k, j, 1:2], axis=0),
                                                bounds_check=last_row, oob_is_err=False).then_inc(s[k], 16)

                with only_if(pool, flag, 1):
                    last_row = pool.to_reg(N - 1)
                    fast_turns(pool, lambda n: body(last_row, n), 2, 0)

            @block.vector
            def _(dve):
                V = nc.vector
                at = lambda name, n: col[name][:, n.slot:n.slot + 1]

                def mask(n):
                    k = n.slot
                    dve.wait_ge(s_rec[k], n.dma_count())
                    V.tensor_scalar(loc[:, k, :], rec[:, k, :, 0], block_row[0:LANES, bass.ds(n.number, 1)], None, ALU.subtract).then_inc(s_loc, 1)

                def mask_rows(n):
                    k = n.slot
                    dve.wait_ge(s_loc, n.count())
                    for j in range(2):
                        last = V.tensor_scalar(pen[:, k, j, :], iota_h[:, :], loc[:, k, j:j + 1], MASKED, ALU.not_equal, ALU.mult)
                    last.then_inc(s_pen, 1)

                def add_edges(n):
                    k = n.slot
                    dve.wait_ge(s_ev[k], n.dma_count())
                    dve.wait_ge(s_hsa[k], n.dma_count())
                    dve.wait_ge(s_hsb[k], n.dma_count())
                    if n.exists(UN):
                        dve.wait_ge(s_G, n.count(1 - UN))
                    V.tensor_tensor(g[:, k, :], hs[:, k, :], ev[:, k, :], ALU.add).then_inc(s_g, 1)

                def maximum(n):
                    dve.wait_ge(s_S, n.count())
                    V.reduce_max(at("mx", n), pS[n.slot % 2][:, 0:W], AX.X).then_inc(s_mx, 1)

                def maximum_2(n):
                    dve.wait_ge(s_evA, n.count())
                    dve.wait_ge(s_mx, n.count())
                    V.tensor_scalar(at("M", n), at("mx", n), aq[:, n.slot, CB:CB + 1], M_NONE, ALU.add, ALU.max).then_inc(s_M, 1)

                def maximum_3(n):
                    dve.wait_ge(s_M, n.count())
                    V.tensor_tensor(at("nM", n), aq[:, n.slot, CB:CB + 1], at("M", n), ALU.subtract).then_inc(s_nM, 1)

                def weights_sum(n):
                    dve.wait_ge(s_exp, n.count())
                    V.tensor_scalar(at("has", n), at("L", n), 0.0, None, ALU.is_gt)
                    V.tensor_scalar(at("Lg", n), at("L", n), 1e-30, None, ALU.max).then_inc(s_L, 1)

                def weights_inv(n):
                    dve.wait_ge(s_L, n.count())
                    if n.exists(UN):
                        dve.wait_ge(s_st[n.slot // HG], n.dma_count(1))
                    V.reciprocal(at("inv", n), at("Lg", n)).then_inc(s_inv, 1)
                    V.scalar_tensor_tensor(o[:, n.slot, :], aq[:, n.slot, P:2 * P], at("has", n), aq[:, n.slot, 0:P],
                                           ALU.mult, ALU.add).then_inc(s_mix, 1)

                def finish(n):
                    dve.wait_ge(s_N, n.count())
                    dve.wait_ge(s_inv, n.count())
                    dve.wait_ge(s_mix, n.count())
                    V.scalar_tensor_tensor(pre[:, n.slot % 2, :], pN[:, 0:P], at("inv", n), o[:, n.slot, :],
                                           ALU.mult, ALU.add).then_inc(s_sum, 1)

                def finish_2(n):
                    dve.wait_ge(s_sum, n.count())
                    V.scalar_tensor_tensor(o[:, n.slot, :], pre[:, n.slot % 2, :], SLOPE, pre[:, n.slot % 2, :],
                                           ALU.mult, ALU.max).then_inc(s_out, 1)

                def body(n):
                    for step, ahead in ((maximum, -3), (mask, 1), (maximum_2, -3), (mask_rows, 1), (maximum_3, -3), (add_edges, 1),
                                        (weights_sum, -4), (finish, -7), (weights_inv, -4), (finish_2, -7)):
                        m = n + ahead
                        if m.exists():
                            step(m)

                with only_if(dve, flag, 1):
                    link = Chain(dve, s_w)
                    dve.wait_ge(s_wload, 7 * 16)
                    link(V.memset(w23[:, CB + 1:CQ], 0.0))
                    link(V.tensor_copy(iota_h[:, :], iota_n[0:LANES, :]))
                    link(V.tensor_tensor(w23[:, P:2 * P], w2[:, :], w23[:, 0:P], ALU.subtract))
                    link(V.memset(bias[:, :], 0.0))
                    link(V.tensor_copy(bias[:, 0:P], brow[:, 2, :]))
                    link(V.tensor_tensor(bias[:, P:2 * P], brow[:, 0, :], brow[:, 1, :], ALU.add))
                    link(V.tensor_tensor(bias[:, P:2 * P], bias[:, P:2 * P], brow[:, 2, :], ALU.subtract))
                    link(V.tensor_copy(part[:, 0, :], bias[:, :]))
                    link(V.tensor_tensor(left[:, 0, :], bias[:, :], part[:, 0, :], ALU.subtract))
                    link(V.tensor_copy(part[:, 1, :], left[:, 0, :]))
                    link(V.tensor_tensor(left[:, 1, :], left[:, 0, :], part[:, 1, :], ALU.subtract))
                    link(V.tensor_copy(part[:, 2, :], left[:, 1, :]))
                    for k in range(3):
                        link(V.tensor_scalar(own[:, k, :], part[:, k, :], ident[0:3, k:k + 1], None, ALU.mult))
                    link(V.tensor_tensor(own[:, 0, :], own[:, 0, :], own[:, 1, :], ALU.add))
                    link(V.tensor_tensor(parts[:, :], own[:, 0, :], own[:, 2, :], ALU.add))
                    dve.wait_ge(s_wT, 1)
                    V.tensor_copy(w1t[:, :], pT[0][:, 0:P]).then_inc(s_prep, 1)
                    fast_turns(dve, body, 1, 7)

            @block.scalar
            def _(act):
                A = nc.scalar
                at = lambda name, n: col[name][:, n.slot:n.slot + 1]

                def transposes_out(n):
                    act.wait_ge(s_T, n.count())
                    A.copy(hgT[:, n.slot % 4, :], pT[n.slot % 2][:, 0:P + W]).then_inc(s_evT, 1)

                def products_out(n):
                    act.wait_ge(s_A, n.count())
                    if n.exists(UN):
                        act.wait_ge(s_mix, n.count(1 - UN))
                    A.copy(aq[:, n.slot, :], pA[:, 0:AQ]).then_inc(s_evA, 1)

                def exponentials(n):
                    act.wait_ge(s_nM, n.count())
                    A.activation(w[:, n.slot % 2, :], pS[n.slot % 2][:, 0:W], ACT.Exp, bias=at("nM", n),
                                 accum_out=at("L", n)).then_inc(s_exp, 1)

                def weights_out(n):
                    act.wait_ge(s_Wt, n.count())
                    A.copy(wT[:, n.slot % 2, :, :], pW[0:LANES, 0:2 * P].rearrange("p (j n) -> p j n", j=2)).then_inc(s_evW, 1)

                def sums_out(n):
                    act.wait_ge(s_G, n.count())
                    if n.exists(2):
                        act.wait_ge(s_N, n.count(-1))
                    A.copy(sT[:, n.slot % 2, :], pG[:, 0:P]).then_inc(s_evG, 1)

                def body(n):
                    for step, back in ((transposes_out, 0), (products_out, 1), (exponentials, 3), (weights_out, 4), (sums_out, 5)):
                        if (n - back).exists():
                            step(n - back)

                with only_if(act, flag, 1):
                    fast_turns(act, body, 0, 5)

            @block.tensor
            def _(pe):
                T = nc.tensor

                def transposes(n):
                    k = n.slot
                    ends = isinstance(n.q, int) and n.number >= NB - NB % HG
                    pe.wait_ge(s_h[k // HG], n.dma_count(-1 if ends else 0))
                    pe.wait_ge(s_g, n.count())
                    if n.exists(2):
                        pe.wait_ge(s_evT, n.count(-1))
                    T.transpose(pT[k % 2][:, 0:P], hb[:, k, :], ident[:, :])
                    for j in range(2):
                        last = T.transpose(pT[k % 2][:, P + j * LANES:P + (j + 1) * LANES], g[:, k, j * P:(j + 1) * P], ident[0:LANES, 0:LANES])
                    last.then_inc(s_T, 1)

                def products(n):
                    k = n.slot
                    pe.wait_ge(s_evT, n.count())
                    if n.exists(1):
                        pe.wait_ge(s_evA, n.count(0))
                    T.matmul(pA[:, 0:CQ], hgT[:, k % 4, 0:P], w23[:, :], start=True, stop=False)
                    T.matmul(pA[:, 0:CQ], consts["onesb"][0:3, :], parts[:, :], start=False, stop=True)
                    T.matmul(pA[:, CQ:AQ], w1t[:, :], hgT[:, k % 4, 0:P], start=True, stop=True).then_inc(s_A, 1)

                def scores(n):
                    k = n.slot
                    pe.wait_ge(s_evA, n.count())
                    pe.wait_ge(s_pen, n.count())
                    if n.exists(2):
                        pe.wait_ge(s_exp, n.count(-1))
                    T.matmul(pS[k % 2][:, 0:W], aq[:, k, CQ:AQ], hgT[:, k % 4, P:P + W], start=True, stop=False)
                    for j in range(2):
                        last = T.matmul(pS[k % 2][:, j * LANES:(j + 1) * LANES], pen[:, k, j, :], identb[0:LANES, 0:LANES], start=False, stop=(j == 1))
                    last.then_inc(s_S, 1)

                def weights_T(n):
                    k = n.slot
                    pe.wait_ge(s_exp, n.count())
                    if n.exists(1):
                        pe.wait_ge(s_evW, n.count(0))
                    for j in range(2):
                        last = T.transpose(pW[0:LANES, j * P:(j + 1) * P], w[:, k % 2, j * LANES:(j + 1) * LANES], ident[:, :])
                    last.then_inc(s_Wt, 1)

                def weighted_sums(n):
                    k = n.slot
                    pe.wait_ge(s_evW, n.count())
                    if n.exists(1):
                        pe.wait_ge(s_evG, n.count(0))
                    for j in range(2):
                        last = T.matmul(pG[:, 0:P], g[:, k, j * P:(j + 1) * P], wT[:, k % 2, j, :], start=(j == 0), stop=(j == 1))
                    last.then_inc(s_G, 1)

                def through_w1(n):
                    pe.wait_ge(s_evG, n.count())
                    if n.exists(1):
                        pe.wait_ge(s_sum, n.count(0))
                    T.matmul(pN[:, 0:P], sT[:, n.slot % 2, :], w1[:, :], start=True, stop=True).then_inc(s_N, 1)

                def body(n):
                    for step, back in ((transposes, 0), (products, 1), (scores, 2), (weights_T, 4), (weighted_sums, 5), (through_w1, 6)):
                        if (n - back).exists():
                            step(n - back)

                with only_if(pe, flag, 1):
                    pe.wait_ge(s_wload, 7 * 16)
                    T.transpose(pT[0][:, 0:P], w1[:, :], ident[:, :]).then_inc(s_wT, 1)
                    pe.wait_ge(s_prep, 1)
                    fast_turns(pe, body, 0, 6)


def fast_support(nc, d, tab, consts):
    iota_n, block_row = consts["iota_n"], consts["block_row"]
    starts, flag = tab["starts"], tab["flag"]
    ctx = ExitStack()
    with ctx:
        sb = lambda name, shape, dt: ctx.enter_context(nc.sbuf_tensor(f"r_{name}", shape, dt))
        pb = lambda name, shape, dt: ctx.enter_context(nc.psum_tensor(f"r_{name}", shape, dt))
        phase_sem = ctx.enter_context(phase_semaphores(nc))
        sem = lambda name: phase_sem(f"r_{name}")
        ring = lambda name: [sem(f"{name}{k}") for k in range(UN)]
        rec = sb("rec", [LANES, UN, 2, 4], F32)
        idx = sb("idx", [LANES, UN, 2], I32)
        loc = sb("loc", [LANES, UN, 2], F32)
        xg = sb("xg", [LANES, UN, 2, XW], F32)
        wf = sb("wf", [LANES, UN, 2], F32)
        A = sb("A", [LANES, UN, 2, P], F32)
        sup = sb("sup", [P, UN, P], F32)
        pR = [pb(f"p{k}", [P, 512], F32) for k in range(UN)]
        s_rec, s_xga, s_xgb, s_st = (ring(n) for n in ("rec", "xga", "xgb", "st"))
        s_idx, s_loc, s_wf, s_A, s_R, s_sup = (sem(n) for n in ("idx", "loc", "wf", "A", "R", "sup"))
        with nc.Block() as block:
            @block.sync
            def _(sp):
                def body(n):
                    m = n + 6
                    if m.exists():
                        start = sp.value_load(starts[0:1, bass.ds(m.number, 1)], min_val=0, max_val=E - W)
                        if m.exists(UN):
                            sp.wait_ge(s_A, m.count(1 - UN))
                        sp.dma_start(rec[:, m.slot, :, :], d["src", "recs"][bass.ds(start, W), :].rearrange("(p j) t -> p j t", j=2)).then_inc(s_rec[m.slot], 16)
                    m = n - 1
                    if m.exists():
                        sp.wait_ge(s_sup, m.count())
                        sp.dma_start(d["sup"][bass.ds(m.number * P, P), :], sup[:, m.slot, :]).then_inc(s_st[m.slot], 16)

                with only_if(sp, flag, 1):
                    fast_turns(sp, body, 6, 1)
                    for k in range(UN):
                        sp.wait_ge(s_st[k], 16 * len(range(k, NB, UN)))

            @block.gpsimd
            def _(pool):
                def body(last_row, n):
                    m = n + 2
                    if not m.exists():
                        return
                    if m.exists(UN):
                        pool.wait_ge(s_R, m.count(1 - UN))
                    wait_apart(pool, s_idx, m.count())
                    for j, s in enumerate((s_xga, s_xgb)):
                        pool.indirect_dma_start(out=xg[:, m.slot, j, :], out_offset=None, in_=d["xtab"],
                                                in_offset=bass.IndirectOffsetOnAxis(ap=idx[:, m.slot, j:j + 1], axis=0),
                                                bounds_check=last_row, oob_is_err=False).then_inc(s[m.slot], 16)

                with only_if(pool, flag, 1):
                    last_row = pool.to_reg(N - 1)
                    fast_turns(pool, lambda n: body(last_row, n), 2, 0)

            @block.vector
            def _(dve):
                V = nc.vector

                def body(n):
                    m = n + 4
                    if m.exists():
                        k = m.slot
                        dve.wait_ge(s_rec[k], m.dma_count())
                        if m.exists(UN):
                            dve.wait_ge(s_xga[k], m.dma_count(1))
                            dve.wait_ge(s_xgb[k], m.dma_count(1))
                        V.tensor_copy(idx[:, k, :], rec[:, k, :, 1]).then_inc(s_idx, 1)
                        V.tensor_scalar(loc[:, k, :], rec[:, k, :, 0], block_row[0:LANES, bass.ds(m.number, 1)], None, ALU.subtract).then_inc(s_loc, 1)
                    if n.exists():
                        k = n.slot
                        dve.wait_ge(s_xga[k], n.dma_count())
                        dve.wait_ge(s_xgb[k], n.dma_count())
                        V.tensor_tensor(wf[:, k, :], rec[:, k, :, 2], xg[:, k, :, P], ALU.mult).then_inc(s_wf, 1)
                        dve.wait_ge(s_loc, n.count())
                        dve.wait_ge(s_wf, n.count())
                        if n.exists(UN):
                            dve.wait_ge(s_R, n.count(1 - UN))
                        for j in range(2):
                            last = V.tensor_scalar(A[:, k, j, :], iota_n[0:LANES, :], loc[:, k, j:j + 1], wf[:, k, j:j + 1], ALU.is_equal, ALU.mult)
                        last.then_inc(s_A, 1)

                with only_if(dve, flag, 1):
                    fast_turns(dve, body, 4, 0)

            @block.tensor
            def _(pe):
                def body(n):
                    if not n.exists():
                        return
                    k = n.slot
                    pe.wait_ge(s_A, n.count())
                    if n.exists(UN):
                        pe.wait_ge(s_sup, n.count(1 - UN))
                    for j in range(2):
                        last = nc.tensor.matmul(pR[k][:, 0:P], A[:, k, j, :], xg[:, k, j, 0:P], start=(j == 0), stop=(j == 1))
                    last.then_inc(s_R, 1)

                with only_if(pe, flag, 1):
                    fast_turns(pe, body, 0, 0)

            @block.scalar
            def _(act):
                def body(n):
                    if not n.exists():
                        return
                    k = n.slot
                    act.wait_ge(s_R, n.count())
                    if n.exists(UN):
                        act.wait_ge(s_st[k], n.dma_count(1))
                    nc.scalar.copy(sup[:, k, :], pR[k][:, 0:P]).then_inc(s_sup, 1)

                with only_if(act, flag, 1):
                    fast_turns(act, body, 0, 0)


def general_support(nc, d, tab, consts):
    keep, base, flag = tab["keep"], tab["base"], tab["flag"]
    iota_n = consts["iota_n"]
    recs, items, xtab = d["src", "recs"], d["src", "items"], d["xtab"]
    ctx = ExitStack()
    with ctx:
        sb = lambda name, shape, dt: ctx.enter_context(nc.sbuf_tensor(f"f_{name}", shape, dt))
        pb = lambda name, shape, dt: ctx.enter_context(nc.psum_tensor(f"f_{name}", shape, dt))
        phase_sem = ctx.enter_context(phase_semaphores(nc))
        sem = lambda name: phase_sem(f"f_{name}")
        rec, idx = sb("rec", [P, 4], F32), sb("idx", [P, 1], I32)
        xg = sb("xg", [P, XW], F32)
        wf, loc, A = sb("wf", [P, 1], F32), sb("loc", [P, 1], F32), sb("A", [P, P], F32)
        acc = sb("acc", [P, P], F32)
        pG = pb("pG", [P, 512], F32)
        s = {n: sem(n) for n in ("rec", "idx", "xg", "A", "G", "dve", "out", "st")}
        with nc.Block() as block:
            @block.sync
            def _(sp):
                with only_if(sp, flag, 0):
                    with sp.Fori(0, ITEMS) as i:
                        row = sp.value_load(items[bass.ds(i, 1), 0:1], min_val=0, max_val=NPAD - P)
                        erow = sp.value_load(items[bass.ds(i, 1), 1:2], min_val=0, max_val=EPAD - P)
                        sp.dma_start(rec[:, :], recs[bass.ds(erow, P), :]).then_inc(s["rec"], 16)
                        sp.wait_ge(s["out"], i + 1)
                        sp.dma_start(d["sup"][bass.ds(row, P), :], acc[:, :]).then_inc(s["st"], 16)
                        wait_apart(sp, s["st"], i * 16 + 16)

            @block.gpsimd
            def _(pool):
                with only_if(pool, flag, 0):
                    last_row = pool.to_reg(N - 1)
                    with pool.Fori(0, ITEMS) as i:
                        wait_apart(pool, s["idx"], i + 1)
                        pool.indirect_dma_start(out=xg[:, :], out_offset=None, in_=xtab,
                                                in_offset=bass.IndirectOffsetOnAxis(ap=idx[:, 0:1], axis=0),
                                                bounds_check=last_row, oob_is_err=False).then_inc(s["xg"], 16)

            @block.tensor
            def _(pe):
                with only_if(pe, flag, 0):
                    with pe.Fori(0, ITEMS) as i:
                        pe.wait_ge(s["A"], i + 1)
                        nc.tensor.matmul(pG[:, 0:P], A[:, :], xg[:, 0:P], start=True, stop=True).then_inc(s["G"], 1)

            @block.vector
            def _(dve):
                with only_if(dve, flag, 0):
                    nc.vector.memset(acc[:, :], 0.0).then_inc(s["dve"], 1)
                    dve.wait_ge(s["dve"], 1)
                    with dve.Fori(0, ITEMS) as i:
                        link = OffsetChain(dve, s["dve"], 2, i, 1)
                        here = lambda t: t[:, bass.ds(i, 1)]
                        dve.wait_ge(s["rec"], i * 16 + 16)
                        nc.vector.tensor_copy(idx[:, :], rec[:, 1:2]).then_inc(s["idx"], 1)
                        link(nc.vector.tensor_tensor(loc[:, :], rec[:, 0:1], here(base), ALU.subtract))
                        dve.wait_ge(s["xg"], i * 16 + 16)
                        link(nc.vector.tensor_tensor(wf[:, :], rec[:, 2:3], xg[:, P:P + 1], ALU.mult))
                        nc.vector.tensor_scalar(A[:, :], iota_n[:, :], loc[:, 0:1], wf[:, 0:1], ALU.is_equal, ALU.mult).then_inc(s["A"], 1)
                        dve.wait_ge(s["G"], i + 1)
                        if_first = nc.vector.scalar_tensor_tensor(acc[:, :], acc[:, :], here(keep), pG[:, 0:P], ALU.mult, ALU.add)
                        if_first.then_inc(s["out"], 1)
                        dve.wait_ge(s["st"], i * 16 + 16)
                        link.end()


def row_pass(nc, name, in_a, in_b, out, final):
    GR = 16
    groups = N // (P * GR)
    tail = N - groups * P * GR
    TG = 8
    TP = tail // TG
    assert TP * TG == tail and groups % 2 == 0
    ctx = ExitStack()
    with ctx:
        sb = lambda n, shape, dt: ctx.enter_context(nc.sbuf_tensor(f"{name}_{n}", shape, dt))
        phase_sem = ctx.enter_context(phase_semaphores(nc))
        sem = lambda n: phase_sem(f"{name}_{n}")
        WA = XW if final else P
        WO = P if final else XW
        a = [sb(f"a{k}", [P, GR, WA], F32) for k in range(2)]
        b = [sb(f"b{k}", [P, GR, P], F32) for k in range(2)]
        o = [sb(f"o{k}", [P, GR, WO], F32) for k in range(2)]
        sq = sb("sq", [P, GR, P], F32)
        st6 = sb("st6", [P, GR, 6], F32)
        mv = sb("mv", [P, GR, 2], F32)
        cols = sb("cols", [P, 16, GR], F32)
        nrm = [sb(f"nrm{k}", [P, 2, GR], F32) for k in range(2)]
        s_in = [[sem(f"in{t}{k}") for k in range(2)] for t in range(2)]
        s_st = [sem(f"st{k}") for k in range(2)]
        s_dve, s_sq, s_sqd, s_arg, s_fn, s_nrm, s_fac, s_out = (sem(n) for n in ("dve", "sq", "sqd", "arg", "fn", "nrm", "fac", "out"))

        def rows(t, m, p=P, g=GR):
            return t[bass.ds(m * (P * GR), p * g), :].rearrange("(p g) f -> p g f", g=g)

        def turns(eng, body):
            for k in range(2):
                body(k, k, P, GR)
            with eng.Fori(1, groups // 2) as q:
                for k in range(2):
                    body(q * 2 + k, k, P, GR)
            body(groups, 0, TP, TG)

        def per_group(m, n):
            return m * n + n

        def earlier(m):
            return not (isinstance(m, int) and m < 2)

        def slot_dma(m, k, back=0):
            return ((m - k) // 2 + (1 - back)) * 16 if isinstance(m, int) else (m - k) * 8 + (1 - back) * 16

        with nc.Block() as block:
            @block.sync
            def _(sp):
                def load(m, k, p, g):
                    if earlier(m):
                        sp.wait_ge(s_out, (m - 1) * 1)
                    sp.dma_start(a[k][0:p, 0:g, :], rows(in_a, m, p, g)).then_inc(s_in[0][k], 16)
                    sp.dma_start(b[k][0:p, 0:g, :], rows(in_b, m, p, g)).then_inc(s_in[1][k], 16)

                turns(sp, load)

            @block.gpsimd
            def _(pool):
                def store(m, k, p, g):
                    wait_apart(pool, s_out, per_group(m, 1))
                    if not final:
                        wait_apart(pool, s_fac, per_group(m, 1))
                    pool.dma_start(rows(out, m, p, g), o[k][0:p, 0:g, :]).then_inc(s_st[k], 16)

                turns(pool, store)
                pool.wait_ge(s_st[0], 16 * (groups // 2 + 1))
                pool.wait_ge(s_st[1], 16 * (groups // 2))

            @block.scalar
            def _(act):
                def body(m, k, p, g):
                    c = lambda i: cols[0:p, i, 0:g]
                    act.wait_ge(s_arg, per_group(m, 1))
                    if final:
                        nc.scalar.activation(c(8), c(7), ACT.Exp, scale=-2.0).then_inc(s_fn, 1)
                    act.wait_ge(s_nrm, per_group(m, 1))
                    if earlier(m):
                        act.wait_ge(s_st[k], slot_dma(m, k, 1))
                    for r in range(g):
                        last = nc.scalar.activation(o[k][0:p, r, 0:P], b[k][0:p, r, :], ACT.Identity,
                                                    bias=nrm[k][0:p, 1, r:r + 1], scale=nrm[k][0:p, 0, r:r + 1])
                    last.then_inc(s_out, 1)

                def body_first(m, k, p, g):
                    c = lambda i: cols[0:p, i, 0:g]
                    act.wait_ge(s_nrm, per_group(m, 1))
                    if earlier(m):
                        act.wait_ge(s_st[k], slot_dma(m, k, 1))
                    for r in range(g):
                        last = nc.scalar.activation(o[k][0:p, r, 0:P], b[k][0:p, r, :], ACT.Identity,
                                                    bias=nrm[k][0:p, 1, r:r + 1], scale=nrm[k][0:p, 0, r:r + 1])
                    last.then_inc(s_out, 1)
                    act.wait_ge(s_arg, per_group(m, 1))
                    nc.scalar.activation(c(8), c(7), ACT.Ln, bias=1.0, scale=1.0)
                    nc.scalar.activation(c(9), c(7), ACT.Ln, bias=1.0, scale=-1.0).then_inc(s_fn, 1)

                turns(act, body if final else body_first)

            @block.vector
            def _(dve):
                V = nc.vector

                def normalise(link, m, k, p, g):
                    c = lambda i: cols[0:p, i, 0:g]
                    for r in range(g):
                        last = V.bn_stats(st6[0:p, r, :], b[k][0:p, r, :])
                    link(last, alone=True)
                    for r in range(g):
                        last = V.bn_aggr(mv[0:p, r, :], st6[0:p, r, :])
                    link(last)
                    link(V.tensor_scalar(c(0), mv[0:p, 0:g, 1], EPS, None, ALU.add))
                    rsqrt_steps(nc, link, c(1), c(0), c(2), c(3))
                    if earlier(m):
                        dve.wait_ge(s_out, (m - 1) * 1)
                    V.tensor_copy(nrm[k][0:p, 0, 0:g], c(1))
                    V.scalar_tensor_tensor(nrm[k][0:p, 1, 0:g], mv[0:p, 0:g, 0], -1.0, c(1), ALU.mult, ALU.mult).then_inc(s_nrm, 1)

                def arrive(m, k):
                    dve.wait_ge(s_in[0][k], slot_dma(m, k))
                    dve.wait_ge(s_in[1][k], slot_dma(m, k))

                def first(m, k, p, g):
                    c = lambda i: cols[0:p, i, 0:g]
                    link = OffsetChain(dve, s_dve, FIRST_K, m, 0)
                    arrive(m, k)
                    link(V.tensor_tensor(b[k][0:p, 0:g, :], a[k][0:p, 0:g, :], b[k][0:p, 0:g, :], ALU.add))
                    normalise(link, m, k, p, g)
                    link(V.tensor_tensor(c(2), c(1), c(1), ALU.mult))
                    link(V.scalar_tensor_tensor(c(4), mv[0:p, 0:g, 1], float(P), c(2), ALU.mult, ALU.mult))
                    rsqrt_steps(nc, link, c(5), c(4), c(2), c(3))
                    link(V.tensor_tensor(c(6), c(4), c(5), ALU.mult))
                    link(V.tensor_scalar(c(6), c(6), 1e-15, None, ALU.max))
                    link(V.reciprocal(c(5), c(6)))
                    V.tensor_scalar(c(7), c(6), 1.0 - 1e-7, None, ALU.min).then_inc(s_arg, 1)
                    dve.wait_ge(s_arg, per_group(m, 1))
                    link(V.tensor_scalar(c(10), c(7), 0.25, None, ALU.min))
                    link(V.tensor_tensor(c(10), c(10), c(10), ALU.mult))
                    even_poly_steps(nc, link, c(11), c(10), ARTANH_C, c(2))
                    dve.wait_ge(s_fn, per_group(m, 1))
                    link(V.tensor_tensor(c(12), c(8), c(9), ALU.subtract))
                    link(V.scalar_tensor_tensor(c(12), c(12), 0.5, c(5), ALU.mult, ALU.mult))
                    link(V.tensor_tensor(c(11), c(11), c(12), ALU.subtract))
                    link(V.tensor_scalar(c(2), c(7), 0.25, None, ALU.is_lt))
                    link(V.tensor_tensor(c(11), c(11), c(2), ALU.mult))
                    if earlier(m):
                        dve.wait_ge(s_st[k], slot_dma(m, k, 1))
                    V.tensor_tensor(o[k][0:p, 0:g, P], c(11), c(12), ALU.add).then_inc(s_fac, 1)
                    link.end()

                def second(m, k, p, g):
                    c = lambda i: cols[0:p, i, 0:g]
                    link = OffsetChain(dve, s_dve, SECOND_K, m, 0)
                    arrive(m, k)
                    link(V.tensor_tensor(sq[0:p, 0:g, :], b[k][0:p, 0:g, :], b[k][0:p, 0:g, :], ALU.mult))
                    link(V.reduce_sum(c(4), sq[0:p, 0:g, :], AX.X))
                    rsqrt_steps(nc, link, c(5), c(4), c(2), c(3))
                    link(V.tensor_tensor(c(6), c(4), c(5), ALU.mult))
                    link(V.tensor_scalar(c(6), c(6), 1e-15, None, ALU.max))
                    V.tensor_copy(c(7), c(6)).then_inc(s_arg, 1)
                    link(V.reciprocal(c(5), c(6)))
                    link(V.tensor_scalar(c(10), c(6), 0.3, None, ALU.min))
                    link(V.tensor_tensor(c(10), c(10), c(10), ALU.mult))
                    even_poly_steps(nc, link, c(11), c(10), TANH_C, c(2))
                    dve.wait_ge(s_fn, per_group(m, 1))
                    link(V.tensor_scalar(c(12), c(8), 1.0, None, ALU.add))
                    link(V.reciprocal(c(13), c(12)))
                    link(V.tensor_scalar(c(12), c(8), -1.0, 1.0, ALU.mult, ALU.add))
                    link(V.tensor_tensor(c(12), c(12), c(13), ALU.mult))
                    link(V.tensor_tensor(c(12), c(12), c(5), ALU.mult))
                    link(V.tensor_tensor(c(11), c(11), c(12), ALU.subtract))
                    link(V.tensor_scalar(c(2), c(6), 0.3, None, ALU.is_lt))
                    link(V.tensor_tensor(c(11), c(11), c(2), ALU.mult))
                    link(V.tensor_tensor(c(11), c(11), c(12), ALU.add))
                    link(V.tensor_tensor(c(12), c(11), c(6), ALU.mult))
                    link(V.tensor_scalar(c(12), c(12), 1e-15, None, ALU.max))
                    link(V.tensor_scalar(c(2), c(12), 0.996, None, ALU.is_gt))
                    link(V.reciprocal(c(13), c(12)))
                    link(V.tensor_scalar(c(13), c(13), 0.996, -1.0, ALU.mult, ALU.add))
                    link(V.tensor_tensor(c(13), c(13), c(2), ALU.mult))
                    link(V.tensor_scalar(c(13), c(13), 1.0, None, ALU.add))
                    link(V.tensor_tensor(c(13), c(13), c(11), ALU.mult))
                    for r in range(g):
                        last = V.scalar_tensor_tensor(b[k][0:p, r, :], b[k][0:p, r, :], cols[0:p, 13, r:r + 1],
                                                      a[k][0:p, r, 0:P], ALU.mult, ALU.add)
                    link(last)
                    normalise(link, m, k, p, g)
                    link.end()

                if not final:
                    for k in range(2):
                        V.memset(o[k][:, :, P + 1:XW], 0.0)
                turns(dve, second if final else first)


_INS = ['x', 'src', 'dst', 'edge_attr_128', 'edge_weight'] + [f'L0_gnn_{p}{k}_l{l}' for l in (0, 1) for k in (1, 2, 3) for p in ('W', 'b')]


def kernel(**inputs):
    import numpy as _np
    import concourse.bacc as _bacc
    from concourse import mybir as _mybir
    from concourse.bass_utils import run_bass_kernel_spmd as _run

    nc = _bacc.Bacc("TRN2", target_bir_lowering=False, num_devices=1)
    arrays, args = {}, []
    for name in _INS:
        a = _np.ascontiguousarray(inputs[name])
        arrays[f"in_{name}_dram"] = a
        args.append(nc.dram_tensor(f"in_{name}_dram", a.shape, _mybir.dt.from_np(a.dtype), kind="ExternalInput").ap())
    args.append(nc.dram_tensor("out_0_dram", (N, P), F32, kind="ExternalOutput").ap())
    build(nc, *args)
    r = _run(nc, [arrays], core_ids=[0])
    return r.results[0]["out_0_dram"]
```

```python
import numpy as np
from contextlib import ExitStack, contextmanager
import concourse.bass as bass
from concourse import mybir

F32, F16, BF16, I32 = mybir.dt.float32, mybir.dt.float16, mybir.dt.bfloat16, mybir.dt.int32
ALU = mybir.AluOpType
ACT = mybir.ActivationFunctionType
AX = mybir.AxisListType

P = 128
N = 50000
E = 50000
NB = -(-N // P)
NPAD = NB * P
KC = 392
EPAD = P * KC
ITEMS = NB + NB - 1
IC = -(-ITEMS // P)
FILL_KEY = float(NPAD)
SLOPE = (1.0 / 8.0 + 1.0 / 3.0) / 2.0
EPS = 1e-5
MASKED = -1.0e30
M_NONE = -1.0e29
LANES = 96
W = 2 * LANES
SN = 256
SB = -(-N // SN)
SH = SN // P
SJ = 3
SW = SJ * P
HG = 4
UN = 8
HI, LO = 13, 32
HC = 28
XW = 132


def wait(eng, sem, value):
    eng.wait_ge(sem, value)


def wait_apart(eng, sem, value):
    eng.wait_ge(sem, value)
    eng.nop(nofuse=True)


@contextmanager
def phase_semaphores(nc):
    held = []

    def sem(name):
        held.append(nc.alloc_semaphore(name))
        return held[-1]
    yield sem
    nc.clear_and_free_semaphores(held)
    nc.all_engine_barrier()


@contextmanager
def only_if(eng, flag, wanted):
    value = eng.value_load(flag[0:1, 0:1], min_val=0, max_val=1)
    with eng.If(value == wanted):
        yield


class Chain:

    def __init__(self, eng, sem, per_turn=0, turn=None):
        self.eng, self.sem, self.per_turn, self.turn, self.n = eng, sem, per_turn, turn, 0

    def __call__(self, ins, alone=False):
        self.n += 1
        ins.then_inc(self.sem, 1)
        (wait_apart if alone else wait)(self.eng, self.sem, self.n if self.turn is None else self.turn * self.per_turn + self.n)

    def end(self):
        assert self.turn is None or self.n == self.per_turn, (self.n, self.per_turn)


def rsqrt_steps(nc, link, out, v, t1, t2):
    vi, oi = v.bitcast(I32), out.bitcast(I32)
    link(nc.vector.tensor_scalar(oi, vi, 1, None, ALU.arith_shift_right))
    link(nc.vector.tensor_scalar(oi, oi, -1, 0x5F3759DF, ALU.mult, ALU.add))
    for _ in range(3):
        link(nc.vector.scalar_tensor_tensor(t1, v, -0.5, out, ALU.mult, ALU.mult))
        link(nc.vector.tensor_tensor(t2, t1, out, ALU.mult))
        link(nc.vector.scalar_tensor_tensor(out, t2, 1.5, out, ALU.add, ALU.mult))


def even_poly_steps(nc, link, out, x2, coefficients):
    link(nc.vector.tensor_scalar(out, x2, coefficients[-1], None, ALU.mult))
    for c in coefficients[-2:0:-1]:
        link(nc.vector.scalar_tensor_tensor(out, out, c, x2, ALU.add, ALU.mult))
    link(nc.vector.tensor_scalar(out, out, coefficients[0], None, ALU.add))


ARTANH_C = [1.0 / (2 * k + 1) for k in range(6)]
TANH_C = [1.0, -1 / 3, 2 / 15, -17 / 315, 62 / 2835, -1382 / 155925]


def build(nc, x, src, dst, ea, ew, W1a, b1a, W2a, b2a, W3a, b3a, W1b, b1b, W2b, b2b, W3b, b3b, out):
    dram = lambda name, shape, dt: nc.dram_tensor(name, shape, dt, kind="Internal").ap()
    d = {
        "xpad": dram("xpad", [NPAD, P], F32), "h1": dram("h1", [NPAD, P], F32), "h2": dram("h2", [NPAD, P], F32),
        "xtab": dram("xtab", [N, XW], F32), "sup": dram("sup", [SB * SN, P], F32),
        "pairs": dram("pairs", [EPAD, 2], I32),
    }
    for kind in ("dst", "src"):
        d[kind, "recs"] = dram(f"{kind}_sorted", [EPAD, 4], F32)
        d[kind, "items"] = dram(f"{kind}_items", [P * IC, 2], I32)
    lay = [(W1a, b1a, W2a, b2a, W3a, b3a), (W1b, b1b, W2b, b2b, W3b, b3b)]

    ctx = ExitStack()
    with ctx:
        sb = lambda name, shape, dt: ctx.enter_context(nc.sbuf_tensor(name, shape, dt))
        sem = lambda name: ctx.enter_context(nc.semaphore(name))

        ident = sb("ident", [P, P], F32)
        identb = sb("identb", [P, P], BF16)
        iota_n = sb("iota_n", [P, P], F32)
        iota_b = sb("iota_b", [P, KC], F32)
        iota_16 = sb("iota_16", [P, KC], F16)
        iota_s = sb("iota_s", [P, SN], F32)
        block_row = sb("block_row", [P, KC], F32)
        below = sb("below", [P, P], BF16)
        notbelow = sb("notbelow", [P, P], BF16)
        onesb = sb("onesb", [P, P], BF16)
        onesf = sb("onesf", [P, P], F32)
        s_const = sem("s_const")
        s_const0 = sem("s_const0")
        with nc.Block() as block:
            @block.gpsimd
            def _(pool):
                pool.memset(ident[:, :], 0.0).then_inc(s_const0, 1)
                pool.memset(identb[:, :], 0.0).then_inc(s_const0, 1)
                pool.memset(onesb[:, :], 1.0).then_inc(s_const0, 1)
                pool.memset(onesf[:, :], 1.0).then_inc(s_const0, 1)
                pool.iota(iota_n[:, :], pattern=[[1, P]], base=0, channel_multiplier=0,
                          allow_small_or_imprecise_dtypes=True).then_inc(s_const, 1)
                pool.iota(iota_s[:, :], pattern=[[1, SN]], base=0, channel_multiplier=0,
                          allow_small_or_imprecise_dtypes=True).then_inc(s_const, 1)
                pool.iota(iota_b[:, :], pattern=[[1, KC]], base=0, channel_multiplier=0,
                          allow_small_or_imprecise_dtypes=True).then_inc(s_const, 1)
                pool.iota(iota_16[:, :], pattern=[[1, KC]], base=0, channel_multiplier=0,
                          allow_small_or_imprecise_dtypes=True).then_inc(s_const, 1)
                pool.iota(block_row[:, :], pattern=[[P, KC]], base=0, channel_multiplier=0,
                          allow_small_or_imprecise_dtypes=True).then_inc(s_const, 1)
                pool.wait_ge(s_const0, 4)
                for m in (ident, identb):
                    pool.affine_select(out=m[:, :], in_=m[:, :], compare_op=ALU.not_equal, fill=1.0,
                                       base=0, pattern=[[-1, P]], channel_multiplier=1).then_inc(s_const, 1)
                pool.affine_select(out=below[:, :], in_=onesb[:, :], compare_op=ALU.is_gt, fill=0.0,
                                   base=0, pattern=[[1, P]], channel_multiplier=-1).then_inc(s_const, 1)
                pool.affine_select(out=notbelow[:, :], in_=onesb[:, :], compare_op=ALU.is_ge, fill=0.0,
                                   base=0, pattern=[[-1, P]], channel_multiplier=1).then_inc(s_const, 1)
                pool.wait_ge(s_const, 9)

        consts = dict(iota_s=iota_s, iota_16=iota_16, ident=ident, identb=identb, iota_n=iota_n, iota_b=iota_b, block_row=block_row,
                      below=below, notbelow=notbelow, onesb=onesb, onesf=onesf)
        tables = {}
        tables["dst"] = counting_sort(nc, ctx, "dst", dst, src, ew, x, d, consts)
        for l, (hin, hwide, hout) in enumerate(((x, d["xpad"], d["h1"]), (d["h1"], d["h1"], d["h2"]))):
            layer(nc, l, hin, hwide, hout, ea, d, tables["dst"], lay[l], consts)
        tables["src"] = counting_sort(nc, ctx, "src", src, dst, ew, x, d, consts)
        general_support(nc, d, tables["src"], consts)
        general_map(nc, d["xtab"], d["sup"], out, tables["src"]["flag"])
        fast_support(nc, d, tables["src"], out, consts)


def counting_sort(nc, outer, kind, key_in, oth_in, ew, x, d, consts):
    is_dst = kind == "dst"
    bn, nb, window = (P, NB, W) if is_dst else (SN, SB, SW)
    nc_b = KC if is_dst else -(-(SB + 1) // 8) * 8
    shift = bn.bit_length() - 1
    ob = lambda name, shape, dt: outer.enter_context(nc.sbuf_tensor(f"{kind}_{name}", shape, dt))
    keep, base = ob("keep", [P, P * IC], F32), ob("base", [P, P * IC], F32)
    starts, flag = ob("starts", [P, KC], I32), ob("flag", [P, 1], I32)
    iota_b, below, notbelow, onesb, onesf, ident = (consts[n] for n in ("iota_b", "below", "notbelow", "onesb", "onesf", "ident"))
    ctx = ExitStack()
    with ctx:
        sb = lambda name, shape, dt: ctx.enter_context(nc.sbuf_tensor(f"{kind}_{name}", shape, dt))
        pb = lambda name, shape, dt: ctx.enter_context(nc.psum_tensor(f"{kind}_{name}", shape, dt))
        phase_sem = ctx.enter_context(phase_semaphores(nc))
        sem = lambda name: phase_sem(f"{kind}_{name}")
        ints = sb("ints", [P, 2, KC], I32)
        nxt = sb("nxt", [P, KC], I32)
        pairs = sb("pairs", [P, KC, 2], I32)
        dig_i = sb("dig_i", [P, KC], I32)
        hi = sb("hi", [P, KC], F32)
        lo = sb("lo", [P, KC], F32)
        blk = sb("blk", [P, KC + 4], F32)
        tmp = sb("tmp", [P, KC], F32)
        third = sb("third", [P, KC], F32)
        recs = sb("recs", [P, KC, 4], F32)
        ohi = sb("ohi", [P, 2, HC, HI], BF16)
        olo = sb("olo", [P, 2, HC, LO], BF16)
        hist = sb("hist", [HI, LO], F32)
        diag = sb("diag", [HI, HI, LO], F32)
        oh = sb("oh", [P, 4, KC], BF16)
        scr = sb("scr", [P, KC], F32)
        counts = sb("counts", [P, KC], F32)
        off = sb("off", [P, KC], F32)
        ones = sb("ones", [P, KC], F32)
        few = sb("few", [P, 4], F32)
        posf = sb("posf", [P, 4], F32)
        pos = sb("pos", [P, 4], I32)
        rec4 = sb("rec4", [P, 4, 4], F32)
        tile_i = sb("tile_i", [P, KC], I32)
        last_item = sb("last_item", [P, KC], F32)
        item_id = sb("item_id", [P, IC], F32)
        item_blk = sb("item_blk", [P, IC], F32)
        item_rows = sb("item_rows", [P, IC, 2], I32)
        item_f = sb("item_f", [P, IC, 2], F32)
        rows_bc = sb("rows_bc", [P, P * IC, 2], I32)
        zrow = sb("zrow", [NPAD - N, P], F32)
        bank = [pb(f"bank{i}", [P, 512], F32) for i in range(2)]
        hbank = pb("hbank", [P, 512], F32)
        s_load, s_fill, s_iota, s_dve = sem("load"), sem("fill"), sem("iota"), sem("dve")
        s_digit, s_hmm, s_hist, s_diag, s_total = sem("digit"), sem("hmm"), sem("hist"), sem("diag"), sem("total")
        s_items, s_itab, s_bc, s_pairs, s_pst = sem("items"), sem("itab"), sem("bc"), sem("pairs"), sem("pst")

        with nc.Block() as block:
            @block.gpsimd
            def _(pool):
                pool.memset(ints[:, 0, :], nb * bn).then_inc(s_fill, 1)
                pool.memset(ints[:, 1, :], 0).then_inc(s_fill, 1)
                pool.memset(nxt[:, :], NPAD).then_inc(s_fill, 1)
                if is_dst:
                    pool.iota(third[:, :], pattern=[[1, KC]], base=0, channel_multiplier=KC,
                              allow_small_or_imprecise_dtypes=True).then_inc(s_fill, 1)
                else:
                    pool.memset(third[:, :], 0.0).then_inc(s_fill, 1)
                pool.iota(item_id[:, :], pattern=[[1, IC]], base=0, channel_multiplier=IC,
                          allow_small_or_imprecise_dtypes=True).then_inc(s_iota, 1)

            @block.sync
            def _(sp):
                def load(tile, a, n):
                    left = n - (P - 1) * KC
                    sp.dma_start(tile[0:P // 2, :], a[0:P // 2 * KC].rearrange("(p c) -> p c", c=KC)).then_inc(s_load, 16)
                    sp.dma_start(tile[P // 2:P - 1, :], a[P // 2 * KC:(P - 1) * KC].rearrange("(p c) -> p c", c=KC)).then_inc(s_load, 16)
                    sp.dma_start(tile[P - 1:P, 0:left], a[(P - 1) * KC:n].rearrange("(p c) -> p c", c=left)).then_inc(s_load, 16)

                sp.wait_ge(s_fill, 4)
                load(ints[:, 0, :], key_in, E)
                load(ints[:, 1, :], oth_in, E)
                if is_dst:
                    load(nxt[:, :], key_in[1:E], E - 1)
                    sp.wait_ge(s_pairs, 1)
                    sp.dma_start(d["pairs"].rearrange("(p c) t -> p c t", c=KC), pairs[:, :, :]).then_inc(s_pst, 16)
                else:
                    load(third[:, :], ew, E)
                sp.wait_ge(s_items, 1)
                sp.dma_start(d[kind, "items"].rearrange("(p c) t -> p c t", c=IC), item_rows[:, :, :]).then_inc(s_itab, 16)
                sp.wait_ge(s_itab, 16)
                sp.dma_start(rows_bc[:, :, :],
                             d[kind, "items"].rearrange("(o c) t -> o c t", o=1).to_broadcast([P, P * IC, 2])).then_inc(s_bc, 16)
                sp.wait_ge(s_bc, 16)
                if is_dst:
                    sp.wait_ge(s_pst, 16)

            @block.tensor
            def _(pe):
                pe.wait_ge(s_digit, 1)
                nc.tensor.matmul(hbank[0:HI, 0:LO], ohi[:, 0, 0, :], olo[:, 0, 0, :], start=True, stop=True, skip_group_check=True).then_inc(s_hmm, 1)
                with pe.Fori(0, KC // HC // 2) as q:
                    for b in range(2):
                        pe.wait_ge(s_digit, q * 2 + (b + 2))
                        for c in range(HC):
                            last = nc.tensor.matmul(hbank[0:HI, 0:LO], ohi[:, b, c, :], olo[:, b, c, :], start=False, stop=True, skip_group_check=True)
                        last.then_inc(s_hmm, 1)
                pe.wait_ge(s_diag, 1)
                if is_dst:
                    nc.tensor.matmul(bank[1][:, 0:1], onesf[:, :], few[:, 0:1], start=True, stop=True)
                nc.tensor.matmul(bank[0][:, 0:HI * LO], onesf[0:HI, :], diag[:, :, :].rearrange("p a b -> p (a b)"), start=True, stop=True).then_inc(s_total, 1)

            @block.vector
            def _(dve):
                link = Chain(dve, s_dve)
                link(nc.vector.memset(ohi[:, :, :, :], 0.0))
                nc.vector.memset(olo[:, :, :, :], 0.0).then_inc(s_digit, 1)
                link(nc.vector.memset(blk[:, :], 0.0))
                link(nc.vector.memset(recs[:, :, :], 0.0))
                link(nc.vector.memset(ones[:, :], 1.0))
                dve.wait_ge(s_load, 9 * 16)
                link(nc.vector.tensor_scalar(dig_i[:, :], ints[:, 0, :], shift, None, ALU.arith_shift_right))
                link(nc.vector.tensor_copy(blk[:, 0:KC], dig_i[:, :]))
                link(nc.vector.tensor_scalar(dig_i[:, :], dig_i[:, :], 5, None, ALU.arith_shift_right))
                link(nc.vector.tensor_copy(hi[:, :], dig_i[:, :]))
                link(nc.vector.scalar_tensor_tensor(lo[:, :], hi[:, :], -float(LO), blk[:, 0:KC], ALU.mult, ALU.add))
                with dve.Fori(0, KC // HC // 2) as q:
                    for b in range(2):
                        dve.wait_ge(s_hmm, q * 2 + 1)
                        for oh_d, dig, n in ((ohi, hi, HI), (olo, lo, LO)):
                            last = nc.vector.tensor_tensor(
                                oh_d[:, b, :, :], dig[:, bass.ds((q * 2 + b) * HC, HC)].unsqueeze(2).to_broadcast([P, HC, n]),
                                iota_b[:, 0:n].unsqueeze(1).to_broadcast([P, HC, n]), ALU.is_equal)
                        last.then_inc(s_digit, 1)
                link(nc.vector.tensor_copy(recs[:, :, 0], ints[:, 0, :]))
                link(nc.vector.tensor_copy(recs[:, :, 1], ints[:, 1, :]))
                if is_dst:
                    link(nc.vector.tensor_scalar(tmp[:, :], third[:, :], float(E), None, ALU.is_lt))
                    link(nc.vector.tensor_tensor(recs[:, :, 2], third[:, :], tmp[:, :], ALU.mult))
                    link(nc.vector.tensor_copy(pairs[:, :, 0], ints[:, 0, :]))
                    nc.vector.tensor_copy(pairs[:, :, 1], ints[:, 1, :]).then_inc(s_pairs, 1)
                    link(nc.vector.tensor_tensor(tmp[:, :], nxt[:, :], ints[:, 0, :], ALU.is_lt))
                    link(nc.vector.reduce_sum(few[:, 0:1], tmp[:, :], AX.X))
                else:
                    link(nc.vector.tensor_copy(recs[:, :, 2], third[:, :]))
                dve.wait_ge(s_hmm, KC // HC + 1)
                link(nc.vector.tensor_copy(hist[:, :], hbank[0:HI, 0:LO]))
                nc.vector.tensor_tensor(diag[:, :, :], hist[:, :].unsqueeze(1).to_broadcast([HI, HI, LO]),
                                        ident[0:HI, 0:HI].unsqueeze(2).to_broadcast([HI, HI, LO]), ALU.mult).then_inc(s_diag, 1)
                dve.wait_ge(s_total, 1)
                link(nc.vector.tensor_copy(counts[:, :], bank[0][:, 0:KC]))
                link(nc.vector.reduce_max(few[:, 1:2], counts[:, 0:nb], AX.X))
                link(nc.vector.tensor_scalar(few[:, 2:3], few[:, 1:2], float(window), None, ALU.is_le))
                if is_dst:
                    link(nc.vector.tensor_scalar(few[:, 3:4], bank[1][:, 0:1], 0.0, None, ALU.is_equal))
                    link(nc.vector.tensor_tensor(few[:, 2:3], few[:, 2:3], few[:, 3:4], ALU.mult))
                link(nc.vector.tensor_copy(flag[:, :], few[:, 2:3]))
                link(nc.vector.tensor_tensor_scan(off[:, :], ones[:, :], counts[:, :], 0.0, ALU.mult, ALU.add))
                link(nc.vector.tensor_copy(tile_i[:, :], off[:, :]))
                link(nc.vector.tensor_scalar(tile_i[:, :], tile_i[:, :], 7, None, ALU.arith_shift_right))
                link(nc.vector.tensor_tensor(last_item[:, :], tile_i[:, :], iota_b[:, :], ALU.add))
                link(nc.vector.tensor_tensor(off[:, :], off[:, :], counts[:, :], ALU.subtract))
                link(nc.vector.tensor_scalar(starts[:, :], off[:, :], float(E - window), None, ALU.min))
                dve.wait_ge(s_iota, 1)
                for j in range(IC):
                    link(nc.vector.tensor_scalar(scr[:, 0:nb], last_item[:, 0:nb], item_id[:, j:j + 1], None,
                                                 ALU.is_lt, ALU.add, accum_out=item_blk[:, j:j + 1]))
                link(nc.vector.tensor_scalar(item_f[:, :, 0], item_blk[:, :], float(bn), None, ALU.mult))
                link(nc.vector.tensor_tensor(item_f[:, :, 1], item_id[:, :], item_blk[:, :], ALU.subtract))
                link(nc.vector.tensor_scalar(item_f[:, :, 1], item_f[:, :, 1], float(P), None, ALU.mult))
                nc.vector.tensor_copy(item_rows[:, :, :], item_f[:, :, :]).then_inc(s_items, 1)
                dve.wait_ge(s_bc, 16)
                link(nc.vector.tensor_copy(base[:, :], rows_bc[:, :, 0]))
                link(nc.vector.memset(keep[:, 0:1], 0.0))
                link(nc.vector.tensor_tensor(keep[:, 1:], base[:, 1:], base[:, :P * IC - 1], ALU.is_equal))

        held = dict(flag=flag, off=off, blk=blk, recs=recs, bank=bank, oh=oh, scr=scr, pos=pos, posf=posf, rec4=rec4, zrow=zrow)
        if is_dst:
            scatter_dst(nc, held, x, d, consts)
        else:
            scatter_src_and_rows(nc, held, nc_b, x, d, consts)
    return dict(keep=keep, base=base, starts=starts, flag=flag)


def scatter_dst(nc, t, x, d, consts):
    flag, off, blk, recs, bank, oh, scr, pos, posf, rec4, zrow = (
        t[n] for n in ("flag", "off", "blk", "recs", "bank", "oh", "scr", "pos", "posf", "rec4", "zrow"))
    iota_b, below, notbelow, onesb, onesf = (consts[n] for n in ("iota_b", "below", "notbelow", "onesb", "onesf"))
    with phase_semaphores(nc) as phase_sem:
        sem = lambda name: phase_sem(f"dst_{name}")
        s_oh, s_cnt, s_rank, s_pos, s_rec = (sem(n) for n in ("oh", "cnt", "rank", "pos", "rec"))
        s_sc = [sem(f"sc{i}") for i in range(4)]
        s_cp, s_z = sem("cp"), sem("z")
        with nc.Block() as block:
            def guarded(eng, program):
                with only_if(eng, flag, 0):
                    program()

            @block.gpsimd
            def _(pool):
                def program():
                    pool.memset(zrow[:, :], 0.0).then_inc(s_z, 1)
                    last_row = pool.to_reg(EPAD - 1)
                    with pool.Fori(0, KC // 4) as q:
                        for j in range(4):
                            pool.wait_ge(s_pos, q * 4 + (j + 1))
                            wait_apart(pool, s_rec, q * 4 + (j + 1))
                            pool.indirect_dma_start(
                                out=d["dst", "recs"], out_offset=bass.IndirectOffsetOnAxis(ap=pos[:, j:j + 1], axis=0),
                                in_=rec4[:, j, :], in_offset=None, bounds_check=last_row, oob_is_err=False,
                            ).then_inc(s_sc[j], 16)
                    for j in range(4):
                        pool.wait_ge(s_sc[j], 16 * KC // 4)
                guarded(pool, program)

            @block.sync
            def _(sp):
                def program():
                    sp.dma_start(d["xpad"][0:N, :], x).then_inc(s_cp, 16)
                    sp.wait_ge(s_z, 1)
                    sp.dma_start(d["xpad"][N:NPAD, :], zrow[:, :]).then_inc(s_cp, 16)
                    sp.wait_ge(s_cp, 32)
                guarded(sp, program)

            @block.vector
            def _(dve):
                def onehot(q, j):
                    nc.vector.tensor_scalar(oh[:, j % 4, 0:KC], consts["iota_16"][:, 0:KC], blk[:, bass.ds(q * 4 + j, 1)], None,
                                            ALU.is_equal).then_inc(s_oh, 1)

                def turn(q):
                    for j in range(4):
                        dve.wait_ge(s_cnt, q * 4 + (j + 1))
                        nc.vector.scalar_tensor_tensor(scr[:, 0:KC], iota_b[:, 0:KC], blk[:, bass.ds(q * 4 + j, 1)],
                                                       bank[j % 2][:, 0:KC], ALU.is_equal, ALU.mult,
                                                       accum_out=posf[:, j:j + 1]).then_inc(s_rank, 1)
                        onehot(q, j + 2)
                        if not (isinstance(q, int) and q == 0):
                            dve.wait_ge(s_sc[j], q * 16)
                        dve.wait_ge(s_rank, q * 4 + (j + 3))
                        nc.vector.tensor_copy(pos[:, j:j + 1], posf[:, j:j + 1]).then_inc(s_pos, 1)
                        nc.vector.tensor_copy(rec4[:, j, :], recs[:, bass.ds(q * 4 + j, 1), :].rearrange("p a b -> p (a b)")).then_inc(s_rec, 1)

                def program():
                    nc.vector.memset(oh[:, :, :], 0.0).then_inc(s_rank, 2)
                    dve.wait_ge(s_rank, 2)
                    onehot(0, 0)
                    onehot(0, 1)
                    turn(0)
                    with dve.Fori(1, KC // 4) as q:
                        turn(q)
                guarded(dve, program)

            @block.tensor
            def _(pe):
                mm = lambda c, w, j, **k: nc.tensor.matmul(bank[c][:, 0:KC], w[:, :], oh[:, j, 0:KC], skip_group_check=True, **k)

                def program():
                    for c in range(2):
                        nc.tensor.matmul(bank[c][:, 0:KC], onesf[0:1, :], off[0:1, 0:KC], start=True, stop=True, skip_group_check=True)
                    with pe.Fori(0, KC // 4) as q:
                        for j in range(4):
                            pe.wait_ge(s_oh, q * 4 + (j + 1))
                            pe.wait_ge(s_rank, q * 4 + (j + 1))
                            mm(j % 2, notbelow, (j - 2) % 4, start=False, stop=True)
                            mm(j % 2, onesb, (j - 1) % 4, start=False, stop=True)
                            mm(j % 2, below, j, start=False, stop=True).then_inc(s_cnt, 1)
                guarded(pe, program)


def scatter_src_and_rows(nc, t, nc_b, x, d, consts):
    GR = 32
    RING = 2 * GR
    SLOTS = 8
    TP, TG = 106, 8
    assert (KC - KC % GR) * P + TP * TG == N
    off, blk, recs, bank, oh, scr = (t[n] for n in ("off", "blk", "recs", "bank", "oh", "scr"))
    iota_b, below, notbelow, onesb, onesf = (consts[n] for n in ("iota_b", "below", "notbelow", "onesb", "onesf"))
    ctx = ExitStack()
    with ctx:
        sb = lambda name, shape, dt: ctx.enter_context(nc.sbuf_tensor(f"p_{name}", shape, dt))
        phase_sem = ctx.enter_context(phase_semaphores(nc))
        sem = lambda name: phase_sem(f"p_{name}")
        posf = sb("posf", [P, SLOTS], F32)
        pos = sb("pos", [P, SLOTS], I32)
        rec4 = sb("rec4", [P, SLOTS, 4], F32)
        a = sb("a", [P, 2, GR, XW], F32)
        b = sb("b", [P, 2, GR, P], F32)
        st6 = sb("st6", [P, GR, 6], F32)
        mv = sb("mv", [P, 2, GR, 2], F32)
        cols = sb("cols", [P, 2, 13, GR], F32)
        nrm = sb("nrm", [P, 2, 2, GR], F32)
        s_oh, s_cnt, s_rank, s_pos, s_rec = (sem(n) for n in ("oh", "cnt", "rank", "pos", "rec"))
        s_sc = [sem(f"sc{i}") for i in range(SLOTS)]
        s_ina, s_inb, s_st = ([sem(f"{n}{k}") for k in range(2)] for n in ("ina", "inb", "st"))
        s_dve, s_arg, s_fn, s_nrm, s_fac, s_out = (sem(n) for n in ("dve", "arg", "fn", "nrm", "fac", "out"))

        def turns(eng, body, ahead, behind):
            fast_turns(eng, body, ahead, behind, RING, KC, 1)

        def group_at(n, distance):
            first = n - distance
            return first if first.slot % GR == 0 and first.exists() else None

        def shape(first):
            return (TP, TG) if isinstance(first.q, int) and first.number == KC - KC % GR else (P, GR)

        def rows(table, first):
            p, g = shape(first)
            return table[bass.ds(first.number * P, p * g), :].rearrange("(p g) f -> p g f", g=g)

        with nc.Block() as block:
            @block.gpsimd
            def _(pool):
                last_row = pool.to_reg(EPAD - 1)
                with pool.Fori(0, KC // SLOTS) as q:
                    for j in range(SLOTS):
                        pool.wait_ge(s_pos, q * SLOTS + (j + 1))
                        wait_apart(pool, s_rec, q * SLOTS + (j + 1))
                        pool.indirect_dma_start(
                            out=d["src", "recs"], out_offset=bass.IndirectOffsetOnAxis(ap=pos[:, j:j + 1], axis=0),
                            in_=rec4[:, j, :], in_offset=None, bounds_check=last_row, oob_is_err=False,
                        ).then_inc(s_sc[j], 16)
                for j in range(SLOTS):
                    pool.wait_ge(s_sc[j], 16 * (KC // SLOTS))

            @block.sync
            def _(sp):
                def load(first):
                    p, g = shape(first)
                    par = first.slot // GR
                    if first.exists(RING):
                        sp.wait_ge(s_st[par], first.dma_count(1))
                    sp.dma_start(a[0:p, par, 0:g, 0:P], rows(x, first)).then_inc(s_ina[par], 16)
                    sp.dma_start(b[0:p, par, 0:g, :], rows(d["h2"], first)).then_inc(s_inb[par], 16)

                def store(first):
                    p, g = shape(first)
                    par = first.slot // GR
                    sp.wait_ge(s_out, first.group_count(GR))
                    sp.wait_ge(s_fac, first.group_count(GR))
                    sp.dma_start(rows(d["xtab"], first), a[0:p, par, 0:g, :]).then_inc(s_st[par], 16)

                def body(n):
                    for step, distance in ((load, 4 - GR), (store, GR - 1)):
                        first = group_at(n, distance)
                        if first:
                            step(first)

                turns(sp, body, GR - 4, GR - KC % GR)
                for k in range(2):
                    sp.wait_ge(s_st[k], 16 * len(range(k, -(-KC // GR), 2)))

            @block.vector
            def _(dve):
                V = nc.vector

                def onehot(n):
                    V.tensor_scalar(oh[:, n.slot % 4, 0:nc_b], consts["iota_16"][:, 0:nc_b], blk[:, bass.ds(n.number, 1)], None,
                                    ALU.is_equal).then_inc(s_oh, 1)

                def rank(n):
                    dve.wait_ge(s_cnt, n.count())
                    j = n.slot % SLOTS
                    V.scalar_tensor_tensor(scr[:, 0:nc_b], iota_b[:, 0:nc_b], blk[:, bass.ds(n.number, 1)],
                                           bank[n.slot % 2][:, 0:nc_b], ALU.is_equal, ALU.mult,
                                           accum_out=posf[:, j:j + 1]).then_inc(s_rank, 1)

                def position(n):
                    j = n.slot % SLOTS
                    if n.exists(SLOTS):
                        dve.wait_ge(s_sc[j], n.dma_count(1, slots=SLOTS))
                    dve.wait_ge(s_rank, n.count(3))
                    V.tensor_copy(pos[:, j:j + 1], posf[:, j:j + 1]).then_inc(s_pos, 1)
                    V.tensor_copy(rec4[:, j, :], recs[:, bass.ds(n.number, 1), :].rearrange("p a b -> p (a b)")).then_inc(s_rec, 1)


                def part(first, i, parts):
                    g = shape(first)[1]
                    return i * g // parts, (i + 1) * g // parts

                def add(link, c, first, i):
                    p, par = shape(first)[0], first.slot // GR
                    if i == 0:
                        dve.wait_ge(s_ina[par], first.dma_count())
                        dve.wait_ge(s_inb[par], first.dma_count())
                    lo, hi = part(first, i, 4)
                    last = V.tensor_tensor(b[0:p, par, lo:hi, :], a[0:p, par, lo:hi, 0:P], b[0:p, par, lo:hi, :], ALU.add)
                    if i == 3:
                        link(last)

                def statistics(link, c, first, i):
                    p, par = shape(first)[0], first.slot // GR
                    for r in range(*part(first, i, 8)):
                        last = V.bn_stats(st6[0:p, r, :], b[0:p, par, r, :])
                    if i == 7:
                        link(last, alone=True)

                def mean(link, c, first, i):
                    p, par = shape(first)[0], first.slot // GR
                    for r in range(*part(first, i, 4)):
                        last = V.bn_aggr(mv[0:p, par, r, :], st6[0:p, r, :])
                    if i == 3:
                        link(last)

                def deviation(link, c, first, i):
                    p, g = shape(first)
                    link(V.tensor_scalar(c(0), mv[0:p, first.slot // GR, 0:g, 1], EPS, None, ALU.add))
                    rsqrt_steps(nc, link, c(1), c(0), c(2), c(3))

                def scales(link, c, first, i):
                    p, g = shape(first)
                    par = first.slot // GR
                    V.tensor_copy(nrm[0:p, par, 0, 0:g], c(1))
                    V.scalar_tensor_tensor(nrm[0:p, par, 1, 0:g], mv[0:p, par, 0:g, 0], -1.0, c(1), ALU.mult, ALU.mult).then_inc(s_nrm, 1)
                    link(V.tensor_tensor(c(2), c(1), c(1), ALU.mult))
                    link(V.scalar_tensor_tensor(c(4), mv[0:p, par, 0:g, 1], float(P), c(2), ALU.mult, ALU.mult))

                def norm(link, c, first, i):
                    rsqrt_steps(nc, link, c(5), c(4), c(2), c(3))

                def norm_inverse(link, c, first, i):
                    link(V.tensor_tensor(c(6), c(4), c(5), ALU.mult))
                    link(V.tensor_scalar(c(6), c(6), 1e-15, None, ALU.max))
                    link(V.tensor_scalar(c(7), c(6), 1.0 - 1e-7, None, ALU.min))
                    link(V.reciprocal(c(5), c(6)))
                    V.tensor_copy(c(6), c(7)).then_inc(s_arg, 1)

                def series(link, c, first, i):
                    link(V.tensor_scalar(c(10), c(4), 0.25 ** 2, None, ALU.min))
                    even_poly_steps(nc, link, c(11), c(10), ARTANH_C)

                def factor(link, c, first, i):
                    p, g = shape(first)
                    dve.wait_ge(s_fn, first.group_count(GR))
                    link(V.tensor_tensor(c(12), c(8), c(9), ALU.subtract))
                    link(V.scalar_tensor_tensor(c(12), c(12), 0.5, c(5), ALU.mult, ALU.mult))
                    link(V.tensor_tensor(c(11), c(11), c(12), ALU.subtract))
                    link(V.scalar_tensor_tensor(c(11), c(7), 0.25, c(11), ALU.is_lt, ALU.mult))
                    V.tensor_tensor(a[0:p, first.slot // GR, 0:g, P], c(11), c(12), ALU.add).then_inc(s_fac, 1)

                stages = ([(add, i, i, i // 3) for i in range(4)] + [(statistics, i, 4 + i, i // 7) for i in range(8)]
                          + [(mean, i, 12 + i, i // 3) for i in range(4)]
                          + [(deviation, 0, 16, 1 + RSQRT_K), (scales, 0, 18, 2), (norm, 0, 19, RSQRT_K), (norm_inverse, 0, 21, 4),
                             (series, 0, 22, 1 + POLY_K), (factor, 0, 28, 4)])
                per_group = sum(links for _, _, _, links in stages)

                def body(n):
                    if n.exists():
                        rank(n)
                        onehot(n + 2)
                    before = 0
                    for stage, i, after, links in stages:
                        first = group_at(n, after)
                        if first:
                            p, g = shape(first)
                            link = OffsetChain(dve, s_dve, per_group, first.group_count(GR, 0), before)
                            stage(link, lambda j: cols[0:p, first.slot // GR, j, 0:g], first, i)
                            assert link.n == links, (stage, link.n)
                        before += links
                    if n.exists():
                        position(n)

                V.memset(a[:, :, :, P + 1:XW], 0.0)
                V.memset(oh[:, :, :], 0.0).then_inc(s_rank, 2)
                dve.wait_ge(s_rank, 2)
                onehot(Block_(0, 0, RING, KC))
                onehot(Block_(0, 1, RING, KC))
                turns(dve, body, 0, GR - KC % GR)

            @block.tensor
            def _(pe):
                mm = lambda c, w, j, **k: nc.tensor.matmul(bank[c][:, 0:nc_b], w[:, :], oh[:, j, 0:nc_b], skip_group_check=True, **k)
                for c in range(2):
                    nc.tensor.matmul(bank[c][:, 0:nc_b], onesf[0:1, :], off[0:1, 0:nc_b], start=True, stop=True, skip_group_check=True)
                with pe.Fori(0, KC // 4) as q:
                    for j in range(4):
                        pe.wait_ge(s_oh, q * 4 + (j + 1))
                        pe.wait_ge(s_rank, q * 4 + (j + 1))
                        mm(j % 2, notbelow, (j - 2) % 4, start=False, stop=True)
                        mm(j % 2, onesb, (j - 1) % 4, start=False, stop=True)
                        mm(j % 2, below, j, start=False, stop=True).then_inc(s_cnt, 1)

            @block.scalar
            def _(act):
                A = nc.scalar

                def logarithms(first, i):
                    p, g = shape(first)
                    c = lambda j: cols[0:p, first.slot // GR, j, 0:g]
                    act.wait_ge(s_arg, first.group_count(GR))
                    A.activation(c(8), c(6), ACT.Ln, bias=1.0, scale=1.0)
                    A.activation(c(9), c(6), ACT.Ln, bias=1.0, scale=-1.0).then_inc(s_fn, 1)

                def apply(first, i):
                    p, g = shape(first)
                    par = first.slot // GR
                    if i == 0:
                        act.wait_ge(s_nrm, first.group_count(GR))
                    for r in range(i * g // 8, (i + 1) * g // 8):
                        last = A.activation(a[0:p, par, r, 0:P], b[0:p, par, r, :], ACT.Identity,
                                            bias=nrm[0:p, par, 1, r:r + 1], scale=nrm[0:p, par, 0, r:r + 1])
                    if i == 7:
                        last.then_inc(s_out, 1)

                steps = [(apply, i, 19 + i) for i in range(5)] + [(logarithms, 0, 24)] + [(apply, i, 19 + i) for i in range(5, 8)]

                def body(n):
                    for step, i, after in steps:
                        first = group_at(n, after)
                        if first:
                            step(first, i)

                turns(act, body, 0, GR - KC % GR)


def layer(nc, l, hin, hwide, hout, ea, d, tab, weights, consts):
    general_layer(nc, l, hwide, hout, ea, d, tab, weights, consts)
    fast_layer(nc, l, hin, hout, ea, d, tab, weights, consts)


def general_layer(nc, l, hin, hout, ea, d, tab, weights, consts):
    keep, base, flag = tab["keep"], tab["base"], tab["flag"]
    recs, items = d["dst", "recs"], d["dst", "items"]
    ident, identb, iota_n = consts["ident"], consts["identb"], consts["iota_n"]
    W1, b1, W2, b2, W3, b3 = weights
    ctx = ExitStack()
    with ctx:
        sb = lambda name, shape, dt: ctx.enter_context(nc.sbuf_tensor(f"l{l}_{name}", shape, dt))
        pb = lambda name, shape, dt: ctx.enter_context(nc.psum_tensor(f"l{l}_{name}", shape, dt))
        phase_sem = ctx.enter_context(phase_semaphores(nc))
        sem = lambda name: phase_sem(f"l{l}_{name}")
        w1 = sb("w1", [P, P], F32)
        w1t = sb("w1t", [P, P], F32)
        w23 = sb("w23", [P, 2, P], F32)
        w2 = sb("w2", [P, P], F32)
        b1col = sb("b1col", [P, 1], F32)
        b1bc = sb("b1bc", [P, P], F32)
        brow = sb("brow", [P, 3, P], F32)
        b23 = sb("b23", [P, 2, P], F32)
        rec = sb("rec", [P, 4], F32)
        idx = sb("idx", [P, 2], I32)
        hb = sb("hb", [P, P], F32)
        hs = sb("hs", [P, P], F32)
        ev = sb("ev", [P, P], F32)
        g = sb("g", [P, P], F32)
        loc = sb("loc", [P, 1], F32)
        pen = sb("pen", [P, P], BF16)
        hT = sb("hT", [P, P], F32)
        qT = sb("qT", [P, P], F32)
        gT = sb("gT", [P, P], F32)
        w = sb("w", [P, P], F32)
        wT = sb("wT", [P, P], F32)
        acc = sb("acc", [P, P], F32)
        accn = sb("accn", [P, P], F32)
        accT = sb("accT", [P, P], F32)
        A = sb("A", [P, 2, P], F32)
        pre = sb("pre", [P, P], F32)
        o = sb("o", [P, P], F32)
        st = sb("st", [P, 16], F32)
        col = {n: st[:, k:k + 1] for k, n in enumerate(
            ("M", "L", "Mold", "mx", "Mn", "nMn", "alpha", "Lnew", "ka", "inv", "has", "t"))}
        pT, pQ, pA, pS, pW, pG, pN, pT2 = [pb(f"p{k}", [P, 512], F32) for k in range(8)]
        names = ("wload", "wdve", "wT", "prep", "rec", "h", "idx", "hs", "ev", "g", "pen", "hT", "hTs", "q", "qs",
                 "a", "gT", "gTs", "s", "m", "al", "w", "wTp", "wTs", "G", "accn", "aT", "aTs", "N", "out", "st", "dve")
        s = {n: sem(n) for n in names}
        K = 14

        with nc.Block() as block:
            @block.sync
            def _(sp):
                with only_if(sp, flag, 0):
                    sp.dma_start(w1[:, :], W1).then_inc(s["wload"], 16)
                    sp.dma_start(w2[:, :], W2).then_inc(s["wload"], 16)
                    sp.dma_start(w23[:, 0, :], W3).then_inc(s["wload"], 16)
                    for n, b in enumerate((b1, b2, b3)):
                        sp.dma_start(brow[:, n, :], b.rearrange("(o n) -> o n", o=1).to_broadcast([P, P])).then_inc(s["wload"], 16)
                    sp.dma_start(b1col[:, :], b1.rearrange("(n o) -> n o", o=1)).then_inc(s["wload"], 16)
                    with sp.Fori(0, ITEMS) as i:
                        row = sp.value_load(items[bass.ds(i, 1), 0:1], min_val=0, max_val=NPAD - P)
                        erow = sp.value_load(items[bass.ds(i, 1), 1:2], min_val=0, max_val=EPAD - P)
                        sp.dma_start(rec[:, :], recs[bass.ds(erow, P), :]).then_inc(s["rec"], 16)
                        sp.dma_start(hb[:, :], hin[bass.ds(row, P), :]).then_inc(s["h"], 16)
                        sp.wait_ge(s["out"], i + 1)
                        sp.dma_start(hout[bass.ds(row, P), :], o[:, :]).then_inc(s["st"], 16)
                        wait_apart(sp, s["st"], i * 16 + 16)

            @block.gpsimd
            def _(pool):
                with only_if(pool, flag, 0):
                    last_row = pool.to_reg(N - 1)
                    with pool.Fori(0, ITEMS) as i:
                        wait_apart(pool, s["idx"], i + 1)
                        pool.indirect_dma_start(out=hs[:, :], out_offset=None, in_=hin,
                                                in_offset=bass.IndirectOffsetOnAxis(ap=idx[:, 0:1], axis=0),
                                                bounds_check=last_row, oob_is_err=False).then_inc(s["hs"], 16)
                        pool.indirect_dma_start(out=ev[:, :], out_offset=None, in_=ea,
                                                in_offset=bass.IndirectOffsetOnAxis(ap=idx[:, 1:2], axis=0),
                                                bounds_check=last_row, oob_is_err=False).then_inc(s["ev"], 16)

            @block.vector
            def _(dve):
                with only_if(dve, flag, 0):
                    dve.wait_ge(s["wload"], 7 * 16)
                    link = Chain(dve, s["wdve"])
                    link(nc.vector.tensor_tensor(w23[:, 1, :], w2[:, :], w23[:, 0, :], ALU.subtract))
                    link(nc.vector.tensor_copy(b23[:, 0, :], brow[:, 2, :]))
                    link(nc.vector.tensor_tensor(b23[:, 1, :], brow[:, 0, :], brow[:, 1, :], ALU.add))
                    link(nc.vector.tensor_tensor(b23[:, 1, :], b23[:, 1, :], brow[:, 2, :], ALU.subtract))
                    link(nc.vector.memset(b1bc[:, :], 0.0))
                    link(nc.vector.tensor_scalar(b1bc[:, :], b1bc[:, :], b1col[:, 0:1], None, ALU.add))
                    link(nc.vector.memset(st[:, :], 0.0))
                    link(nc.vector.memset(acc[:, :], 0.0))
                    dve.wait_ge(s["wT"], 1)
                    nc.vector.tensor_copy(w1t[:, :], pT[:, 0:P]).then_inc(s["prep"], 1)
                    dve.wait_ge(s["prep"], 1)
                    with dve.Fori(0, ITEMS) as i:
                        link = Chain(dve, s["dve"], K, i)
                        here = lambda t: t[:, bass.ds(i, 1)]
                        dve.wait_ge(s["rec"], i * 16 + 16)
                        nc.vector.tensor_copy(idx[:, :], rec[:, 1:3]).then_inc(s["idx"], 1)
                        link(nc.vector.tensor_tensor(loc[:, :], rec[:, 0:1], here(base), ALU.subtract))
                        nc.vector.tensor_scalar(pen[:, :], iota_n[:, :], loc[:, 0:1], MASKED, ALU.not_equal, ALU.mult).then_inc(s["pen"], 1)
                        dve.wait_ge(s["hs"], i * 16 + 16)
                        dve.wait_ge(s["ev"], i * 16 + 16)
                        nc.vector.tensor_tensor(g[:, :], hs[:, :], ev[:, :], ALU.add).then_inc(s["g"], 1)
                        link(nc.vector.tensor_tensor(col["Mold"], col["M"], here(keep), ALU.mult))
                        link(nc.vector.tensor_scalar(col["t"], here(keep), -1.0, -M_NONE, ALU.add, ALU.mult))
                        link(nc.vector.tensor_tensor(col["Mold"], col["Mold"], col["t"], ALU.add))
                        dve.wait_ge(s["s"], i + 1)
                        link(nc.vector.reduce_max(col["mx"], pS[:, 0:P], AX.X))
                        link(nc.vector.tensor_tensor(col["Mn"], col["mx"], col["Mold"], ALU.max))
                        nc.vector.tensor_scalar(col["nMn"], col["Mn"], -1.0, None, ALU.mult).then_inc(s["m"], 1)
                        dve.wait_ge(s["al"], i + 1)
                        link(nc.vector.tensor_tensor(col["ka"], col["alpha"], here(keep), ALU.mult))
                        dve.wait_ge(s["w"], i + 1)
                        link(nc.vector.scalar_tensor_tensor(col["L"], col["L"], col["ka"], col["Lnew"], ALU.mult, ALU.add))
                        link(nc.vector.tensor_copy(col["M"], col["Mn"]))
                        dve.wait_ge(s["G"], i + 1)
                        link(nc.vector.scalar_tensor_tensor(acc[:, :], acc[:, :], col["ka"], pG[:, 0:P], ALU.mult, ALU.add))
                        link(nc.vector.tensor_scalar(col["t"], col["L"], 1e-30, None, ALU.max))
                        link(nc.vector.reciprocal(col["inv"], col["t"]))
                        link(nc.vector.tensor_scalar(col["has"], col["L"], 0.0, None, ALU.is_gt))
                        nc.vector.tensor_scalar(accn[:, :], acc[:, :], col["inv"], None, ALU.mult).then_inc(s["accn"], 1)
                        dve.wait_ge(s["a"], i + 1)
                        link(nc.vector.tensor_tensor(A[:, :, :], pA[:, 0:2 * P].rearrange("p (a b) -> p a b", a=2), b23[:, :, :], ALU.add))
                        dve.wait_ge(s["accn"], i + 1)
                        nc.vector.scalar_tensor_tensor(pre[:, :], A[:, 1, :], col["has"], A[:, 0, :], ALU.mult, ALU.add).then_inc(s["wdve"], 1)
                        dve.wait_ge(s["wdve"], i * 2 + 8 + 1)
                        dve.wait_ge(s["N"], i + 1)
                        nc.vector.tensor_tensor(accn[:, :], pre[:, :], pN[:, 0:P], ALU.add).then_inc(s["wdve"], 1)
                        dve.wait_ge(s["wdve"], i * 2 + 8 + 2)
                        nc.vector.scalar_tensor_tensor(o[:, :], accn[:, :], SLOPE, accn[:, :], ALU.mult, ALU.max).then_inc(s["out"], 1)
                        link.end()

            @block.scalar
            def _(act):
                with only_if(act, flag, 0):
                    with act.Fori(0, ITEMS) as i:
                        act.wait_ge(s["hT"], i + 1)
                        nc.scalar.copy(hT[:, :], pT[:, 0:P]).then_inc(s["hTs"], 1)
                        act.wait_ge(s["q"], i + 1)
                        nc.scalar.copy(qT[:, :], pQ[:, 0:P]).then_inc(s["qs"], 1)
                        act.wait_ge(s["gT"], i + 1)
                        nc.scalar.copy(gT[:, :], pT2[:, 0:P]).then_inc(s["gTs"], 1)
                        act.wait_ge(s["m"], i + 1)
                        nc.scalar.activation(col["alpha"], col["Mold"], ACT.Exp, bias=col["nMn"]).then_inc(s["al"], 1)
                        nc.scalar.activation(w[:, :], pS[:, 0:P], ACT.Exp, bias=col["nMn"], accum_out=col["Lnew"]).then_inc(s["w"], 1)
                        act.wait_ge(s["wTp"], i + 1)
                        nc.scalar.copy(wT[:, :], pW[:, 0:P]).then_inc(s["wTs"], 1)
                        act.wait_ge(s["aT"], i + 1)
                        nc.scalar.copy(accT[:, :], pW[:, P:2 * P]).then_inc(s["aTs"], 1)

            @block.tensor
            def _(pe):
                with only_if(pe, flag, 0):
                    pe.wait_ge(s["wload"], 7 * 16)
                    nc.tensor.transpose(pT[:, 0:P], w1[:, :], ident[:, :]).then_inc(s["wT"], 1)
                    pe.wait_ge(s["prep"], 1)
                    with pe.Fori(0, ITEMS) as i:
                        pe.wait_ge(s["h"], i * 16 + 16)
                        nc.tensor.transpose(pT[:, 0:P], hb[:, :], ident[:, :]).then_inc(s["hT"], 1)
                        pe.wait_ge(s["hTs"], i + 1)
                        nc.tensor.matmul(pQ[:, 0:P], w1t[:, :], hT[:, :], start=True, stop=True).then_inc(s["q"], 1)
                        nc.tensor.matmul(pA[:, 0:2 * P], hT[:, :], w23[:, :, :].rearrange("p a b -> p (a b)"), start=True, stop=True).then_inc(s["a"], 1)
                        pe.wait_ge(s["g"], i + 1)
                        nc.tensor.transpose(pT2[:, 0:P], g[:, :], ident[:, :]).then_inc(s["gT"], 1)
                        pe.wait_ge(s["qs"], i + 1)
                        pe.wait_ge(s["gTs"], i + 1)
                        pe.wait_ge(s["pen"], i + 1)
                        nc.tensor.matmul(pS[:, 0:P], qT[:, :], gT[:, :], start=True, stop=False)
                        nc.tensor.matmul(pS[:, 0:P], hT[:, :], b1bc[:, :], start=False, stop=False)
                        nc.tensor.matmul(pS[:, 0:P], pen[:, :], identb[:, :], start=False, stop=True).then_inc(s["s"], 1)
                        pe.wait_ge(s["w"], i + 1)
                        nc.tensor.transpose(pW[:, 0:P], w[:, :], ident[:, :]).then_inc(s["wTp"], 1)
                        pe.wait_ge(s["wTs"], i + 1)
                        nc.tensor.matmul(pG[:, 0:P], wT[:, :], g[:, :], start=True, stop=True).then_inc(s["G"], 1)
                        pe.wait_ge(s["accn"], i + 1)
                        nc.tensor.transpose(pW[:, P:2 * P], accn[:, :], ident[:, :]).then_inc(s["aT"], 1)
                        pe.wait_ge(s["aTs"], i + 1)
                        nc.tensor.matmul(pN[:, 0:P], accT[:, :], w1[:, :], start=True, stop=True).then_inc(s["N"], 1)


RSQRT_K = 2 + 3 * 3
POLY_K = 1 + 4 + 1
NORMALISE_K = 3 + RSQRT_K
NORM_K = 3 + RSQRT_K
MAPS_K = 7 + 6 + 1 + NORMALISE_K


class OffsetChain(Chain):

    def __init__(self, eng, sem, per_turn, turn, ahead):
        super().__init__(eng, sem, per_turn, turn)
        self.ahead = ahead

    def __call__(self, ins, alone=False):
        self.n += 1
        ins.then_inc(self.sem, 1)
        (wait_apart if alone else wait)(self.eng, self.sem, self.turn * self.per_turn + (self.n + self.ahead))


class Block_:

    def __init__(self, q, k, ring=UN, total=NB):
        self.q, self.k, self.ring, self.total = q, k, ring, total

    def __sub__(self, back):
        return Block_(self.q, self.k - back, self.ring, self.total)

    def __add__(self, ahead):
        return Block_(self.q, self.k + ahead, self.ring, self.total)

    @property
    def number(self):
        return self.q * self.ring + self.k

    @property
    def slot(self):
        return self.k % self.ring

    def count(self, more=1):
        return self.q * self.ring + (self.k + more)

    def dma_count(self, turns_back=0, slots=None):
        slots = slots or self.ring
        return (self.q * (self.ring // slots) + (self.k // slots + 1 - turns_back)) * 16

    def group_count(self, size, more=1):
        return self.q * (self.ring // size) + (self.k // size + more)

    def exists(self, back=0):
        if not isinstance(self.q, int):
            return True
        return 0 <= self.number - back < self.total


def fast_turns(eng, body, ahead, behind, ring=UN, total=NB, peeled=2):
    whole = total // ring
    for k in range(-ahead, peeled * ring):
        body(Block_(0, k, ring, total))
    with eng.Fori(peeled, whole - 1) as q:
        for k in range(ring):
            body(Block_(q, k, ring, total))
    for k in range(ring + total % ring + behind):
        body(Block_(whole - 1, k, ring, total))


def fast_layer(nc, l, hin, hout, ea, d, tab, weights, consts):
    W1, b1, W2, b2, W3, b3 = weights
    ident, identb, iota_n, block_row = (consts[n] for n in ("ident", "identb", "iota_n", "block_row"))
    starts, flag = tab["starts"], tab["flag"]
    CB, CQ = 2 * P, 2 * P + 4
    AQ = CQ + P
    AHEAD = 6
    ctx = ExitStack()
    with ctx:
        sb = lambda name, shape, dt: ctx.enter_context(nc.sbuf_tensor(f"q{l}_{name}", shape, dt))
        pb = lambda name, shape, dt: ctx.enter_context(nc.psum_tensor(f"q{l}_{name}", shape, dt))
        phase_sem = ctx.enter_context(phase_semaphores(nc))
        sem = lambda name: phase_sem(f"q{l}_{name}")
        w1 = sb("w1", [P, P], F32)
        w1t = sb("w1t", [P, P], F32)
        w23 = sb("w23", [P, CQ], F32)
        w2 = sb("w2", [P, P], F32)
        brow = sb("brow", [3, 3, P], F32)
        bias = sb("bias", [3, CQ], F32)
        left = sb("left", [3, 2, CQ], F32)
        part = sb("part", [3, 3, CQ], BF16)
        own = sb("own", [3, 3, CQ], F32)
        parts = sb("parts", [3, CQ], BF16)
        rec = sb("rec", [LANES, UN, 2, 2], I32)
        hb = sb("hb", [P, UN, P], F32)
        hs = sb("hs", [LANES, UN, 2 * P], F32)
        ev = sb("ev", [LANES, UN, 2 * P], F32)
        g = sb("g", [LANES, UN, 2 * P], F32)
        loc = sb("loc", [LANES, UN, 2], F32)
        iota_h = sb("iota_h", [LANES, P], BF16)
        pen = sb("pen", [LANES, UN, 2, P], BF16)
        hgT = sb("hgT", [P, 4, P + W], F32)
        aq = sb("aq", [P, UN, AQ], F32)
        w = sb("w", [P, 2, W], F32)
        wT = sb("wT", [LANES, 2, 2, P], F32)
        sT = sb("sT", [P, 2, P], F32)
        pre = sb("pre", [P, 2, P], F32)
        o = sb("o", [P, UN, P], F32)
        col = {n: sb(n, [P, UN], F32) for n in ("mx", "M", "nM", "L", "Lg", "inv", "has")}
        pT = [pb(f"pT{k}", [P, 512], F32) for k in range(2)]
        pS = [pb(f"pS{k}", [P, 512], F32) for k in range(2)]
        pA, pW, pG, pN = (pb(n, [P, 512], F32) for n in ("pA", "pW", "pG", "pN"))
        s_wload, s_wT, s_prep, s_w = sem("wload"), sem("wT"), sem("prep"), sem("wdve")
        ring = lambda name: [sem(f"{name}{k}") for k in range(UN)]
        groups = lambda name: [sem(f"{name}{k}") for k in range(UN // HG)]
        s_h, s_st = groups("h"), groups("st")
        s_rec, s_ev, s_hsa, s_hsb = (ring(n) for n in ("rec", "ev", "hsa", "hsb"))
        (s_g, s_loc, s_pen, s_T, s_evT, s_A, s_evA, s_S, s_mx, s_M, s_nM, s_exp, s_Wt, s_evW, s_G, s_evG, s_N,
         s_L, s_inv, s_mix, s_pre, s_sum, s_out) = (
            sem(n) for n in ("g", "loc", "pen", "T", "evT", "A", "evA", "S", "mx", "M", "nM", "exp", "Wt", "evW", "G",
                             "evG", "N", "L", "inv", "mix", "pre", "sum", "out"))

        with nc.Block() as block:
            @block.sync
            def _(sp):
                begins = {}

                def begin(n):
                    if n.exists():
                        begins[n.slot] = sp.value_load(starts[0:1, bass.ds(n.number, 1)], min_val=0, max_val=E - W)

                def loads(n):
                    if not n.exists():
                        return
                    k = n.slot
                    start = begins[k]
                    if n.exists(UN):
                        sp.wait_ge(s_pen, n.count(1 - UN))
                        sp.wait_ge(s_g, n.count(1 - UN))
                    sp.dma_start(rec[:, k, :, :], d["pairs"][bass.ds(start, W), :].rearrange("(p j) t -> p j t", j=2)).then_inc(s_rec[k], 16)
                    sp.dma_start(ev[:, k, :], ea[bass.ds(start, W), :].rearrange("(p j) f -> p (j f)", j=2)).then_inc(s_ev[k], 16)

                def rows(n):
                    if not n.exists() or n.slot % HG:
                        return
                    k = n.slot
                    if n.exists(UN):
                        sp.wait_ge(s_T, n.count(HG - UN))
                    left = NB - n.number if isinstance(n.q, int) else HG
                    if left >= HG:
                        sp.dma_start(hb[:, k:k + HG, :], hin[bass.ds(n.number * P, HG * P), :].rearrange("(b p) f -> p b f", p=P)).then_inc(s_h[k // HG], 16)
                    else:
                        first = n.number * P
                        last = (NB - 1) * P
                        sp.dma_start(hb[:, k:k + left - 1, :], hin[first:last, :].rearrange("(b p) f -> p b f", p=P)).then_inc(s_h[k // HG], 16)
                        sp.dma_start(hb[0:hin.shape[0] - last, k + left - 1, :], hin[last:hin.shape[0], :]).then_inc(s_h[k // HG], 16)

                def store(n):
                    if not n.exists() or (n.slot % HG != HG - 1 and not (isinstance(n.q, int) and n.number == NB - 1)):
                        return
                    count = n.slot % HG + 1
                    first = n - (count - 1)
                    sp.wait_ge(s_out, n.count())
                    sp.dma_start(hout[bass.ds(first.number * P, count * P), :].rearrange("(b p) f -> p b f", p=P),
                                 o[:, first.slot:n.slot + 1, :]).then_inc(s_st[n.slot // HG], 16)

                def body(n):
                    if n.slot % HG == 0:
                        for k in range(HG):
                            begin(n + (AHEAD + k))
                    rows(n + 4)
                    loads(n + AHEAD)
                    store(n - 8)

                with only_if(sp, flag, 1):
                    sp.dma_start(w1[:, :], W1).then_inc(s_wload, 16)
                    sp.dma_start(w2[:, :], W2).then_inc(s_wload, 16)
                    sp.dma_start(w23[:, 0:P], W3).then_inc(s_wload, 16)
                    sp.dma_start(w23[:, 2 * P:2 * P + 1], b1.rearrange("(n o) -> n o", o=1)).then_inc(s_wload, 16)
                    for n, b in enumerate((b1, b2, b3)):
                        sp.dma_start(brow[:, n, :], b.rearrange("(o n) -> o n", o=1).to_broadcast([3, P])).then_inc(s_wload, 16)
                    fast_turns(sp, body, 8, 8)
                    for k in range(UN // HG):
                        sp.wait_ge(s_st[k], 16 * len(range(HG * k, NB, UN)))

            @block.gpsimd
            def _(pool):
                def body(last_row, n):
                    m = n + 2
                    if not m.exists():
                        return
                    k = m.slot
                    if m.exists(UN):
                        pool.wait_ge(s_g, m.count(1 - UN))
                    wait_apart(pool, s_rec[k], m.dma_count())
                    for j, s in enumerate((s_hsa, s_hsb)):
                        pool.indirect_dma_start(out=hs[:, k, j * P:(j + 1) * P], out_offset=None, in_=hin,
                                                in_offset=bass.IndirectOffsetOnAxis(ap=rec[:, k, j, 1:2], axis=0),
                                                bounds_check=last_row, oob_is_err=False).then_inc(s[k], 16)

                with only_if(pool, flag, 1):
                    last_row = pool.to_reg(N - 1)
                    fast_turns(pool, lambda n: body(last_row, n), 2, 0)

            @block.vector
            def _(dve):
                V = nc.vector
                at = lambda name, n: col[name][:, n.slot:n.slot + 1]

                def mask(n):
                    k = n.slot
                    dve.wait_ge(s_rec[k], n.dma_count())
                    V.tensor_scalar(loc[:, k, :], rec[:, k, :, 0], block_row[0:LANES, bass.ds(n.number, 1)], None, ALU.subtract).then_inc(s_loc, 1)

                def mask_rows(n):
                    k = n.slot
                    dve.wait_ge(s_loc, n.count())
                    for j in range(2):
                        last = V.tensor_scalar(pen[:, k, j, :], iota_h[:, :], loc[:, k, j:j + 1], MASKED, ALU.not_equal, ALU.mult)
                    last.then_inc(s_pen, 1)

                def add_edges(n):
                    k = n.slot
                    dve.wait_ge(s_ev[k], n.dma_count())
                    dve.wait_ge(s_hsa[k], n.dma_count())
                    dve.wait_ge(s_hsb[k], n.dma_count())
                    if n.exists(UN):
                        dve.wait_ge(s_G, n.count(1 - UN))
                    V.tensor_tensor(g[:, k, :], hs[:, k, :], ev[:, k, :], ALU.add).then_inc(s_g, 1)

                def maximum(n):
                    dve.wait_ge(s_S, n.count())
                    V.reduce_max(at("mx", n), pS[n.slot % 2][:, 0:W], AX.X).then_inc(s_mx, 1)

                def maximum_2(n):
                    dve.wait_ge(s_evA, n.count())
                    dve.wait_ge(s_mx, n.count())
                    V.tensor_scalar(at("M", n), at("mx", n), aq[:, n.slot, CB:CB + 1], M_NONE, ALU.add, ALU.max).then_inc(s_M, 1)

                def maximum_3(n):
                    dve.wait_ge(s_M, n.count())
                    V.tensor_tensor(at("nM", n), aq[:, n.slot, CB:CB + 1], at("M", n), ALU.subtract).then_inc(s_nM, 1)

                def weights_sum(n):
                    dve.wait_ge(s_exp, n.count())
                    V.tensor_scalar(at("has", n), at("L", n), 0.0, None, ALU.is_gt)
                    V.tensor_scalar(at("Lg", n), at("L", n), 1e-30, None, ALU.max).then_inc(s_L, 1)

                def weights_inv(n):
                    dve.wait_ge(s_L, n.count())
                    if n.exists(UN):
                        dve.wait_ge(s_st[n.slot // HG], n.dma_count(1))
                    V.reciprocal(at("inv", n), at("Lg", n)).then_inc(s_inv, 1)
                    V.scalar_tensor_tensor(o[:, n.slot, :], aq[:, n.slot, P:2 * P], at("has", n), aq[:, n.slot, 0:P],
                                           ALU.mult, ALU.add).then_inc(s_mix, 1)

                def finish(n):
                    dve.wait_ge(s_N, n.count())
                    dve.wait_ge(s_inv, n.count())
                    dve.wait_ge(s_mix, n.count())
                    V.scalar_tensor_tensor(pre[:, n.slot % 2, :], pN[:, 0:P], at("inv", n), o[:, n.slot, :],
                                           ALU.mult, ALU.add).then_inc(s_sum, 1)

                def finish_2(n):
                    dve.wait_ge(s_sum, n.count())
                    V.scalar_tensor_tensor(o[:, n.slot, :], pre[:, n.slot % 2, :], SLOPE, pre[:, n.slot % 2, :],
                                           ALU.mult, ALU.max).then_inc(s_out, 1)

                def body(n):
                    for step, ahead in ((maximum, -3), (mask, 1), (maximum_2, -3), (mask_rows, 1), (maximum_3, -3), (add_edges, 1),
                                        (weights_sum, -4), (finish, -7), (weights_inv, -4), (finish_2, -7)):
                        m = n + ahead
                        if m.exists():
                            step(m)

                with only_if(dve, flag, 1):
                    link = Chain(dve, s_w)
                    dve.wait_ge(s_wload, 7 * 16)
                    link(V.memset(w23[:, CB + 1:CQ], 0.0))
                    link(V.tensor_copy(iota_h[:, :], iota_n[0:LANES, :]))
                    link(V.tensor_tensor(w23[:, P:2 * P], w2[:, :], w23[:, 0:P], ALU.subtract))
                    link(V.memset(bias[:, :], 0.0))
                    link(V.tensor_copy(bias[:, 0:P], brow[:, 2, :]))
                    link(V.tensor_tensor(bias[:, P:2 * P], brow[:, 0, :], brow[:, 1, :], ALU.add))
                    link(V.tensor_tensor(bias[:, P:2 * P], bias[:, P:2 * P], brow[:, 2, :], ALU.subtract))
                    link(V.tensor_copy(part[:, 0, :], bias[:, :]))
                    link(V.tensor_tensor(left[:, 0, :], bias[:, :], part[:, 0, :], ALU.subtract))
                    link(V.tensor_copy(part[:, 1, :], left[:, 0, :]))
                    link(V.tensor_tensor(left[:, 1, :], left[:, 0, :], part[:, 1, :], ALU.subtract))
                    link(V.tensor_copy(part[:, 2, :], left[:, 1, :]))
                    for k in range(3):
                        link(V.tensor_scalar(own[:, k, :], part[:, k, :], ident[0:3, k:k + 1], None, ALU.mult))
                    link(V.tensor_tensor(own[:, 0, :], own[:, 0, :], own[:, 1, :], ALU.add))
                    link(V.tensor_tensor(parts[:, :], own[:, 0, :], own[:, 2, :], ALU.add))
                    dve.wait_ge(s_wT, 1)
                    V.tensor_copy(w1t[:, :], pT[0][:, 0:P]).then_inc(s_prep, 1)
                    fast_turns(dve, body, 1, 7)

            @block.scalar
            def _(act):
                A = nc.scalar
                at = lambda name, n: col[name][:, n.slot:n.slot + 1]

                def transposes_out(n):
                    act.wait_ge(s_T, n.count())
                    A.copy(hgT[:, n.slot % 4, :], pT[n.slot % 2][:, 0:P + W]).then_inc(s_evT, 1)

                def products_out(n):
                    act.wait_ge(s_A, n.count())
                    if n.exists(UN):
                        act.wait_ge(s_mix, n.count(1 - UN))
                    A.copy(aq[:, n.slot, :], pA[:, 0:AQ]).then_inc(s_evA, 1)

                def exponentials(n):
                    act.wait_ge(s_nM, n.count())
                    A.activation(w[:, n.slot % 2, :], pS[n.slot % 2][:, 0:W], ACT.Exp, bias=at("nM", n),
                                 accum_out=at("L", n)).then_inc(s_exp, 1)

                def weights_out(n):
                    act.wait_ge(s_Wt, n.count())
                    A.copy(wT[:, n.slot % 2, :, :], pW[0:LANES, 0:2 * P].rearrange("p (j n) -> p j n", j=2)).then_inc(s_evW, 1)

                def sums_out(n):
                    act.wait_ge(s_G, n.count())
                    if n.exists(2):
                        act.wait_ge(s_N, n.count(-1))
                    A.copy(sT[:, n.slot % 2, :], pG[:, 0:P]).then_inc(s_evG, 1)

                def body(n):
                    for step, back in ((transposes_out, 0), (products_out, 1), (exponentials, 3), (weights_out, 4), (sums_out, 5)):
                        if (n - back).exists():
                            step(n - back)

                with only_if(act, flag, 1):
                    fast_turns(act, body, 0, 5)

            @block.tensor
            def _(pe):
                T = nc.tensor

                def transposes(n):
                    k = n.slot
                    ends = isinstance(n.q, int) and n.number >= NB - NB % HG
                    pe.wait_ge(s_h[k // HG], n.dma_count(-1 if ends else 0))
                    pe.wait_ge(s_g, n.count())
                    if n.exists(2):
                        pe.wait_ge(s_evT, n.count(-1))
                    T.transpose(pT[k % 2][:, 0:P], hb[:, k, :], ident[:, :])
                    for j in range(2):
                        last = T.transpose(pT[k % 2][:, P + j * LANES:P + (j + 1) * LANES], g[:, k, j * P:(j + 1) * P], ident[0:LANES, 0:LANES])
                    last.then_inc(s_T, 1)

                def products(n):
                    k = n.slot
                    pe.wait_ge(s_evT, n.count())
                    if n.exists(1):
                        pe.wait_ge(s_evA, n.count(0))
                    T.matmul(pA[:, 0:CQ], hgT[:, k % 4, 0:P], w23[:, :], start=True, stop=False)
                    T.matmul(pA[:, 0:CQ], consts["onesb"][0:3, :], parts[:, :], start=False, stop=True)
                    T.matmul(pA[:, CQ:AQ], w1t[:, :], hgT[:, k % 4, 0:P], start=True, stop=True).then_inc(s_A, 1)

                def scores(n):
                    k = n.slot
                    pe.wait_ge(s_evA, n.count())
                    pe.wait_ge(s_pen, n.count())
                    if n.exists(2):
                        pe.wait_ge(s_exp, n.count(-1))
                    T.matmul(pS[k % 2][:, 0:W], aq[:, k, CQ:AQ], hgT[:, k % 4, P:P + W], start=True, stop=False)
                    for j in range(2):
                        last = T.matmul(pS[k % 2][:, j * LANES:(j + 1) * LANES], pen[:, k, j, :], identb[0:LANES, 0:LANES], start=False, stop=(j == 1))
                    last.then_inc(s_S, 1)

                def weights_T(n):
                    k = n.slot
                    pe.wait_ge(s_exp, n.count())
                    if n.exists(1):
                        pe.wait_ge(s_evW, n.count(0))
                    for j in range(2):
                        last = T.transpose(pW[0:LANES, j * P:(j + 1) * P], w[:, k % 2, j * LANES:(j + 1) * LANES], ident[:, :])
                    last.then_inc(s_Wt, 1)

                def weighted_sums(n):
                    k = n.slot
                    pe.wait_ge(s_evW, n.count())
                    if n.exists(1):
                        pe.wait_ge(s_evG, n.count(0))
                    for j in range(2):
                        last = T.matmul(pG[:, 0:P], g[:, k, j * P:(j + 1) * P], wT[:, k % 2, j, :], start=(j == 0), stop=(j == 1))
                    last.then_inc(s_G, 1)

                def through_w1(n):
                    pe.wait_ge(s_evG, n.count())
                    if n.exists(1):
                        pe.wait_ge(s_sum, n.count(0))
                    T.matmul(pN[:, 0:P], sT[:, n.slot % 2, :], w1[:, :], start=True, stop=True).then_inc(s_N, 1)

                def body(n):
                    for step, back in ((transposes, 0), (products, 1), (scores, 2), (weights_T, 4), (weighted_sums, 5), (through_w1, 6)):
                        if (n - back).exists():
                            step(n - back)

                with only_if(pe, flag, 1):
                    pe.wait_ge(s_wload, 7 * 16)
                    T.transpose(pT[0][:, 0:P], w1[:, :], ident[:, :]).then_inc(s_wT, 1)
                    pe.wait_ge(s_prep, 1)
                    fast_turns(pe, body, 0, 6)


def fast_support(nc, d, tab, out, consts):
    GB = 16
    RING = 2 * GB
    GC = GB * SH
    CHUNK = 4
    START = GB + 2
    ZLOAD, APPLY, STORE = START + 4, START + 17, START + 18
    iota_s, block_row = consts["iota_s"], consts["block_row"]
    starts, flag, xtab = tab["starts"], tab["flag"], d["xtab"]
    LASTROWS = N - (SB - SB % GB) * SN
    ctx = ExitStack()
    with ctx:
        sb = lambda name, shape, dt: ctx.enter_context(nc.sbuf_tensor(f"r_{name}", shape, dt))
        pb = lambda name, shape, dt: ctx.enter_context(nc.psum_tensor(f"r_{name}", shape, dt))
        phase_sem = ctx.enter_context(phase_semaphores(nc))
        sem = lambda name: phase_sem(f"r_{name}")
        ring = lambda name: [sem(f"{name}{k}") for k in range(UN)]
        rec = sb("rec", [P, UN, SJ, 4], F32)
        idx = sb("idx", [P, UN, SJ], I32)
        loc = sb("loc", [P, UN, SJ], F32)
        xg = sb("xg", [P, UN, SJ, XW], F32)
        wf = sb("wf", [P, UN, SJ], F32)
        A = sb("A", [P, UN, SJ, SN], F32)
        sup = sb("sup", [P, RING * SH, P], F32)
        z = sb("z", [P, RING * SH, P], F32)
        sq = sb("sq", [P, UN, SH, P], F32)
        st6 = sb("st6", [P, GC, 6], F32)
        mv = sb("mv", [P, 2, GC, 2], F32)
        cols = sb("cols", [P, 2, 14, GC], F32)
        nrm = sb("nrm", [P, 2, 2, GC], F32)
        pR = [pb(f"p{k}", [P, 512], F32) for k in range(UN)]
        s_rec = ring("rec")
        s_xg = [ring(f"xg{j}_") for j in range(SJ)]
        s_z = [sem(f"z{k}") for k in range(2)]
        s_st = [sem(f"st{k}") for k in range(RING // CHUNK)]
        s_idx, s_loc, s_wf, s_A, s_R, s_sup, s_dve, s_arg, s_fn, s_mapped, s_nrm, s_out = (
            sem(n) for n in ("idx", "loc", "wf", "A", "R", "sup", "dve", "arg", "fn", "mapped", "nrm", "out"))

        def turns(eng, body, ahead, behind):
            fast_turns(eng, body, ahead, behind, RING, SB, 2)

        def group_at(n, distance):
            first = n - distance
            return first if first.slot % GB == 0 and first.exists() else None

        def blocks_of(first):
            return SB - first.number if isinstance(first.q, int) and first.number + GB > SB else GB

        with nc.Block() as block:
            @block.sync
            def _(sp):
                def load(m):
                    start = sp.value_load(starts[0:1, bass.ds(m.number, 1)], min_val=0, max_val=E - SW)
                    if m.exists(UN):
                        sp.wait_ge(s_A, m.count(1 - UN))
                    k = m.slot % UN
                    sp.dma_start(rec[:, k, :, :], d["src", "recs"][bass.ds(start, SW), :].rearrange("(p j) t -> p j t", j=SJ)).then_inc(s_rec[k], 16)

                def transfers(table, tile, row, rows, column, to_table, s):
                    whole = rows // P
                    parts = [(table[bass.ds(row, whole * P), 0:P].rearrange("(c p) f -> p c f", p=P), tile[:, column:column + whole, :])]
                    if rows % P:
                        parts.append((table[row + whole * P:row + rows, 0:P], tile[0:rows % P, column + whole, :]))
                    for there, here in parts:
                        sp.dma_start(there if to_table else here, here if to_table else there).then_inc(s, 16)

                def load_z(first):
                    if first.exists(RING):
                        for c in range(GB // CHUNK):
                            sp.wait_ge(s_st[first.slot // CHUNK + c], first.dma_count(1))
                    rows = GB * SN if blocks_of(first) == GB else LASTROWS
                    transfers(xtab, z, first.number * SN, rows, first.slot * SH, False, s_z[first.slot // GB])

                def store(m):
                    first = m - (CHUNK - 1)
                    sp.wait_ge(s_out, m.count())
                    rows = LASTROWS if isinstance(m.q, int) and m.number == SB - 1 else CHUNK * SN
                    transfers(out, z, first.number * SN, rows, first.slot * SH, True, s_st[first.slot // CHUNK])

                def body(n):
                    if (n + 7).exists():
                        load(n + 7)
                    first = group_at(n, ZLOAD)
                    if first:
                        load_z(first)
                    m = n - STORE
                    if m.exists() and m.slot % CHUNK == CHUNK - 1:
                        store(m)

                with only_if(sp, flag, 1):
                    turns(sp, body, 7, STORE)
                    for k in range(RING // CHUNK):
                        sp.wait_ge(s_st[k], 16 * (len(range(k, SB // CHUNK, RING // CHUNK)) + (k == (SB // CHUNK - 1) % (RING // CHUNK))))

            @block.gpsimd
            def _(pool):
                def body(last_row, n):
                    m = n + 2
                    if not m.exists():
                        return
                    k = m.slot % UN
                    if m.exists(UN):
                        pool.wait_ge(s_R, m.count(1 - UN))
                    wait_apart(pool, s_idx, m.count())
                    for j, s in enumerate(s_xg):
                        pool.indirect_dma_start(out=xg[:, k, j, :], out_offset=None, in_=xtab,
                                                in_offset=bass.IndirectOffsetOnAxis(ap=idx[:, k, j:j + 1], axis=0),
                                                bounds_check=last_row, oob_is_err=False).then_inc(s[k], 16)

                with only_if(pool, flag, 1):
                    last_row = pool.to_reg(N - 1)
                    turns(pool, lambda n: body(last_row, n), 2, 0)

            @block.vector
            def _(dve):
                V = nc.vector

                def indices(m):
                    k = m.slot % UN
                    dve.wait_ge(s_rec[k], m.dma_count(slots=UN))
                    if m.exists(UN):
                        for j in range(SJ):
                            dve.wait_ge(s_xg[j][k], m.dma_count(1, slots=UN))
                    V.tensor_copy(idx[:, k, :], rec[:, k, :, 1]).then_inc(s_idx, 1)
                    V.tensor_scalar(loc[:, k, :], rec[:, k, :, 0], block_row[:, bass.ds(m.number * SH, 1)], None, ALU.subtract).then_inc(s_loc, 1)

                def weights(n):
                    k = n.slot % UN
                    for j in range(SJ):
                        dve.wait_ge(s_xg[j][k], n.dma_count(slots=UN))
                    V.tensor_tensor(wf[:, k, :], rec[:, k, :, 2], xg[:, k, :, P], ALU.mult).then_inc(s_wf, 1)

                def matrix(n):
                    k = n.slot % UN
                    dve.wait_ge(s_loc, n.count())
                    dve.wait_ge(s_wf, n.count())
                    if n.exists(UN):
                        dve.wait_ge(s_R, n.count(1 - UN))
                    for j in range(SJ):
                        last = V.tensor_scalar(A[:, k, j, :], iota_s[:, :], loc[:, k, j:j + 1], wf[:, k, j:j + 1], ALU.is_equal, ALU.mult)
                    last.then_inc(s_A, 1)


                def norm(link, c, first):
                    dve.wait_ge(s_sup, (first + (blocks_of(first) - 1)).count())
                    rsqrt_steps(nc, link, c(5), c(4), c(2), c(3))

                def norm_inverse(link, c, first):
                    link(V.tensor_tensor(c(6), c(4), c(5), ALU.mult))
                    link(V.tensor_scalar(c(6), c(6), 1e-15, None, ALU.max))
                    V.tensor_copy(c(7), c(6)).then_inc(s_arg, 1)
                    link(V.reciprocal(c(5), c(6)))
                    link(V.tensor_scalar(c(10), c(4), 0.3 ** 2, None, ALU.min))

                def series(link, c, first):
                    even_poly_steps(nc, link, c(11), c(10), TANH_C)

                def quotient(link, c, first):
                    dve.wait_ge(s_fn, first.group_count(GB))
                    link(V.tensor_scalar(c(12), c(8), 1.0, None, ALU.add))
                    link(V.reciprocal(c(13), c(12)))
                    link(V.scalar_tensor_tensor(c(12), c(8), 1.0, c(13), ALU.subtract, ALU.mult))
                    link(V.scalar_tensor_tensor(c(12), c(12), -1.0, c(5), ALU.mult, ALU.mult))
                    link(V.tensor_tensor(c(11), c(11), c(12), ALU.subtract))
                    link(V.scalar_tensor_tensor(c(11), c(6), 0.3, c(11), ALU.is_lt, ALU.mult))
                    link(V.tensor_tensor(c(11), c(11), c(12), ALU.add))

                def bound(link, c, first):
                    link(V.tensor_tensor(c(12), c(11), c(6), ALU.mult))
                    link(V.tensor_scalar(c(12), c(12), 1e-15, None, ALU.max))
                    link(V.reciprocal(c(13), c(12)))
                    link(V.tensor_scalar(c(13), c(13), 0.996, -1.0, ALU.mult, ALU.add))
                    link(V.scalar_tensor_tensor(c(13), c(12), 0.996, c(13), ALU.is_gt, ALU.mult))
                    link(V.scalar_tensor_tensor(c(13), c(13), 1.0, c(11), ALU.add, ALU.mult))

                def half(first, which):
                    g = blocks_of(first) * SH
                    return range(which * g // 2, (which + 1) * g // 2)

                def add(first, which):
                    for r in half(first, which):
                        at = first.slot * SH + r
                        last = V.scalar_tensor_tensor(z[:, at, :], sup[:, at, :], cols[:, first.slot // GB, 13, r:r + 1],
                                                      z[:, at, :], ALU.mult, ALU.add)
                    return last

                def add_first(link, c, first):
                    dve.wait_ge(s_z[first.slot // GB], first.dma_count(0 if blocks_of(first) == GB else -1))
                    add(first, 0)

                def add_second(link, c, first):
                    add(first, 1).then_inc(s_mapped, 1)

                def statistics(first, which):
                    for r in half(first, which):
                        last = V.bn_stats(st6[:, r, :], z[:, first.slot * SH + r, :])
                    return last

                def statistics_first(link, c, first):
                    dve.wait_ge(s_mapped, first.group_count(GB))
                    statistics(first, 0)

                def statistics_second(link, c, first):
                    link(statistics(first, 1), alone=True)

                def mean(link, c, first):
                    par = first.slot // GB
                    g = blocks_of(first) * SH
                    for r in range(g):
                        last = V.bn_aggr(mv[:, par, r, :], st6[:, r, :])
                    link(last)
                    link(V.tensor_scalar(c(0), mv[:, par, 0:g, 1], EPS, None, ALU.add))

                def deviation(link, c, first):
                    par = first.slot // GB
                    g = blocks_of(first) * SH
                    rsqrt_steps(nc, link, c(1), c(0), c(2), c(3))
                    V.tensor_copy(nrm[:, par, 0, 0:g], c(1))
                    V.scalar_tensor_tensor(nrm[:, par, 1, 0:g], mv[:, par, 0:g, 0], -1.0, c(1), ALU.mult, ALU.mult).then_inc(s_nrm, 1)

                stages = ((norm, 0, RSQRT_K), (norm_inverse, 1, 4), (series, 2, POLY_K), (quotient, 6, 7), (bound, 7, 6),
                          (add_first, 8, 0), (add_second, 9, 0), (statistics_first, 10, 0), (statistics_second, 11, 1),
                          (mean, 12, 2), (deviation, 13, RSQRT_K))
                per_group = sum(k for _, _, k in stages)

                def body(n):
                    if (n + 5).exists():
                        indices(n + 5)
                    if n.exists():
                        weights(n)
                    before = 0
                    for stage, after, links in stages:
                        first = group_at(n, START + after)
                        if first:
                            link = OffsetChain(dve, s_dve, per_group, first.group_count(GB, 0), before)
                            g = blocks_of(first) * SH
                            stage(link, lambda i: cols[:, first.slot // GB, i, 0:g], first)
                            assert link.n == links, (stage, link.n)
                        before += links
                    if n.exists():
                        matrix(n)

                with only_if(dve, flag, 1):
                    turns(dve, body, 5, START + 13)

            @block.tensor
            def _(pe):
                def body(n):
                    if not n.exists():
                        return
                    k = n.slot % UN
                    pe.wait_ge(s_A, n.count())
                    if n.exists(UN):
                        pe.wait_ge(s_sup, n.count(1 - UN))
                    for h in range(SH):
                        for j in range(SJ):
                            last = nc.tensor.matmul(pR[k][:, h * P:(h + 1) * P], A[:, k, j, h * P:(h + 1) * P], xg[:, k, j, 0:P],
                                                    start=(j == 0), stop=(j == SJ - 1))
                    last.then_inc(s_R, 1)

                with only_if(pe, flag, 1):
                    turns(pe, body, 0, 0)

            @block.scalar
            def _(act):
                def sums(n):
                    k = n.slot % UN
                    act.wait_ge(s_R, n.count())
                    if n.slot % GB == 0 and n.exists(RING):
                        act.wait_ge(s_mapped, (n - RING).group_count(GB))
                    nc.scalar.copy(sup[:, n.slot * SH:(n.slot + 1) * SH, :], pR[k][:, 0:SN].rearrange("p (h f) -> p h f", h=SH))
                    for h in range(SH):
                        c = (n.slot % GB) * SH + h
                        last = nc.scalar.activation(sq[:, k, h, :], pR[k][:, h * P:(h + 1) * P], ACT.Square,
                                                    accum_out=cols[:, n.slot // GB, 4, c:c + 1])
                    last.then_inc(s_sup, 1)

                def apply(m):
                    if m.slot % GB == 0:
                        act.wait_ge(s_nrm, m.group_count(GB))
                    par = m.slot // GB
                    for h in range(SH):
                        c = (m.slot % GB) * SH + h
                        row = z[:, m.slot * SH + h, :]
                        last = nc.scalar.activation(row, row, ACT.Identity, bias=nrm[:, par, 1, c:c + 1], scale=nrm[:, par, 0, c:c + 1])
                    last.then_inc(s_out, 1)

                def body(n):
                    if n.exists():
                        sums(n)
                    first = group_at(n, START + 4)
                    if first:
                        g = blocks_of(first) * SH
                        act.wait_ge(s_arg, first.group_count(GB))
                        nc.scalar.activation(cols[:, first.slot // GB, 8, 0:g], cols[:, first.slot // GB, 7, 0:g], ACT.Exp,
                                             scale=-2.0).then_inc(s_fn, 1)
                    m = n - APPLY
                    if m.exists():
                        apply(m)

                with only_if(act, flag, 1):
                    turns(act, body, 0, APPLY)


def general_support(nc, d, tab, consts):
    keep, base, flag = tab["keep"], tab["base"], tab["flag"]
    iota_s = consts["iota_s"]
    recs, items, xtab = d["src", "recs"], d["src", "items"], d["xtab"]
    ITEMS = SB + NB - 1
    ctx = ExitStack()
    with ctx:
        sb = lambda name, shape, dt: ctx.enter_context(nc.sbuf_tensor(f"f_{name}", shape, dt))
        pb = lambda name, shape, dt: ctx.enter_context(nc.psum_tensor(f"f_{name}", shape, dt))
        phase_sem = ctx.enter_context(phase_semaphores(nc))
        sem = lambda name: phase_sem(f"f_{name}")
        rec, idx = sb("rec", [P, 4], F32), sb("idx", [P, 1], I32)
        xg = sb("xg", [P, XW], F32)
        wf, loc, A = sb("wf", [P, 1], F32), sb("loc", [P, 1], F32), sb("A", [P, SN], F32)
        acc = sb("acc", [P, SN], F32)
        pG = pb("pG", [P, 512], F32)
        s = {n: sem(n) for n in ("rec", "idx", "xg", "A", "G", "dve", "out", "st")}
        with nc.Block() as block:
            @block.sync
            def _(sp):
                with only_if(sp, flag, 0):
                    with sp.Fori(0, ITEMS) as i:
                        row = sp.value_load(items[bass.ds(i, 1), 0:1], min_val=0, max_val=SB * SN - SN)
                        erow = sp.value_load(items[bass.ds(i, 1), 1:2], min_val=0, max_val=EPAD - P)
                        sp.dma_start(rec[:, :], recs[bass.ds(erow, P), :]).then_inc(s["rec"], 16)
                        sp.wait_ge(s["out"], i + 1)
                        sp.dma_start(d["sup"][bass.ds(row, SN), :].rearrange("(h p) f -> p h f", p=P),
                                     acc[:, :].rearrange("p (h f) -> p h f", h=SH)).then_inc(s["st"], 16)
                        wait_apart(sp, s["st"], i * 16 + 16)

            @block.gpsimd
            def _(pool):
                with only_if(pool, flag, 0):
                    last_row = pool.to_reg(N - 1)
                    with pool.Fori(0, ITEMS) as i:
                        wait_apart(pool, s["idx"], i + 1)
                        pool.indirect_dma_start(out=xg[:, :], out_offset=None, in_=xtab,
                                                in_offset=bass.IndirectOffsetOnAxis(ap=idx[:, 0:1], axis=0),
                                                bounds_check=last_row, oob_is_err=False).then_inc(s["xg"], 16)

            @block.tensor
            def _(pe):
                with only_if(pe, flag, 0):
                    with pe.Fori(0, ITEMS) as i:
                        pe.wait_ge(s["A"], i + 1)
                        for h in range(SH):
                            last = nc.tensor.matmul(pG[:, h * P:(h + 1) * P], A[:, h * P:(h + 1) * P], xg[:, 0:P], start=True, stop=True)
                        last.then_inc(s["G"], 1)

            @block.vector
            def _(dve):
                with only_if(dve, flag, 0):
                    nc.vector.memset(acc[:, :], 0.0).then_inc(s["dve"], 1)
                    dve.wait_ge(s["dve"], 1)
                    with dve.Fori(0, ITEMS) as i:
                        link = OffsetChain(dve, s["dve"], 2, i, 1)
                        here = lambda t: t[:, bass.ds(i, 1)]
                        dve.wait_ge(s["rec"], i * 16 + 16)
                        nc.vector.tensor_copy(idx[:, :], rec[:, 1:2]).then_inc(s["idx"], 1)
                        link(nc.vector.tensor_tensor(loc[:, :], rec[:, 0:1], here(base), ALU.subtract))
                        dve.wait_ge(s["xg"], i * 16 + 16)
                        link(nc.vector.tensor_tensor(wf[:, :], rec[:, 2:3], xg[:, P:P + 1], ALU.mult))
                        nc.vector.tensor_scalar(A[:, :], iota_s[:, :], loc[:, 0:1], wf[:, 0:1], ALU.is_equal, ALU.mult).then_inc(s["A"], 1)
                        dve.wait_ge(s["G"], i + 1)
                        nc.vector.scalar_tensor_tensor(acc[:, :], acc[:, :], here(keep), pG[:, 0:SN], ALU.mult, ALU.add).then_inc(s["out"], 1)
                        dve.wait_ge(s["st"], i * 16 + 16)
                        link.end()


def general_map(nc, in_a, in_b, out, flag):
    GR, RING = 32, 4
    groups = N // (P * GR)
    tail = N - groups * P * GR
    TG = 8
    TP = tail // TG
    assert TP * TG == tail and groups % RING == 0
    ctx = ExitStack()
    with ctx:
        sb = lambda n, shape, dt: ctx.enter_context(nc.sbuf_tensor(f"m_{n}", shape, dt))
        phase_sem = ctx.enter_context(phase_semaphores(nc))
        sem = lambda n: phase_sem(f"m_{n}")
        a = [sb(f"a{k}", [P, GR, XW], F32) for k in range(RING)]
        b = [sb(f"b{k}", [P, GR, P], F32) for k in range(RING)]
        sq = sb("sq", [P, GR, P], F32)
        st6 = sb("st6", [P, GR, 6], F32)
        mv = sb("mv", [P, RING, GR, 2], F32)
        cols = sb("cols", [P, RING, 14, GR], F32)
        nrm = sb("nrm", [P, RING, 2, GR], F32)
        ring = lambda n: [sem(f"{n}{k}") for k in range(RING)]
        s_ina, s_inb, s_st = ring("ina"), ring("inb"), ring("st")
        s_dve, s_dve2, s_sq, s_arg, s_fn, s_nrm, s_out = (sem(n) for n in ("dve", "dve2", "sq", "arg", "fn", "nrm", "out"))

        def guarded(eng):
            return only_if(eng, flag, 0)

        def turns(eng, body, ahead=0, behind=0):
            fast_turns(eng, body, ahead, behind, RING, groups + 1, 1)

        def shape(m):
            return (TP, TG) if isinstance(m.q, int) and m.number == groups else (P, GR)

        def rows(t, m):
            p, g = shape(m)
            return t[bass.ds(m.number * (P * GR), p * g), :].rearrange("(p g) f -> p g f", g=g)

        def col(m):
            p, g = shape(m)
            return lambda i: cols[0:p, m.slot, i, 0:g]

        with nc.Block() as block:
            @block.sync
            def _(sp):
                def load(m):
                    p, g = shape(m)
                    k = m.slot
                    if m.exists(RING):
                        sp.wait_ge(s_st[k], m.dma_count(1))
                    sp.dma_start(b[k][0:p, 0:g, :], rows(in_b, m)).then_inc(s_inb[k], 16)
                    sp.dma_start(a[k][0:p, 0:g, 0:in_a.shape[1]], rows(in_a, m)).then_inc(s_ina[k], 16)

                with guarded(sp):
                    turns(sp, load)

            @block.gpsimd
            def _(pool):
                def store(m):
                    p, g = shape(m)
                    wait_apart(pool, s_out, m.count())
                    pool.dma_start(rows(out, m), b[m.slot][0:p, 0:g, :]).then_inc(s_st[m.slot], 16)

                with guarded(pool):
                    turns(pool, store)
                    for k in range(RING):
                        pool.wait_ge(s_st[k], 16 * len(range(k, groups + 1, RING)))

            @block.scalar
            def _(act):
                A = nc.scalar

                def apply(m):
                    p, g = shape(m)
                    k = m.slot
                    act.wait_ge(s_nrm, m.count())
                    for r in range(g):
                        last = A.activation(b[k][0:p, r, 0:P], b[k][0:p, r, :], ACT.Identity,
                                            bias=nrm[0:p, k, 1, r:r + 1], scale=nrm[0:p, k, 0, r:r + 1])
                    last.then_inc(s_out, 1)

                def exponential(m):
                    c = col(m)
                    act.wait_ge(s_arg, m.count())
                    A.activation(c(8), c(7), ACT.Exp, scale=-2.0).then_inc(s_fn, 1)

                def squares(m):
                    p, g = shape(m)
                    k = m.slot
                    act.wait_ge(s_inb[k], m.dma_count())
                    for r in range(g):
                        last = A.activation(sq[0:p, r, :], b[k][0:p, r, :], ACT.Square, accum_out=cols[0:p, k, 4, r:r + 1])
                    last.then_inc(s_sq, 1)

                def second(m):
                    if m.exists():
                        exponential(m)
                    if (m + 1).exists():
                        squares(m + 1)
                    if (m - 1).exists():
                        apply(m - 1)

                with guarded(act):
                    turns(act, second, 1, 1)

            @block.vector
            def _(dve):
                V = nc.vector

                def normalise(link, m):
                    p, g = shape(m)
                    c = col(m)
                    k = m.slot
                    for r in range(g):
                        last = V.bn_stats(st6[0:p, r, :], b[k][0:p, r, :])
                    link(last, alone=True)
                    for r in range(g):
                        last = V.bn_aggr(mv[0:p, k, r, :], st6[0:p, r, :])
                    link(last)
                    link(V.tensor_scalar(c(0), mv[0:p, k, 0:g, 1], EPS, None, ALU.add))
                    rsqrt_steps(nc, link, c(1), c(0), c(2), c(3))
                    V.tensor_copy(nrm[0:p, k, 0, 0:g], c(1))
                    V.scalar_tensor_tensor(nrm[0:p, k, 1, 0:g], mv[0:p, k, 0:g, 0], -1.0, c(1), ALU.mult, ALU.mult).then_inc(s_nrm, 1)

                def norm(link, c):
                    rsqrt_steps(nc, link, c(5), c(4), c(2), c(3))
                    link(V.tensor_tensor(c(6), c(4), c(5), ALU.mult))
                    link(V.tensor_scalar(c(6), c(6), 1e-15, None, ALU.max))
                    link(V.reciprocal(c(5), c(6)))

                def series(m):
                    c = col(m)
                    link = OffsetChain(dve, s_dve, NORM_K + 1 + POLY_K, m.number, 0)
                    dve.wait_ge(s_sq, m.count())
                    norm(link, c)
                    V.tensor_copy(c(7), c(6)).then_inc(s_arg, 1)
                    link(V.tensor_scalar(c(10), c(4), 0.3 ** 2, None, ALU.min))
                    even_poly_steps(nc, link, c(11), c(10), TANH_C)
                    link.end()

                def mapped_sum(m):
                    p, g = shape(m)
                    c = col(m)
                    k = m.slot
                    link = OffsetChain(dve, s_dve2, MAPS_K, m.number, 0)
                    dve.wait_ge(s_fn, m.count())
                    link(V.tensor_scalar(c(12), c(8), 1.0, None, ALU.add))
                    link(V.reciprocal(c(13), c(12)))
                    link(V.scalar_tensor_tensor(c(12), c(8), 1.0, c(13), ALU.subtract, ALU.mult))
                    link(V.scalar_tensor_tensor(c(12), c(12), -1.0, c(5), ALU.mult, ALU.mult))
                    link(V.tensor_tensor(c(11), c(11), c(12), ALU.subtract))
                    link(V.scalar_tensor_tensor(c(11), c(6), 0.3, c(11), ALU.is_lt, ALU.mult))
                    link(V.tensor_tensor(c(11), c(11), c(12), ALU.add))
                    link(V.tensor_tensor(c(12), c(11), c(6), ALU.mult))
                    link(V.tensor_scalar(c(12), c(12), 1e-15, None, ALU.max))
                    link(V.reciprocal(c(13), c(12)))
                    link(V.tensor_scalar(c(13), c(13), 0.996, -1.0, ALU.mult, ALU.add))
                    link(V.scalar_tensor_tensor(c(13), c(12), 0.996, c(13), ALU.is_gt, ALU.mult))
                    link(V.scalar_tensor_tensor(c(13), c(13), 1.0, c(11), ALU.add, ALU.mult))
                    dve.wait_ge(s_ina[k], m.dma_count())
                    for r in range(g):
                        last = V.scalar_tensor_tensor(b[k][0:p, r, :], b[k][0:p, r, :], cols[0:p, k, 13, r:r + 1],
                                                      a[k][0:p, r, 0:P], ALU.mult, ALU.add)
                    link(last)
                    normalise(link, m)
                    link.end()

                def body(m):
                    if m.exists():
                        series(m)
                    if (m - 1).exists():
                        mapped_sum(m - 1)

                with guarded(dve):
                    turns(dve, body, 0, 1)


_INS = ['x', 'src', 'dst', 'edge_attr_128', 'edge_weight'] + [f'L0_gnn_{p}{k}_l{l}' for l in (0, 1) for k in (1, 2, 3) for p in ('W', 'b')]


def kernel(**inputs):
    import numpy as _np
    import concourse.bacc as _bacc
    from concourse import mybir as _mybir
    from concourse.bass_utils import run_bass_kernel_spmd as _run

    nc = _bacc.Bacc("TRN2", target_bir_lowering=False, num_devices=1)
    arrays, args = {}, []
    for name in _INS:
        a = _np.ascontiguousarray(inputs[name])
        arrays[f"in_{name}_dram"] = a
        args.append(nc.dram_tensor(f"in_{name}_dram", a.shape, _mybir.dt.from_np(a.dtype), kind="ExternalInput").ap())
    args.append(nc.dram_tensor("out_0_dram", (N, P), F32, kind="ExternalOutput").ap())
    build(nc, *args)
    r = _run(nc, [arrays], core_ids=[0])
    return r.results[0]["out_0_dram"]
```
